# Optimizing a Trainium2 kernel written in Bass

```python
import numpy as np
import jax
import jax.numpy as jnp

def _softmax(x, axis=-1):
    return jax.nn.softmax(x, axis=axis)

def _gelu(x):
    return jax.nn.gelu(x, approximate=True)

def _silu(x):
    return jax.nn.silu(x)

def _sigmoid(x):
    return jax.nn.sigmoid(x)

def _layernorm(x, axis=-1, eps=1e-05):
    m = jnp.mean(x, axis=axis, keepdims=True)
    v = jnp.var(x, axis=axis, keepdims=True)
    return (x - m) / jnp.sqrt(v + eps)

def _scatter_add(tgt, idx, src, axis=0):
    return tgt.at[idx].add(src)

def _segment_sum(src, seg, n):
    return jax.ops.segment_sum(src, seg, n)
kernel_name = 'mk_early_fusion_embed_d1_tok_img768_r4_867a82'

def setup_inputs(seed: int=0):
    np.random.seed(seed)
    _w = jnp.asarray

    def _rec_inputs():
        import jax
        import jax.numpy as jnp
        _rk = jax.random.key(seed)
        x = 7.57192e-06 + 1.00007 * jax.random.normal(jax.random.fold_in(_rk, 1), (32, 3, 96, 96), jnp.float32)
        x_txt = jax.random.randint(jax.random.fold_in(_rk, 51), (32, 128), 0, 12564, jnp.int32)
        return (x, x_txt)
    x, x_txt = _rec_inputs()

    def _L0_tok_setup():
        import jax, jax.numpy as jnp
        import numpy as np
        K = 4
        STRIDE = 4
        EPS = 1e-05
        SLOPE = 0.01

        def conv2d(x, w, b, stride):
            out = jax.lax.conv_general_dilated(x, w, (stride, stride), 'VALID', dimension_numbers=('NCHW', 'OIHW', 'NCHW'))
            return out + b[None, :, None, None]

        def batchnorm(x, g, b, m, v):
            inv = g / jnp.sqrt(v + EPS)
            return x * inv[None, :, None, None] + (b - m * inv)[None, :, None, None]

        def leaky_relu(x):
            return jnp.where(x >= 0, x, SLOPE * x)

        def deform_conv(x, offset, w, b):
            B, C, H, W = x.shape
            Ho, Wo = (offset.shape[2], offset.shape[3])
            KK = K * K
            off = offset.reshape(B, KK, 2, Ho, Wo)
            kh = jnp.repeat(jnp.arange(K), K).astype(x.dtype)
            kw = jnp.tile(jnp.arange(K), K).astype(x.dtype)
            base_y = (jnp.arange(Ho) * STRIDE).astype(x.dtype)
            base_x = (jnp.arange(Wo) * STRIDE).astype(x.dtype)
            py = base_y[None, None, :, None] + kh[None, :, None, None] + off[:, :, 0]
            px = base_x[None, None, None, :] + kw[None, :, None, None] + off[:, :, 1]
            y0 = jnp.floor(py)
            x0 = jnp.floor(px)
            wy = py - y0
            wx = px - x0

            def corner(yc, xc):
                yi = yc.astype(jnp.int32)
                xi = xc.astype(jnp.int32)
                valid = (yi >= 0) & (yi < H) & (xi >= 0) & (xi < W)
                yi = jnp.clip(yi, 0, H - 1)
                xi = jnp.clip(xi, 0, W - 1)
                v = jax.vmap(lambda img, a, c: img[:, a, c])(x, yi, xi)
                return v * valid[:, None].astype(x.dtype)
            v00 = corner(y0, x0)
            v01 = corner(y0, x0 + 1)
            v10 = corner(y0 + 1, x0)
            v11 = corner(y0 + 1, x0 + 1)
            wy_ = wy[:, None]
            wx_ = wx[:, None]
            sampled = v00 * (1 - wy_) * (1 - wx_) + v01 * (1 - wy_) * wx_ + v10 * wy_ * (1 - wx_) + v11 * wy_ * wx_
            out = jnp.einsum('bckhw,ock->bohw', sampled, w.reshape(w.shape[0], C, KK))
            return out + b[None, :, None, None]
        key = jax.random.key(seed)
        ks = jax.random.split(key, 16)
        f32 = jnp.float32
        inp = {'x': jax.random.normal(ks[0], (64, 3, 224, 224), f32), 'stem_w': jax.random.normal(ks[1], (96, 3, 4, 4), f32) * 0.1, 'stem_b': jax.random.normal(ks[2], (96,), f32) * 0.05, 'bn1_g': jax.random.uniform(ks[3], (96,), f32, 0.5, 1.5), 'bn1_b': jax.random.normal(ks[4], (96,), f32) * 0.05, 'bn1_m': jax.random.normal(ks[5], (96,), f32) * 0.05, 'bn1_v': jax.random.uniform(ks[6], (96,), f32, 0.5, 1.5), 'off_w': jax.random.normal(ks[7], (32, 96, 4, 4), f32) * 0.02, 'off_b': jax.random.normal(ks[8], (32,), f32) * 0.02, 'dcn_w': jax.random.normal(ks[9], (192, 96, 4, 4), f32) * 0.05, 'dcn_b': jax.random.normal(ks[10], (192,), f32) * 0.05, 'bn2_g': jax.random.uniform(ks[11], (192,), f32, 0.5, 1.5), 'bn2_b': jax.random.normal(ks[12], (192,), f32) * 0.05, 'bn2_m': jax.random.normal(ks[13], (192,), f32) * 0.05, 'bn2_v': jax.random.uniform(ks[14], (192,), f32, 0.5, 1.5)}
        return inp
    _L0_tok_all = _L0_tok_setup()
    _L0_tok_in = {k: v for k, v in _L0_tok_all.items() if k in ('stem_w', 'stem_b', 'bn1_g', 'bn1_b', 'bn1_m', 'bn1_v', 'off_w', 'off_b', 'dcn_w', 'dcn_b', 'bn2_g', 'bn2_b', 'bn2_m', 'bn2_v')}
    del _L0_tok_all

    def _L0_txt_setup():
        import jax, jax.numpy as jnp
        import numpy as np
        VOCAB = 50257
        DIM = 192
        PADDING_IDX = 0
        NUM_BITS = 8
        QMAX = 2 ** (NUM_BITS - 1) - 1

        def fake_quant_lastdim(w):
            absmax = jnp.max(jnp.abs(w), axis=-1, keepdims=True)
            scale = jnp.maximum(absmax, 1e-08) / QMAX
            q = jnp.clip(jnp.round(w / scale), -QMAX, QMAX) * scale
            return w + jax.lax.stop_gradient(q - w)
        key = jax.random.key(seed)
        k_w, k_i = jax.random.split(key)
        weight = jax.random.normal(k_w, (VOCAB, DIM), dtype=jnp.float32) * 0.02
        input = jax.random.randint(k_i, (8, 128), 0, VOCAB, dtype=jnp.int64)
        return {'weight': weight, 'input': input}
    _L0_txt_all = _L0_txt_setup()
    _L0_txt_in = {k: v for k, v in _L0_txt_all.items() if k in ('weight',)}
    del _L0_txt_all

    def _L0_attn_setup():
        import jax, jax.numpy as jnp
        import numpy as np
        D_MODEL = 192
        N_HEADS = 12
        D_HEAD = D_MODEL // N_HEADS
        LOCAL_WINDOW = 128
        SCALE = 1.0 / np.sqrt(D_HEAD).astype(np.float32)
        key = jax.random.key(seed)
        ks = jax.random.split(key, 6)
        B, N, D = (2, 512, D_MODEL)
        x = jax.random.normal(ks[0], (B, N, D), dtype=jnp.float32)
        init = 0.02
        Wq = jax.random.normal(ks[1], (D, D), dtype=jnp.float32) * init
        Wk = jax.random.normal(ks[2], (D, D), dtype=jnp.float32) * init
        Wv = jax.random.normal(ks[3], (D, D), dtype=jnp.float32) * init
        Wo = jax.random.normal(ks[4], (D, D), dtype=jnp.float32) * init
        bq = jnp.zeros((D,), dtype=jnp.float32)
        bk = jnp.zeros((D,), dtype=jnp.float32)
        bv = jnp.zeros((D,), dtype=jnp.float32)
        bo = jnp.zeros((D,), dtype=jnp.float32)
        return {'x': x, 'Wq': Wq, 'bq': bq, 'Wk': Wk, 'bk': bk, 'Wv': Wv, 'bv': bv, 'Wo': Wo, 'bo': bo}
    _L0_attn_all = _L0_attn_setup()
    _L0_attn_in = {k: v for k, v in _L0_attn_all.items() if k in ('Wq', 'bq', 'Wk', 'bk', 'Wv', 'bv', 'Wo', 'bo')}
    del _L0_attn_all

    def _L0_ffn_setup():
        import jax, jax.numpy as jnp
        import numpy as np
        D_MODEL = 192
        KAN_HIDDEN = 512
        NUM_CP = 16
        DEGREE = 3
        RMIN, RMAX = (-4.0, 4.0)

        def bspline_basis(x, num_cp=NUM_CP, degree=DEGREE, rmin=RMIN, rmax=RMAX):
            h = (rmax - rmin) / (num_cp - degree)
            knots = rmin - degree * h + jnp.arange(num_cp + degree + 1, dtype=x.dtype) * h
            xe = x[..., None]
            b = ((xe >= knots[:-1]) & (xe < knots[1:])).astype(x.dtype)
            for d in range(1, degree + 1):
                t0 = knots[:-(d + 1)]
                t1 = knots[d:-1]
                t2 = knots[d + 1:]
                t3 = knots[1:-d]
                b = (xe - t0) / (t1 - t0) * b[..., :-1] + (t2 - xe) / (t2 - t3) * b[..., 1:]
            return b

        def kan_layer(x, w):
            basis = bspline_basis(x)
            return jnp.einsum('ndk,odk->no', basis, w)
        key = jax.random.key(seed)
        kx, k1, k2 = jax.random.split(key, 3)
        x = jax.random.normal(kx, (2, 512, D_MODEL), dtype=jnp.float32)
        w1 = jax.random.normal(k1, (KAN_HIDDEN, D_MODEL, NUM_CP), dtype=jnp.float32) * (1.0 / np.sqrt(D_MODEL * NUM_CP))
        w2 = jax.random.normal(k2, (D_MODEL, KAN_HIDDEN, NUM_CP), dtype=jnp.float32) * (1.0 / np.sqrt(KAN_HIDDEN * NUM_CP))
        return {'x': x, 'w1': w1, 'w2': w2}
    _L0_ffn_all = _L0_ffn_setup()
    _L0_ffn_in = {k: v for k, v in _L0_ffn_all.items() if k in ('w1', 'w2')}
    del _L0_ffn_all
    return {'x': x, 'x_txt': x_txt, 'L0_tok_stem_w': _L0_tok_in['stem_w'], 'L0_tok_stem_b': _L0_tok_in['stem_b'], 'L0_tok_bn1_g': _L0_tok_in['bn1_g'], 'L0_tok_bn1_b': _L0_tok_in['bn1_b'], 'L0_tok_bn1_m': _L0_tok_in['bn1_m'], 'L0_tok_bn1_v': _L0_tok_in['bn1_v'], 'L0_tok_off_w': _L0_tok_in['off_w'], 'L0_tok_off_b': _L0_tok_in['off_b'], 'L0_tok_dcn_w': _L0_tok_in['dcn_w'], 'L0_tok_dcn_b': _L0_tok_in['dcn_b'], 'L0_tok_bn2_g': _L0_tok_in['bn2_g'], 'L0_tok_bn2_b': _L0_tok_in['bn2_b'], 'L0_tok_bn2_m': _L0_tok_in['bn2_m'], 'L0_tok_bn2_v': _L0_tok_in['bn2_v'], 'L0_txt_weight': _L0_txt_in['weight'], 'L0_attn_Wq': _L0_attn_in['Wq'], 'L0_attn_bq': _L0_attn_in['bq'], 'L0_attn_Wk': _L0_attn_in['Wk'], 'L0_attn_bk': _L0_attn_in['bk'], 'L0_attn_Wv': _L0_attn_in['Wv'], 'L0_attn_bv': _L0_attn_in['bv'], 'L0_attn_Wo': _L0_attn_in['Wo'], 'L0_attn_bo': _L0_attn_in['bo'], 'L0_ffn_w1': _L0_ffn_in['w1'], 'L0_ffn_w2': _L0_ffn_in['w2']}

def reference(x, x_txt, L0_tok_stem_w, L0_tok_stem_b, L0_tok_bn1_g, L0_tok_bn1_b, L0_tok_bn1_m, L0_tok_bn1_v, L0_tok_off_w, L0_tok_off_b, L0_tok_dcn_w, L0_tok_dcn_b, L0_tok_bn2_g, L0_tok_bn2_b, L0_tok_bn2_m, L0_tok_bn2_v, L0_txt_weight, L0_attn_Wq, L0_attn_bq, L0_attn_Wk, L0_attn_bk, L0_attn_Wv, L0_attn_bv, L0_attn_Wo, L0_attn_bo, L0_ffn_w1, L0_ffn_w2):
    import jax
    import jax.numpy as jnp

    def _L0_tok_ref(x, stem_w, stem_b, bn1_g, bn1_b, bn1_m, bn1_v, off_w, off_b, dcn_w, dcn_b, bn2_g, bn2_b, bn2_m, bn2_v):
        import jax, jax.numpy as jnp
        import numpy as np
        K = 4
        STRIDE = 4
        EPS = 1e-05
        SLOPE = 0.01

        def conv2d(x, w, b, stride):
            out = jax.lax.conv_general_dilated(x, w, (stride, stride), 'VALID', dimension_numbers=('NCHW', 'OIHW', 'NCHW'))
            return out + b[None, :, None, None]

        def batchnorm(x, g, b, m, v):
            inv = g / jnp.sqrt(v + EPS)
            return x * inv[None, :, None, None] + (b - m * inv)[None, :, None, None]

        def leaky_relu(x):
            return jnp.where(x >= 0, x, SLOPE * x)

        def deform_conv(x, offset, w, b):
            B, C, H, W = x.shape
            Ho, Wo = (offset.shape[2], offset.shape[3])
            KK = K * K
            off = offset.reshape(B, KK, 2, Ho, Wo)
            kh = jnp.repeat(jnp.arange(K), K).astype(x.dtype)
            kw = jnp.tile(jnp.arange(K), K).astype(x.dtype)
            base_y = (jnp.arange(Ho) * STRIDE).astype(x.dtype)
            base_x = (jnp.arange(Wo) * STRIDE).astype(x.dtype)
            py = base_y[None, None, :, None] + kh[None, :, None, None] + off[:, :, 0]
            px = base_x[None, None, None, :] + kw[None, :, None, None] + off[:, :, 1]
            y0 = jnp.floor(py)
            x0 = jnp.floor(px)
            wy = py - y0
            wx = px - x0

            def corner(yc, xc):
                yi = yc.astype(jnp.int32)
                xi = xc.astype(jnp.int32)
                valid = (yi >= 0) & (yi < H) & (xi >= 0) & (xi < W)
                yi = jnp.clip(yi, 0, H - 1)
                xi = jnp.clip(xi, 0, W - 1)
                v = jax.vmap(lambda img, a, c: img[:, a, c])(x, yi, xi)
                return v * valid[:, None].astype(x.dtype)
            v00 = corner(y0, x0)
            v01 = corner(y0, x0 + 1)
            v10 = corner(y0 + 1, x0)
            v11 = corner(y0 + 1, x0 + 1)
            wy_ = wy[:, None]
            wx_ = wx[:, None]
            sampled = v00 * (1 - wy_) * (1 - wx_) + v01 * (1 - wy_) * wx_ + v10 * wy_ * (1 - wx_) + v11 * wy_ * wx_
            out = jnp.einsum('bckhw,ock->bohw', sampled, w.reshape(w.shape[0], C, KK))
            return out + b[None, :, None, None]
        h = conv2d(x, stem_w, stem_b, 4)
        h = leaky_relu(batchnorm(h, bn1_g, bn1_b, bn1_m, bn1_v))
        offset = conv2d(h, off_w, off_b, 4)
        h = deform_conv(h, offset, dcn_w, dcn_b)
        h = leaky_relu(batchnorm(h, bn2_g, bn2_b, bn2_m, bn2_v))
        B, C, Ho, Wo = h.shape
        return h.reshape(B, C, Ho * Wo).transpose(0, 2, 1)

    def _L0_txt_ref(weight, input):
        import jax, jax.numpy as jnp
        import numpy as np
        VOCAB = 50257
        DIM = 192
        PADDING_IDX = 0
        NUM_BITS = 8
        QMAX = 2 ** (NUM_BITS - 1) - 1

        def fake_quant_lastdim(w):
            absmax = jnp.max(jnp.abs(w), axis=-1, keepdims=True)
            scale = jnp.maximum(absmax, 1e-08) / QMAX
            q = jnp.clip(jnp.round(w / scale), -QMAX, QMAX) * scale
            return w + jax.lax.stop_gradient(q - w)
        quant_weight = fake_quant_lastdim(weight)
        return quant_weight[input]

    def _L0_attn_ref(x, Wq, bq, Wk, bk, Wv, bv, Wo, bo):
        import jax, jax.numpy as jnp
        import numpy as np
        D_MODEL = 192
        N_HEADS = 12
        D_HEAD = D_MODEL // N_HEADS
        LOCAL_WINDOW = 128
        SCALE = 1.0 / np.sqrt(D_HEAD).astype(np.float32)
        B, N, D = x.shape
        H, d = (N_HEADS, D_HEAD)
        q = (x @ Wq + bq).reshape(B, N, H, d).transpose(0, 2, 1, 3)
        k = (x @ Wk + bk).reshape(B, N, H, d).transpose(0, 2, 1, 3)
        v = (x @ Wv + bv).reshape(B, N, H, d).transpose(0, 2, 1, 3)
        scores = jnp.einsum('bhqd,bhkd->bhqk', q, k) * SCALE
        idx = jnp.arange(N)
        half = LOCAL_WINDOW // 2
        allowed = jnp.abs(idx[:, None] - idx[None, :]) <= half
        scores = jnp.where(allowed[None, None], scores, -jnp.inf)
        attn = jax.nn.softmax(scores, axis=-1)
        out = jnp.einsum('bhqk,bhkd->bhqd', attn, v)
        out = out.transpose(0, 2, 1, 3).reshape(B, N, D)
        return out @ Wo + bo

    def _L0_ffn_ref(x, w1, w2):
        import jax, jax.numpy as jnp
        import numpy as np
        D_MODEL = 192
        KAN_HIDDEN = 512
        NUM_CP = 16
        DEGREE = 3
        RMIN, RMAX = (-4.0, 4.0)

        def bspline_basis(x, num_cp=NUM_CP, degree=DEGREE, rmin=RMIN, rmax=RMAX):
            h = (rmax - rmin) / (num_cp - degree)
            knots = rmin - degree * h + jnp.arange(num_cp + degree + 1, dtype=x.dtype) * h
            xe = x[..., None]
            b = ((xe >= knots[:-1]) & (xe < knots[1:])).astype(x.dtype)
            for d in range(1, degree + 1):
                t0 = knots[:-(d + 1)]
                t1 = knots[d:-1]
                t2 = knots[d + 1:]
                t3 = knots[1:-d]
                b = (xe - t0) / (t1 - t0) * b[..., :-1] + (t2 - xe) / (t2 - t3) * b[..., 1:]
            return b

        def kan_layer(x, w):
            basis = bspline_basis(x)
            return jnp.einsum('ndk,odk->no', basis, w)
        B, T, D = x.shape
        input_dtype = x.dtype
        h = x.reshape(B * T, D).astype(jnp.float32)
        h = kan_layer(h, w1)
        h = kan_layer(h, w2)
        h = h.astype(input_dtype)
        return h.reshape(B, T, -1)
    h = _L0_tok_ref(x, L0_tok_stem_w, L0_tok_stem_b, L0_tok_bn1_g, L0_tok_bn1_b, L0_tok_bn1_m, L0_tok_bn1_v, L0_tok_off_w, L0_tok_off_b, L0_tok_dcn_w, L0_tok_dcn_b, L0_tok_bn2_g, L0_tok_bn2_b, L0_tok_bn2_m, L0_tok_bn2_v)
    h = jnp.concatenate([h, _L0_txt_ref(L0_txt_weight, x_txt)], axis=1)
    h = h + _L0_attn_ref(_layernorm(h, axis=-1), L0_attn_Wq, L0_attn_bq, L0_attn_Wk, L0_attn_bk, L0_attn_Wv, L0_attn_bv, L0_attn_Wo, L0_attn_bo)
    h = h + _L0_ffn_ref(_layernorm(h, axis=-1), L0_ffn_w1, L0_ffn_w2)
    return h

_drawn_inputs = setup_inputs


def setup_inputs(seed=0):
    import zlib

    import numpy as np

    out = dict(_drawn_inputs(seed))
    spreads = {'L0_attn_bq': (0.0, 0.8),
     'L0_attn_bk': (0.0, 0.8),
     'L0_attn_bv': (0.0, 0.1),
     'L0_attn_bo': (0.0, 0.1)}
    factors = {'L0_attn_Wq': 8.0, 'L0_attn_Wk': 8.0}
    for name, (base, spread) in spreads.items():
        noise = np.random.default_rng([zlib.crc32(name.encode()), seed]).standard_normal(out[name].shape)
        drawn = base * np.exp(spread * noise) if base else spread * noise
        out[name] = jnp.asarray(drawn.astype(out[name].dtype))
    for name, factor in factors.items():
        out[name] = (out[name] * factor).astype(out[name].dtype)
    return out
```

```python
from contextlib import ExitStack

import concourse.bass as bass
from concourse import mybir

ALU = mybir.AluOpType
ACT = mybir.ActivationFunctionType
F32 = mybir.dt.float32
F32R = mybir.dt.float32r
BF16 = mybir.dt.bfloat16
I32 = mybir.dt.int32
AX_X = mybir.AxisListType.X

P = 128
B = 32
D = 192
D0, D1 = 128, 64
C1 = 96
K = 4
TAPS = K * K
HS = 24
PIX = HS * HS
HO = 6
VIS = HO * HO
TXT = 128
TOK = VIS + TXT
ROWS = TOK // 2
PAIRS = B // 2
PT = 2 * TOK
ALL = B * TOK
SAMPLES = TAPS * VIS
PATCH = 3 * TAPS
PIXC = 96
NPIXC = PIX // PIXC
HEADS, DH = 12, 16
HG = HEADS // 4
KPAD = 96
HID = 512
NCP = 16
EPS = 1e-5
SLOPE = 0.01
QMAX = 127.0
MAGIC = 12582912.0
NEG = -1.0e30
SPL_SCALE = 13.0 / 32.0
SPL_BIAS = (4.0 * 13.0 / 8.0 + 3.0) / 4.0 - 0.5
VT = B * VIS // P
OT = ALL // P


class Step:

    def __init__(self, engine, sem, base=0):
        self.engine, self.sem, self.base, self.n = engine, sem, base, 0

    def mark(self, ins):
        ins.then_inc(self.sem, 1)
        self.n += 1
        return self.n

    def after(self, n):
        self.engine.wait_ge(self.sem, self.base + n)

    def run(self, ins):
        self.after(self.mark(ins))


def memories(nc, stack):
    def sb(name, shape, dt=F32):
        return stack.enter_context(nc.sbuf_tensor(name, shape, dt))

    def ps(name, shape):
        return stack.enter_context(nc.psum_tensor(name, shape, F32))

    def sem(name):
        return stack.enter_context(nc.semaphore(name))

    return sb, ps, sem


def fold_norm(nc, dve, s, pow_done, rows, std, inv, half):
    bias, gamma, beta, mean, var = (rows[:, j, :] for j in range(5))
    s.run(nc.vector.tensor_scalar(std[:, :], var, EPS, None, ALU.add))
    dve.wait_ge(pow_done, 1)
    s.run(nc.vector.tensor_tensor(half[:, :], inv[:, :], inv[:, :], ALU.mult))
    s.run(nc.vector.tensor_tensor(half[:, :], half[:, :], std[:, :], ALU.mult))
    s.run(nc.vector.tensor_scalar(half[:, :], half[:, :], -0.5, 1.5, ALU.mult, ALU.add))
    s.run(nc.vector.tensor_tensor(inv[:, :], inv[:, :], half[:, :], ALU.mult))
    s.run(nc.vector.tensor_tensor(inv[:, :], inv[:, :], gamma, ALU.mult))
    s.run(nc.vector.tensor_tensor(std[:, :], bias, mean, ALU.subtract))
    s.run(nc.vector.tensor_tensor(std[:, :], std[:, :], inv[:, :], ALU.mult))
    s.run(nc.vector.tensor_tensor(std[:, :], std[:, :], beta, ALU.add))
    return std[:, :]


def stem_phase(nc, patches, stem_w, cvec, hT_all, pix_scr, txt_idx, table, txt_scr):
    with ExitStack() as stack:
        sb, ps, sem = memories(nc, stack)
        patch = [sb(f"patch{u}", [P, PIX]) for u in range(2)]
        w = sb("stem_weights", [P, C1])
        rows = sb("stem_vectors", [P, 5, C1])
        half = sb("stem_half", [P, C1])
        std = sb("stem_std", [P, C1])
        inv = sb("stem_inv", [P, C1])
        chan = ps("by_channel", [P, 2, 2, 512])
        pix = ps("by_pixel", [P, 2, 2, 512])
        by_pixel = [sb(f"stem_by_pixel{u}", [P, PIX]) for u in range(4)]
        idx = sb("text_index", [P, B], I32)
        emb = [sb(f"text_rows{u}", [P, D]) for u in range(4)]
        quant = [sb(f"text_quant{u}", [P, D]) for u in range(4)]
        q_amax = sb("text_amax", [P, 4])
        q_scale = sb("text_scale", [P, 4])
        q_rec = sb("text_rec", [P, 4])
        vectors_in = sem("vectors_in")
        zeroed = sem("stem_zeroed")
        ones_set = sem("stem_ones")
        bn = sem("stem_bn")
        bn_pow = sem("stem_pow")
        w_ready = sem("stem_w_ready")
        patch_in = [sem(f"patch_in{u}") for u in range(2)]
        stem_done = sem("stem_done")
        scaled = sem("stem_scaled")
        stem_read = sem("stem_read")
        pixel_out = [sem(f"stem_pixel_out{u}") for u in range(4)]
        idx_in = sem("text_index_in")
        emb_in = [sem(f"text_in{u}") for u in range(4)]
        q_step = sem("text_step")
        q_done = sem("text_done")
        txt_out = [sem(f"text_out{u}") for u in range(4)]
        block = stack.enter_context(nc.Block())

        @block.sync
        def _(sp):
            sp.dma_start(rows[:, :, :], cvec).then_inc(vectors_in, 16)
            sp.wait_ge(zeroed, 1)
            sp.dma_start(w[0:PATCH, :], stem_w).then_inc(vectors_in, 16)
            for u in range(2):
                sp.dma_start(patch[u][0:PATCH, :], patches[:, u, :]).then_inc(patch_in[u], 16)

            def results_out(t, u):
                sp.wait_ge(stem_read, 2 * (4 * t + u) + 2)
                sp.dma_start(pix_scr[bass.ds(4 * t + u, 1), :, :].rearrange("b p n -> p (b n)"),
                             by_pixel[u][0:PIXC, :]).then_inc(pixel_out[u], 16)
                sp.wait_ge(q_done, 4 * t + u + 1)
                sp.dma_start(txt_scr[bass.ds((4 * t + u) * TXT, TXT), :], quant[u][:, :]).then_inc(txt_out[u], 16)

            with sp.Fori(0, B // 4 - 1) as t:
                for u in range(4):
                    sp.wait_ge(stem_done, 4 * t + u + 1)
                    sp.dma_start(patch[u % 2][0:PATCH, :],
                                 patches[:, bass.ds(4 * t + u + 2, 1), :].rearrange("p b n -> p (b n)")
                                 ).then_inc(patch_in[u % 2], 16)
                    results_out(t, u)
            for u in range(4):
                t = B // 4 - 1
                if u < 2:
                    sp.wait_ge(stem_done, 4 * t + u + 1)
                    sp.dma_start(patch[u][0:PATCH, :], patches[:, 4 * t + u + 2, :]).then_inc(patch_in[u], 16)
                results_out(t, u)
            for u in range(4):
                sp.wait_ge(txt_out[u], 16 * (B // 4))
                sp.wait_ge(pixel_out[u], 16 * (B // 4))

        @block.gpsimd
        def _(pool):
            pool.memset(patch[0][:, :], 0.0)
            pool.memset(patch[1][:, :], 0.0)
            pool.memset(w[:, :], 0.0).then_inc(zeroed, 1)
            pool.memset(half[:, :], -0.5).then_inc(zeroed, 1)
            pool.dma_start(idx[:, :], txt_idx).then_inc(idx_in, 16)
            pool.wait_ge(zeroed, 2)
            pool.memset(patch[0][KPAD:KPAD + 1, :], 1.0).then_inc(ones_set, 1)
            pool.memset(patch[1][KPAD:KPAD + 1, :], 1.0).then_inc(ones_set, 1)
            pool.wait_ge(ones_set, 2)
            pool.wait_ge(bn, 1)
            pool.tensor_tensor(inv[:, :], std[:, :], half[:, :], ALU.pow).then_inc(bn_pow, 1)
            pool.wait_ge(idx_in, 16)
            for b in range(B):
                if b >= 4:
                    pool.wait_ge(q_done, b - 3)
                pool.indirect_dma_start(emb[b % 4][:, :], None, table,
                                        bass.IndirectOffsetOnAxis(idx[:, b:b + 1], 0)).then_inc(emb_in[b % 4], 16)

        @block.vector
        def _(dve):
            s = Step(dve, bn)
            dve.wait_ge(vectors_in, 32)
            shift = fold_norm(nc, dve, s, bn_pow, rows, std, inv, half)
            nc.vector.tensor_tensor(w[0:PATCH, :], w[0:PATCH, :], inv[0:PATCH, :], ALU.mult).then_inc(w_ready, 1)
            nc.vector.tensor_copy(w[KPAD:KPAD + 1, :], shift[KPAD:KPAD + 1, :]).then_inc(w_ready, 1)

            def image(t, u, first):
                for n, (src, dst) in enumerate(((chan, hT_all[0:C1, bass.ds((4 * t + u) * PIX, PIX)]),
                                                (pix, by_pixel[u][0:PIXC, :]))):
                    dve.wait_ge(scaled, 8 * t + 2 * u + n + 1)
                    y = dst.rearrange("p (h n) -> p h n", h=2)
                    nc.vector.tensor_tensor(y, src[0:C1, u % 2, :, 0:PIX // 2], y, ALU.max).then_inc(stem_read, 1)
                e, q = emb[u], quant[u]
                s = Step(dve, q_step, 7 * (4 * t + u))
                dve.wait_ge(emb_in[u], 16 * t + 16)
                s.run(nc.vector.tensor_reduce(q_amax[:, u:u + 1], e[:, :], AX_X, ALU.max, apply_absolute_value=True))
                s.run(nc.vector.tensor_scalar(q_scale[:, u:u + 1], q_amax[:, u:u + 1], 1e-8, 1.0 / QMAX,
                                              ALU.max, ALU.mult))
                s.run(nc.vector.reciprocal(q_rec[:, u:u + 1], q_scale[:, u:u + 1]))
                if not first:
                    dve.wait_ge(txt_out[u], 16 * t)
                s.run(nc.vector.tensor_scalar(q[:, :], e[:, :], q_rec[:, u:u + 1], MAGIC, ALU.mult, ALU.add))
                s.run(nc.vector.tensor_scalar(q[:, :], q[:, :], MAGIC, -QMAX, ALU.subtract, ALU.max))
                s.run(nc.vector.tensor_scalar(q[:, :], q[:, :], QMAX, q_scale[:, u:u + 1], ALU.min, ALU.mult))
                s.run(nc.vector.tensor_tensor(q[:, :], q[:, :], e[:, :], ALU.subtract))
                nc.vector.tensor_tensor(q[:, :], e[:, :], q[:, :], ALU.add).then_inc(q_done, 1)

            for u in range(4):
                image(0, u, True)
            with dve.Fori(1, B // 4) as t:
                for u in range(4):
                    image(t, u, False)

        @block.tensor
        def _(pe):
            pe.wait_ge(w_ready, 2)
            pe.wait_ge(ones_set, 2)

            def image(t, u, first):
                pe.wait_ge(patch_in[u], 16 * t + 16)
                if not first:
                    pe.wait_ge(stem_read, 4 * t + 2 * u - 2)
                x = patch[u]
                for h in range(2):
                    nc.tensor.matmul(chan[0:C1, u, h, 0:PIX // 2], w[0:KPAD + 1, :],
                                     x[0:KPAD + 1, h * PIX // 2:(h + 1) * PIX // 2], start=True, stop=True)
                for c in range(NPIXC):
                    last = nc.tensor.matmul(pix[0:PIXC, u, c // 3, (c % 3) * C1:(c % 3 + 1) * C1],
                                            x[0:KPAD + 1, c * PIXC:(c + 1) * PIXC], w[0:KPAD + 1, :],
                                            start=True, stop=True)
                last.then_inc(stem_done, 1)

            for u in range(2):
                image(0, u, True)
            with pe.Fori(1, B // 2) as t:
                for u in range(2):
                    image(t, u, False)

        @block.scalar
        def _(act):
            def image(t, u, first):
                act.wait_ge(stem_done, 4 * t + u + 1)
                if not first:
                    act.wait_ge(pixel_out[u], 16 * t)
                for src, dst in ((chan, hT_all[0:C1, bass.ds((4 * t + u) * PIX, PIX)]),
                                 (pix, by_pixel[u][0:PIXC, :])):
                    nc.scalar.activation(dst.rearrange("p (h n) -> p h n", h=2),
                                         src[0:C1, u % 2, :, 0:PIX // 2], ACT.Copy, scale=SLOPE).then_inc(scaled, 1)

            for u in range(4):
                image(0, u, True)
            with act.Fori(1, B // 4) as t:
                for u in range(4):
                    image(t, u, False)


def offset_phase(nc, off_w, off_vec, grid, hT_all, pos_scr):
    GI = 8
    NG = B // GI
    with ExitStack() as stack:
        sb, ps, sem = memories(nc, stack)
        w = sb("offset_weights", [P, TAPS, 2 * TAPS])
        bias = sb("offset_bias", [P, 1])
        base = sb("offset_grid", [P, GI * VIS])
        pos = sb("offset_pos", [P, NG, GI * VIS])
        acc = ps("offset_acc", [P, NG, 512])
        weights_in = sem("offset_weights_in")
        conv_done = sem("offset_conv_done")
        pos_ready = sem("offset_pos_ready")
        pos_out = sem("offset_pos_out")
        block = stack.enter_context(nc.Block())

        @block.sync
        def _(sp):
            sp.dma_start(w[0:C1, :, :], off_w).then_inc(weights_in, 16)
            sp.dma_start(bias[0:2 * TAPS, :], off_vec).then_inc(weights_in, 16)
            sp.dma_start(base[0:2 * TAPS, :], grid).then_inc(weights_in, 16)
            for g in range(NG):
                sp.wait_ge(pos_ready, g + 1)
                sp.dma_start(pos_scr[g * GI:(g + 1) * GI, :].rearrange("b (c n) -> c b n", n=VIS),
                             pos[0:2 * TAPS, g, :].rearrange("c (b n) -> c b n", n=VIS)).then_inc(pos_out, 16)
            sp.wait_ge(pos_out, 16 * NG)

        @block.tensor
        def _(pe):
            pe.wait_ge(weights_in, 48)
            taps = hT_all[0:C1, :].rearrange("p (b i r j s) -> p r s b i j", b=B, i=HO, r=K, j=HO, s=K)
            for g in range(NG):
                for kk in range(TAPS):
                    last = nc.tensor.matmul(acc[0:2 * TAPS, g, 0:GI * VIS], w[0:C1, kk, :],
                                            taps[:, kk // K, kk % K, g * GI:(g + 1) * GI],
                                            start=(kk == 0), stop=(kk == TAPS - 1))
                last.then_inc(conv_done, 1)

        @block.vector
        def _(dve):
            dve.wait_ge(weights_in, 48)
            for g in range(NG):
                dve.wait_ge(conv_done, g + 1)
                nc.vector.scalar_tensor_tensor(pos[0:2 * TAPS, g, :], acc[0:2 * TAPS, g, 0:GI * VIS],
                                               bias[0:2 * TAPS, 0:1], base[0:2 * TAPS, :],
                                               ALU.add, ALU.add).then_inc(pos_ready, 1)


def sample_phase(nc, pos_scr, pix_neg, pix_scr, samp_all):
    S2 = SAMPLES // 2
    with ExitStack() as stack:
        sb, ps, sem = memories(nc, stack)
        neg = sb("pixel_neg", [P, NPIXC + 1])
        pos = [sb(f"sample_pos{u}", [P, 2 * SAMPLES]) for u in range(2)]
        h = [sb(f"sample_h{u}", [P, PIX]) for u in range(2)]
        hx = [sb(f"hat_x{u}", [P, SAMPLES]) for u in range(2)]
        dy = [sb(f"dist_y{u}", [P, NPIXC, SAMPLES]) for u in range(2)]
        wt = sb("hat_weights", [P, 2, NPIXC, SAMPLES])
        acc = ps("sample_acc", [P, 2, 2, 512])
        const_in = sem("pixel_in")
        pos_in = [sem(f"sample_pos_in{u}") for u in range(2)]
        h_in = [sem(f"sample_h_in{u}") for u in range(2)]
        dist = sem("sample_dist")
        clipped = sem("sample_clipped")
        weights = sem("sample_weights")
        product = sem("sample_product")
        stored = sem("sample_stored")
        block = stack.enter_context(nc.Block())

        @block.sync
        def _(sp):
            sp.dma_start(neg[0:PIXC, :], pix_neg).then_inc(const_in, 16)

            def load(b, u):
                sp.dma_start(pos[u][0:PIXC, :], pos_scr[bass.ds(b, 1), :].rearrange("a n -> (a n)")
                             .partition_broadcast(PIXC)).then_inc(pos_in[u], 16)

            for u in range(2):
                load(u, u)
            with sp.Fori(1, B // 2) as t:
                for u in range(2):
                    sp.wait_ge(dist, 2 * t + u - 1)
                    load(2 * t + u, u)

        @block.gpsimd
        def _(pool):
            def load(b, u):
                pool.dma_start(h[u][0:PIXC, :], pix_scr[bass.ds(b, 1), :, :].rearrange("b p n -> p (b n)")
                               ).then_inc(h_in[u], 16)

            for u in range(2):
                load(u, u)
            with pool.Fori(1, B // 2) as t:
                for u in range(2):
                    pool.wait_ge(product, 2 * t + u - 1)
                    load(2 * t + u, u)

        @block.vector
        def _(dve):
            def weigh(t, u, first):
                s = Step(dve, clipped, 2 * (2 * t + u))
                dve.wait_ge(dist, 2 * t + u + 1)
                s.mark(nc.vector.tensor_scalar(hx[u][0:PIXC, :], hx[u][0:PIXC, :], 1.0, 1.0, ALU.min, ALU.subtract))
                s.run(nc.vector.tensor_scalar(dy[u][0:PIXC], dy[u][0:PIXC], 1.0, 1.0, ALU.min, ALU.subtract))
                if not first:
                    dve.wait_ge(product, 2 * t + u - 1)
                nc.vector.tensor_tensor(wt[0:PIXC, u], dy[u][0:PIXC],
                                        hx[u][0:PIXC, :].rearrange("p (a n) -> p a n", a=1)
                                        .to_broadcast([PIXC, NPIXC, SAMPLES]), ALU.mult).then_inc(weights, 1)

            for u in range(2):
                weigh(0, u, True)
            with dve.Fori(1, B // 2) as t:
                for u in range(2):
                    weigh(t, u, False)

        @block.scalar
        def _(act):
            act.wait_ge(const_in, 16)

            def distances(t, u, first):
                p = pos[u][0:PIXC, :].rearrange("p (k a n) -> p a k n", k=TAPS, a=2)
                act.wait_ge(pos_in[u], 16 * t + 16)
                if not first:
                    act.wait_ge(weights, 2 * t + u - 1)
                for c in range(NPIXC):
                    nc.scalar.activation(dy[u][0:PIXC, c, :].rearrange("p (k n) -> p k n", k=TAPS), p[:, 0],
                                         ACT.Abs, bias=neg[0:PIXC, c:c + 1])
                nc.scalar.activation(hx[u][0:PIXC, :].rearrange("p (k n) -> p k n", k=TAPS), p[:, 1],
                                     ACT.Abs, bias=neg[0:PIXC, NPIXC:NPIXC + 1]).then_inc(dist, 1)

            def store(t, u):
                act.wait_ge(product, 2 * t + u + 1)
                nc.scalar.activation(
                    samp_all[0:C1, :, bass.ds((2 * t + u) * VIS, VIS)],
                    acc[0:C1, u, :, 0:S2].rearrange("p h (k n) -> p h k n", n=VIS), ACT.Copy).then_inc(stored, 1)

            distances(0, 0, True)
            distances(0, 1, True)
            with act.Fori(1, B // 2) as t:
                for u in range(2):
                    distances(t, u, False)
                    store(t - 1, u)
            for u in range(2):
                store(B // 2 - 1, u)

        @block.tensor
        def _(pe):
            def image(t, u, first):
                pe.wait_ge(h_in[u], 16 * t + 16)
                pe.wait_ge(weights, 2 * t + u + 1)
                if not first:
                    pe.wait_ge(stored, 2 * t + u - 1)
                for half in range(2):
                    for c in range(NPIXC):
                        last = nc.tensor.matmul(acc[0:C1, u, half, 0:S2], h[u][0:PIXC, c * C1:(c + 1) * C1],
                                                wt[0:PIXC, u, c, half * S2:(half + 1) * S2],
                                                start=(c == 0), stop=(c == NPIXC - 1))
                last.then_inc(product, 1)

            for u in range(2):
                image(0, u, True)
            with pe.Fori(1, B // 2) as t:
                for u in range(2):
                    image(t, u, False)


def deform_phase(nc, dcn_w, vec, samp_all, vis_scr):
    with ExitStack() as stack:
        sb, ps, sem = memories(nc, stack)
        w = sb("deform_weights", [P, TAPS, D])
        rows = sb("deform_vectors", [P, 5, D])
        half = sb("deform_half", [P, D])
        std = sb("deform_std", [P, D])
        inv = sb("deform_inv", [P, D])
        tok = sb("deform_tokens", [P, VT, D])
        acc = ps("deform_acc", [P, 4, 512])
        vectors_in = sem("deform_in")
        half_set = sem("deform_half_set")
        bn = sem("deform_bn")
        bn_pow = sem("deform_pow")
        product = sem("deform_product")
        step = sem("deform_step")
        tok_ready = sem("deform_ready")
        tok_out = sem("deform_out")
        block = stack.enter_context(nc.Block())

        @block.sync
        def _(sp):
            sp.dma_start(rows[:, :, :], vec).then_inc(vectors_in, 16)
            sp.dma_start(w[0:C1, :, :], dcn_w).then_inc(vectors_in, 16)
            for t in range(VT):
                sp.wait_ge(tok_ready, t + 1)
                sp.dma_start(vis_scr[t * P:(t + 1) * P, :], tok[:, t, :]).then_inc(tok_out, 16)
            sp.wait_ge(tok_out, 16 * VT)

        @block.gpsimd
        def _(pool):
            pool.memset(half[:, :], -0.5).then_inc(half_set, 1)
            pool.wait_ge(half_set, 1)
            pool.wait_ge(bn, 1)
            pool.tensor_tensor(inv[:, :], std[:, :], half[:, :], ALU.pow).then_inc(bn_pow, 1)

        @block.tensor
        def _(pe):
            pe.wait_ge(vectors_in, 32)
            for t in range(VT):
                if t >= 4:
                    pe.wait_ge(step, 3 * (t - 4) + 1)
                for kk in range(TAPS):
                    last = nc.tensor.matmul(acc[:, t % 4, 0:D], samp_all[0:C1, kk, t * P:(t + 1) * P],
                                            w[0:C1, kk, :], start=(kk == 0), stop=(kk == TAPS - 1))
                last.then_inc(product, 1)

        @block.vector
        def _(dve):
            dve.wait_ge(vectors_in, 32)
            s = Step(dve, bn)
            shift = fold_norm(nc, dve, s, bn_pow, rows, std, inv, half)
            s = Step(dve, step)
            for t in range(VT):
                dve.wait_ge(product, t + 1)
                y = tok[:, t, :]
                s.run(nc.vector.tensor_tensor(y, acc[:, t % 4, 0:D], inv[:, :], ALU.mult))
                s.run(nc.vector.tensor_tensor(y, y, shift, ALU.add))
                s.run(nc.vector.scalar_tensor_tensor(y, y, SLOPE, y, ALU.mult, ALU.max))
                dve.sem_inc(tok_ready, 1)


def layer_norm(nc, dve, s, held, pow_done, pow_count, x, xn, stats, mv, ve, rstd, tmp):
    for n in range(4):
        s.mark(nc.vector.bn_stats(stats[0:ROWS, n, :], x[0:ROWS, n, :]))
    s.after(4)
    dve.sem_inc(held, 1)
    for n in range(4):
        last = s.mark(nc.vector.bn_aggr(mv[0:ROWS, n, :], stats[0:ROWS, n, :]))
    s.after(last)
    s.mark(nc.vector.tensor_scalar(ve[0:ROWS, :], mv[0:ROWS, :, 1], EPS, None, ALU.add))
    dve.wait_ge(pow_done, pow_count)
    s.run(nc.vector.tensor_tensor(tmp[0:ROWS, :], rstd[0:ROWS, :], rstd[0:ROWS, :], ALU.mult))
    s.run(nc.vector.tensor_tensor(tmp[0:ROWS, :], tmp[0:ROWS, :], ve[0:ROWS, :], ALU.mult))
    s.run(nc.vector.tensor_scalar(tmp[0:ROWS, :], tmp[0:ROWS, :], -0.5, 1.5, ALU.mult, ALU.add))
    s.run(nc.vector.tensor_tensor(rstd[0:ROWS, :], rstd[0:ROWS, :], tmp[0:ROWS, :], ALU.mult))
    for n in range(4):
        last = nc.vector.tensor_scalar(xn[0:ROWS, n, 0:D], x[0:ROWS, n, :], mv[0:ROWS, n, 0:1],
                                       rstd[0:ROWS, n:n + 1], ALU.subtract, ALU.mult)
        if n < 3:
            s.mark(last)
    return last


LN_VAR = 9
LN_STEPS = 16


def attend_phase(nc, a, vis_scr, txt_scr, h_scr):
    SCALE = DH ** -0.5
    VH = DH + 1
    NX = 22
    SC = 3 * TOK
    with ExitStack() as stack:
        sb, ps, sem = memories(nc, stack)
        wq = sb("attend_wq", [P, 2, HG, P])
        wk = sb("attend_wk", [P, 2, HG, P])
        wv = sb("attend_wv", [P, 2, D])
        wo = sb("attend_wo", [P, 2, D])
        bqk = sb("attend_bqk", [P, 2 * HG])
        brow = sb("attend_bv_bo", [P, 2, D])
        ident = sb("attend_identity", [P, P])
        identb = sb("attend_identity_bf16", [P, P], BF16)
        mask = sb("window_mask", [P, 2, SC])
        maskb = sb("window_mask_bf16", [P, 2, SC], BF16)
        minus_half = sb("attend_half", [P, 4])
        x = [sb(f"attend_x{u}", [P, 4, D]) for u in range(2)]
        resid = [sb(f"attend_resid{u}", [P, 4, D]) for u in range(2)]
        xn = sb("attend_xn", [P, 4, D])
        stats, mv = sb("attend_stats", [P, 4, 6]), sb("attend_mv", [P, 4, 2])
        ve, rstd, tmp = (sb(f"attend_{k}", [P, 4]) for k in ("ve", "rstd", "tmp"))
        xT = sb("attend_xT", [P, 2, PT])
        qT = [sb(f"attend_qT{u}", [P, HG, PT]) for u in range(2)]
        kT = [sb(f"attend_kT{u}", [P, HG, PT]) for u in range(2)]
        va = [sb(f"attend_v{u}", [P, 4, HEADS, VH]) for u in range(2)]
        mx = sb("attend_max", [P, 2, HEADS])
        pr = [sb(f"attend_probs{u}", [P, HEADS, TOK]) for u in range(2)]
        prT = [sb(f"attend_probsT{u}", [P, 2 * HEADS, ROWS]) for u in range(2)]
        den = sb("attend_den", [P, HEADS])
        o = [sb(f"attend_o{u}", [P, D]) for u in range(2)]
        oT = [sb(f"attend_oT{u}", [P, 2, ROWS]) for u in range(2)]
        h2 = [sb(f"attend_h{u}", [P, 4, D]) for u in range(2)]
        sc = ps("scores", [P, 4, 512])
        tp = ps("probs_transposed", [P, 2, 512])
        xb = ps("attend_spare", [P, 2, 512])
        dve_held, pe_held = sem("attend_dve_held"), sem("attend_pe_held")
        const_in, consts, ones_set, half_set = sem("attend_const_in"), sem("attend_consts"), sem("attend_ones"), sem("attend_half_set")
        x_in = [sem(f"attend_x_in{u}") for u in range(2)]
        resid_ready = sem("attend_resid_ready")
        ln, pow_done, xn_ready = sem("attend_ln"), sem("attend_pow"), sem("attend_xn_ready")
        filled = [sem(f"spare_filled{i}") for i in range(2)]
        emptied = [sem(f"spare_emptied{i}") for i in range(2)]
        xT_ready = sem("attend_xT_ready")
        qkT_ready = sem("attend_qkT_ready")
        v_ready = sem("attend_v_ready")
        scored = sem("attend_scored")
        maxed = sem("attend_maxed")
        shifted = sem("attend_shifted")
        exped = sem("attend_exped")
        turned = sem("attend_turned")
        turned_read = sem("attend_turned_read")
        inverted = sem("attend_inverted")
        o_ready = sem("attend_o_ready")
        oT_ready = sem("attend_oT_ready")
        h_ready = sem("attend_h_ready")
        h_out = [sem(f"attend_h_out{u}") for u in range(2)]
        block = stack.enter_context(nc.Block())
        NCONST = 9

        V0 = (8, 9)
        XT_USE, Q_USE, K_USE, V_USE = (1, 2), (6, 7, 8), (12, 13, 14), (15, 16)
        O_USE, OT_USE, Y_USE = (0, 3, 9, 17), (4, 10, 18, 20), (5, 11, 19, 21)

        def use(t, k):
            skipped = 0
            if isinstance(t, int) and t == PAIRS - 1:
                skipped = sum(j < k and j % 2 == k % 2 for j in XT_USE + Q_USE + K_USE + V_USE)
            return k % 2, 5 + (NX // 2) * t + k // 2 - skipped

        @block.sync
        def _(sp):
            for dst, src in ((wq, a["wq"]), (wk, a["wk"]), (wv, a["wv"]), (wo, a["wo"]), (bqk, a["bqk"]),
                             (brow, a["bv_bo"]), (ident, a["identity"]), (mask, a["mask"])):
                sp.dma_start(dst[:], src).then_inc(const_in, 16)

            vis = vis_scr.rearrange("(b v) d -> v b d", v=VIS)
            txt = txt_scr.rearrange("(b v) d -> v b d", v=TXT)
            rest = ROWS - VIS

            def load(t, u):
                b = bass.ds(2 * t, 2)
                even, odd = x[u][:, 0:4:2, :], x[u][:, 1:4:2, :]
                sp.dma_start(even[0:VIS], vis[:, b, :]).then_inc(x_in[u], 16)
                sp.dma_start(even[VIS:ROWS], txt[0:rest, b, :]).then_inc(x_in[u], 16)
                sp.dma_start(odd[0:ROWS], txt[rest:TXT, b, :]).then_inc(x_in[u], 16)

            def leave(t, u):
                sp.wait_ge(h_ready, 4 * t + 4)
                sp.dma_start(h_scr[bass.ds(t * PT, PT), :].rearrange("(n p) d -> p n d", p=ROWS),
                             h2[u][0:ROWS]).then_inc(h_out[u], 16)

            load(0, 0)
            load(1, 1)
            with sp.Fori(0, PAIRS // 2 - 1) as tt:
                for u in range(2):
                    sp.wait_ge(resid_ready, 2 * tt + u + 1)
                    sp.wait_ge(xn_ready, 2 * tt + u + 1)
                    load(2 * tt + u + 2, u)
                    leave(2 * tt + u, u)
            for u in range(2):
                leave(PAIRS - 2 + u, u)
            for u in range(2):
                sp.wait_ge(h_out[u], 16 * (PAIRS // 2))

        @block.gpsimd
        def _(pool):
            pool.memset(minus_half[:, :], -0.5).then_inc(half_set, 1)
            for u in range(2):
                pool.memset(va[u][:], 1.0).then_inc(ones_set, 1)
            pool.wait_ge(half_set, 1)
            pool.wait_ge(ones_set, 2)
            pool.wait_ge(const_in, 16 * (NCONST - 1))

            def pair(tt, u):
                t = 2 * tt + u
                pool.wait_ge(ln, LN_STEPS * t + LN_VAR)
                pool.tensor_tensor(rstd[0:ROWS, :], ve[0:ROWS, :], minus_half[0:ROWS, :], ALU.pow).then_inc(pow_done, 1)
                if not (isinstance(tt, int) and tt == 0):
                    pool.wait_ge(h_ready, 4 * t - 4)
                pool.tensor_tensor(resid[u][0:ROWS], x[u][0:ROWS],
                                   brow[0:ROWS, 1:2, :].to_broadcast([ROWS, 4, D]), ALU.add).then_inc(resid_ready, 1)

            pair(0, 0)
            pair(0, 1)
            with pool.Fori(1, PAIRS // 2) as tt:
                for u in range(2):
                    pair(tt, u)

        @block.vector
        def _(dve):
            dve.wait_ge(const_in, 16 * (NCONST - 1))
            nc.vector.tensor_copy(identb[:], ident[:]).then_inc(consts, 1)
            nc.vector.tensor_copy(maskb[:], mask[:]).then_inc(consts, 1)
            dve.wait_ge(ones_set, 2)

            def norm(tt, u):
                t = 2 * tt + u
                dve.wait_ge(x_in[u], 48 * tt + 48)
                last = layer_norm(nc, dve, Step(dve, ln, LN_STEPS * t), dve_held, pow_done, t + 1, x[u], xn, stats, mv,
                                  ve, rstd, tmp)
                last.then_inc(xn_ready, 1)

            def softmax_in(t, n):
                g = 4 * t + n
                m = mx[0:ROWS, n % 2, :].rearrange("p (j k) -> p j k", j=4)
                s4 = sc[0:ROWS, :, 0:SC].rearrange("p j (k n) -> p j k n", n=TOK)
                dve.wait_ge(scored, g + 1)
                nc.vector.tensor_reduce(m, s4, AX_X, ALU.max).then_inc(maxed, 1)
                dve.wait_ge(maxed, g + 1)
                nc.vector.tensor_tensor(pr[n % 2][0:ROWS].rearrange("p (j k) n -> p j k n", j=4), s4,
                                        m.rearrange("p j (k n) -> p j k n", n=1).to_broadcast([ROWS, 4, 3, TOK]),
                                        ALU.subtract).then_inc(shifted, 1)

            def weigh(t, n):
                bank, c = use(t, O_USE[n])
                acc = xb[0:ROWS, bank, 0:HEADS * VH].rearrange("p (h d) -> p h d", d=VH)
                dve.wait_ge(filled[bank], c + 1)
                nc.vector.reciprocal(den[0:ROWS, :].rearrange("p (h a) -> p h a", a=1),
                                     acc[:, :, DH:VH]).then_inc(inverted, 1)
                dve.wait_ge(inverted, 4 * t + n + 1)
                nc.vector.tensor_tensor(o[n % 2][0:ROWS, :].rearrange("p (h d) -> p h d", d=DH), acc[:, :, 0:DH],
                                        den[0:ROWS, :].rearrange("p (h a) -> p h a", a=1)
                                        .to_broadcast([ROWS, HEADS, DH]), ALU.mult).then_inc(o_ready, 1)
                dve.wait_ge(o_ready, 4 * t + n + 1)
                dve.sem_inc(emptied[bank], 1)

            def residual(t, u, n):
                bank, c = use(t, Y_USE[n])
                dve.wait_ge(filled[bank], c + 1)
                nc.vector.tensor_tensor(h2[u][0:ROWS, n, :], xb[0:ROWS, bank, 0:D], resid[u][0:ROWS, n, :],
                                        ALU.add).then_inc(emptied[bank], 1)
                dve.wait_ge(emptied[bank], c + 1)
                dve.sem_inc(h_ready, 1)

            def values(t, u, first):
                for i in range(2):
                    bank, c = (V0[i] % 2, V0[i] // 2) if first else use(t - 1, V_USE[i])
                    dve.wait_ge(filled[bank], c + 1)
                    for n in range(2):
                        last = nc.vector.tensor_tensor(
                            va[u][0:ROWS, 2 * i + n, :, 0:DH],
                            xb[0:ROWS, bank, n * D:(n + 1) * D].rearrange("p (h d) -> p h d", d=DH),
                            brow[0:ROWS, 0, :].rearrange("p (h d) -> p h d", d=DH), ALU.add)
                        last.then_inc(v_ready, 1)
                    dve.wait_ge(v_ready, 4 * t + 2 * i + 2)
                    dve.sem_inc(emptied[bank], 1)

            def pair(tt, u, last):
                t = 2 * tt + u
                softmax_in(t, 1)
                if not last:
                    norm(tt + (u + 1) // 2, (u + 1) % 2)
                weigh(t, 0)
                softmax_in(t, 2)
                weigh(t, 1)
                if not_first(tt, u):
                    dve.wait_ge(h_out[u], 16 * tt)
                dve.wait_ge(resid_ready, t + 1)
                residual(t, u, 0)
                softmax_in(t, 3)
                weigh(t, 2)
                residual(t, u, 1)
                if not last:
                    values(t + 1, (u + 1) % 2, False)
                    softmax_in(t + 1, 0)
                weigh(t, 3)
                residual(t, u, 2)
                residual(t, u, 3)

            def not_first(tt, u):
                return not (isinstance(tt, int) and tt == 0)

            norm(0, 0)
            values(0, 0, True)
            softmax_in(0, 0)
            for u in range(2):
                pair(0, u, False)
            with dve.Fori(1, PAIRS // 2 - 1) as tt:
                for u in range(2):
                    pair(tt, u, False)
            for u in range(2):
                pair(PAIRS // 2 - 1, u, u == 1)

        @block.scalar
        def _(act):
            act.wait_ge(const_in, 16 * (NCONST - 1))

            def empty(dst, src, bank, c, done, bias=None):
                act.wait_ge(filled[bank], c + 1)
                if bias is None:
                    nc.scalar.activation(dst, src, ACT.Copy).then_inc(emptied[bank], 1)
                else:
                    nc.scalar.activation(dst, src, ACT.Identity, bias=bias).then_inc(emptied[bank], 1)
                act.wait_ge(emptied[bank], c + 1)
                act.sem_inc(done, 1)

            def project(t, u, part, at):
                if part == "x":
                    for i, rows in enumerate((D0, D1)):
                        bank, c = at(i)
                        empty(xT[0:rows, i, :], xb[0:rows, bank, 0:PT], bank, c, xT_ready)
                else:
                    dst, off = (qT, 0) if part == "q" else (kT, HG)
                    for g in range(HG):
                        bank, c = at(g)
                        empty(dst[u][:, g, :], xb[:, bank, 0:PT], bank, c, qkT_ready, bqk[:, off + g:off + g + 1])

            def softmax(t, n):
                g = 4 * t + n
                y = pr[n % 2][0:ROWS]
                act.wait_ge(shifted, g + 1)
                nc.scalar.activation(y, y, ACT.Exp, scale=SCALE).then_inc(exped, 1)
                for f in range(4):
                    act.wait_ge(turned, 4 * g + f + 1)
                    nc.scalar.activation(prT[n % 2][0:ROWS, 6 * f:6 * f + 6, :],
                                         tp[0:ROWS, f % 2, 0:6 * ROWS].rearrange("p (a n) -> p a n", n=ROWS),
                                         ACT.Copy).then_inc(turned_read, 1)

            def out_transposed(t, n):
                bank, c = use(t, OT_USE[n])
                act.wait_ge(filled[bank], c + 1)
                nc.scalar.activation(oT[n % 2][0:D0, 0, :], xb[0:D0, bank, 0:ROWS], ACT.Copy).then_inc(oT_ready, 1)
                nc.scalar.activation(oT[n % 2][0:D1, 1, :], xb[0:D1, bank, P:P + ROWS], ACT.Copy).then_inc(oT_ready, 1)
                act.wait_ge(oT_ready, 8 * t + 2 * n + 2)
                act.sem_inc(emptied[bank], 1)

            def pair(tt, u, last):
                t = 2 * tt + u
                v = (u + 1) % 2
                softmax(t, 0)
                if not last:
                    project(t + 1, v, "x", lambda i: use(t, XT_USE[i]))
                softmax(t, 1)
                out_transposed(t, 0)
                if not last:
                    project(t + 1, v, "q", lambda i: use(t, Q_USE[i]))
                softmax(t, 2)
                out_transposed(t, 1)
                if not last:
                    project(t + 1, v, "k", lambda i: use(t, K_USE[i]))
                softmax(t, 3)
                out_transposed(t, 2)
                out_transposed(t, 3)

            project(0, 0, "x", lambda i: (i % 2, i // 2))
            project(0, 0, "q", lambda i: (i % 2, 1 + i // 2))
            project(0, 0, "k", lambda i: ((i + 1) % 2, 1 + (3 + i) // 2))
            with act.Fori(0, PAIRS // 2 - 1) as tt:
                for u in range(2):
                    pair(tt, u, False)
            for u in range(2):
                pair(PAIRS // 2 - 1, u, u == 1)

        @block.tensor
        def _(pe):
            pe.wait_ge(const_in, 16 * (NCONST - 1))
            pe.wait_ge(consts, 2)

            def claim(bank, c):
                if not (isinstance(c, int) and c == 0):
                    pe.wait_ge(emptied[bank], c)

            def turn_x(t, at):
                pe.wait_ge(xn_ready, t + 1)
                for i, (d, rows) in enumerate(((0, D0), (D0, D1))):
                    bank, c = at(i)
                    claim(bank, c)
                    pe.sem_inc(pe_held, 1)
                    for n in range(4):
                        last = nc.tensor.transpose(xb[0:rows, bank, n * ROWS:(n + 1) * ROWS],
                                                   xn[0:ROWS, n, d:d + rows], ident[0:ROWS, 0:ROWS])
                    last.then_inc(filled[bank], 1)

            def project(t, u, w, at):
                if w is wq:
                    pe.wait_ge(xT_ready, 2 * t + 2)
                for g in range(HG):
                    bank, c = at(g)
                    claim(bank, c)
                    nc.tensor.matmul(xb[:, bank, 0:PT], w[0:D0, 0, g, :], xT[0:D0, 0, :], start=True, stop=False)
                    nc.tensor.matmul(xb[:, bank, 0:PT], w[0:D1, 1, g, :], xT[0:D1, 1, :],
                                     start=False, stop=True).then_inc(filled[bank], 1)

            def values(at):
                for i in range(2):
                    bank, c = at(i)
                    claim(bank, c)
                    for n in range(2):
                        cols = slice((2 * i + n) * ROWS, (2 * i + n + 1) * ROWS)
                        y = xb[0:ROWS, bank, n * D:(n + 1) * D]
                        nc.tensor.matmul(y, xT[0:D0, 0, cols], wv[0:D0, 0, :], start=True, stop=False)
                        last = nc.tensor.matmul(y, xT[0:D1, 1, cols], wv[0:D1, 1, :], start=False, stop=True)
                    last.then_inc(filled[bank], 1)

            def scores(t, u, n, first=False):
                g_ = 4 * t + n
                if n == 0:
                    pe.wait_ge(qkT_ready, 6 * t + 6)
                if not first:
                    pe.wait_ge(shifted, g_)
                for j in range(4):
                    nc.tensor.matmul(sc[0:ROWS, j, 0:SC], identb[0:ROWS, 0:ROWS], maskb[0:ROWS, n % 2, :],
                                     start=True, stop=False)
                for g in range(HG):
                    for j in range(4):
                        r = slice(32 * j, 32 * j + DH)
                        last = nc.tensor.matmul(sc[0:ROWS, j, g * TOK:(g + 1) * TOK],
                                                qT[u][r, g, n * ROWS:(n + 1) * ROWS],
                                                kT[u][r, g, n // 2 * TOK:(n // 2 + 1) * TOK],
                                                start=False, stop=(g == HG - 1))
                last.then_inc(scored, 1)

            def mix(t, u, n, first):
                g_ = 4 * t + n
                pe.wait_ge(exped, g_ + 1)
                for f in range(4):
                    if not (first and f < 2):
                        pe.wait_ge(turned_read, 4 * g_ + f - 1)
                    for i in range(6):
                        h, c = divmod(6 * f + i, 2)
                        last = nc.tensor.transpose(tp[0:ROWS, f % 2, i * ROWS:(i + 1) * ROWS],
                                                   pr[n % 2][0:ROWS, h, c * ROWS:(c + 1) * ROWS],
                                                   ident[0:ROWS, 0:ROWS])
                    last.then_inc(turned, 1)
                bank, c = use(t, O_USE[n])
                claim(bank, c)
                if n == 0:
                    pe.wait_ge(v_ready, 4 * t + 4)
                pe.wait_ge(turned_read, 4 * g_ + 4)
                for k in range(HEADS):
                    head = 4 * (k % HG) + k // HG
                    for c in range(2):
                        last = nc.tensor.matmul(xb[0:ROWS, bank, head * VH:(head + 1) * VH],
                                                prT[n % 2][0:ROWS, 2 * k + c, :], va[u][0:ROWS, n // 2 * 2 + c, head, :],
                                                start=(c == 0), stop=(c == 1))
                last.then_inc(filled[bank], 1)

            def project_out(t, n):
                g_ = 4 * t + n
                bank, c = use(t, OT_USE[n])
                claim(bank, c)
                pe.wait_ge(o_ready, g_ + 1)
                nc.tensor.transpose(xb[0:D0, bank, 0:ROWS], o[n % 2][0:ROWS, 0:D0], ident[0:ROWS, 0:ROWS])
                nc.tensor.transpose(xb[0:D1, bank, P:P + ROWS], o[n % 2][0:ROWS, D0:D],
                                    ident[0:ROWS, 0:ROWS]).then_inc(filled[bank], 1)
                bank, c = use(t, Y_USE[n])
                claim(bank, c)
                pe.wait_ge(oT_ready, 2 * g_ + 2)
                nc.tensor.matmul(xb[0:ROWS, bank, 0:D], oT[n % 2][0:D0, 0, :], wo[0:D0, 0, :], start=True, stop=False)
                nc.tensor.matmul(xb[0:ROWS, bank, 0:D], oT[n % 2][0:D1, 1, :], wo[0:D1, 1, :],
                                 start=False, stop=True).then_inc(filled[bank], 1)

            def pair(tt, u, last, first=False):
                t = 2 * tt + u
                v = (u + 1) % 2
                scores(t, u, 1)
                mix(t, u, 0, first)
                if not last:
                    turn_x(t + 1, lambda i: use(t, XT_USE[i]))
                scores(t, u, 2)
                mix(t, u, 1, False)
                project_out(t, 0)
                if not last:
                    project(t + 1, v, wq, lambda i: use(t, Q_USE[i]))
                scores(t, u, 3)
                mix(t, u, 2, False)
                project_out(t, 1)
                if not last:
                    project(t + 1, v, wk, lambda i: use(t, K_USE[i]))
                    values(lambda i: use(t, V_USE[i]))
                    scores(t + 1, v, 0)
                mix(t, u, 3, False)
                project_out(t, 2)
                project_out(t, 3)

            turn_x(0, lambda i: (i % 2, i // 2))
            project(0, 0, wq, lambda i: (i % 2, 1 + i // 2))
            project(0, 0, wk, lambda i: ((i + 1) % 2, 1 + (3 + i) // 2))
            values(lambda i: (V0[i] % 2, V0[i] // 2))
            scores(0, 0, 0, True)
            pair(0, 0, False, True)
            pair(0, 1, False)
            with pe.Fori(1, PAIRS // 2 - 1) as tt:
                for u in range(2):
                    pair(tt, u, False)
            for u in range(2):
                pair(PAIRS // 2 - 1, u, u == 1)


class Spline:

    def __init__(self, nc, sb, sem, name, cols):
        self.nc, self.cols = nc, cols
        self.s, self.t, self.a, self.a2, self.b, self.b2 = (
            sb(f"{name}_{k}", [P, cols]) for k in ("s", "t", "a", "a2", "b", "b2"))
        self.n = [sb(f"{name}_n{u}", [P, cols]) for u in range(2)]
        self.v = [sb(f"{name}_v{u}", [P, cols]) for u in range(2)]
        self.f = [sb(f"{name}_f{i}", [P, cols]) for i in range(4)]
        (self.s_ready, self.n_ready, self.z_ready, self.t_ready, self.a_ready, self.a2_ready, self.b_ready,
         self.b2_ready, self.a3_ready, self.b3_ready, self.v_ready, self.f_ready, self.f_used) = (
            sem(f"{name}_{k}") for k in ("s_ready", "n_ready", "z_ready", "t_ready", "a_ready", "a2_ready", "b_ready",
                                         "b2_ready", "a3_ready", "b3_ready", "v_ready", "f_ready", "f_used"))

        self.held = sem(f"{name}_pool_held")

    def round_act(self, act, k, u, first, parts):
        act.wait_ge(self.s_ready, parts * (k + 1))
        if not first:
            act.wait_ge(self.f_ready, 4 * (k - 1))
        self.nc.scalar.activation(self.n[u][:], self.s[:], ACT.Copy, bias=MAGIC).then_inc(self.n_ready, 1)

    def powers_act(self, act, k, first):
        act.wait_ge(self.z_ready, k + 1)
        if not first:
            act.wait_ge(self.a_ready, k)
        self.nc.scalar.activation(self.t[:], self.s[:], ACT.Abs, scale=4.0).then_inc(self.t_ready, 1)
        act.wait_ge(self.t_ready, k + 1)
        if not first:
            act.wait_ge(self.v_ready, k)
        self.nc.scalar.activation(self.b[:], self.t[:], ACT.Relu, bias=1.0, scale=-1.0).then_inc(self.b_ready, 1)
        self.nc.scalar.activation(self.a2[:], self.t[:], ACT.Square, bias=2.0, scale=-1.0).then_inc(self.a2_ready, 1)
        act.wait_ge(self.b_ready, k + 1)
        self.nc.scalar.activation(self.b2[:], self.b[:], ACT.Square, scale=2.0).then_inc(self.b2_ready, 1)

    def cube_pool(self, pool, k, first):
        if not first:
            pool.wait_ge(self.a3_ready, k)
        pool.wait_ge(self.t_ready, k + 1)
        pool.sem_inc(self.held, 1)
        pool.tensor_scalar(self.a[:], self.t[:], -1.0, 2.0, ALU.mult, ALU.add).then_inc(self.a_ready, 1)
        pool.wait_ge(self.b2_ready, k + 1)
        pool.tensor_tensor(self.b2[:], self.b2[:], self.b[:], ALU.mult).then_inc(self.b3_ready, 1)

    def center_dve(self, dve, k, u):
        dve.wait_ge(self.n_ready, k + 1)
        self.nc.vector.scalar_tensor_tensor(self.s[:], self.n[u][:], MAGIC, self.s[:], ALU.subtract,
                                            ALU.subtract).then_inc(self.z_ready, 1)

    def cube_dve(self, dve, k):
        dve.wait_ge(self.a_ready, k + 1)
        dve.wait_ge(self.a2_ready, k + 1)
        self.nc.vector.tensor_tensor(self.a2[:], self.a2[:], self.a[:], ALU.mult).then_inc(self.a3_ready, 1)

    def value_dve(self, dve, k, u):
        dve.wait_ge(self.b3_ready, k + 1)
        dve.wait_ge(self.a3_ready, k + 1)
        self.nc.vector.tensor_tensor(self.v[u][:], self.a2[:], self.b2[:], ALU.subtract).then_inc(self.v_ready, 1)

    def take_dve(self, dve, k, u, i, first):
        if i == 0:
            dve.wait_ge(self.v_ready, k + 1)
        if not first:
            dve.wait_ge(self.f_used, 4 * k + i - 3)
        self.nc.vector.scalar_tensor_tensor(self.f[i][:], self.n[u][:], MAGIC + i, self.v[u][:], ALU.is_equal,
                                            ALU.mult).then_inc(self.f_ready, 1)


def spline1_phase(nc, a, h_scr, hid_scr):
    SETS = 6
    W2X = 2 * D0
    MC = HID // P
    with ExitStack() as stack:
        sb, ps, sem = memories(nc, stack)
        spl = Spline(nc, sb, sem, "spline1", SETS * PT)
        w = sb("spline1_weights", [P, 4, SETS, HID])
        bias = sb("spline1_offset", [P, SETS])
        ident = sb("spline1_identity", [P, P])
        minus_half = sb("spline1_half", [P, 4])
        x = [sb(f"spline1_x{u}", [P, 4, D]) for u in range(2)]
        xn = sb("spline1_xn", [P, 4, W2X])
        stats, mv = sb("spline1_stats", [P, 4, 6]), sb("spline1_mv", [P, 4, 2])
        ve, rstd, tmp = (sb(f"spline1_{k}", [P, 4]) for k in ("ve", "rstd", "tmp"))
        hid = [sb(f"spline1_hid{u}", [P, PT]) for u in range(2)]
        acc = ps("spline1_acc", [P, MC, 512])
        xT = ps("spline1_xT", [P, 2, 512])
        dve_held = sem("spline1_dve_held")
        const_in, w_in, half_set = sem("spline1_const_in"), sem("spline1_w_in"), sem("spline1_half_set")
        x_in = [sem(f"spline1_x_in{u}") for u in range(2)]
        ln, pow_done, xn_ready, twice = (sem(f"spline1_{k}") for k in ("ln", "pow", "xn_ready", "twice"))
        xT_ready = sem("spline1_xT_ready")
        summed = sem("spline1_summed")
        emptied = sem("spline1_emptied")
        hid_out = [sem(f"spline1_hid_out{u}") for u in range(2)]
        block = stack.enter_context(nc.Block())

        @block.sync
        def _(sp):
            sp.dma_start(ident[:], a["identity"]).then_inc(const_in, 16)
            sp.dma_start(bias[:], a["spline1_bias"]).then_inc(const_in, 16)

            def load(t, u):
                sp.dma_start(x[u][0:ROWS], h_scr[bass.ds(t * PT, PT), :].rearrange("(n p) d -> p n d", p=ROWS)
                             ).then_inc(x_in[u], 16)

            def leave(t):
                for m in range(MC):
                    sp.wait_ge(emptied, MC * t + m + 1)
                    sp.dma_start(hid_scr[:, m, bass.ds(t * PT, PT)], hid[m % 2][:]).then_inc(hid_out[m % 2], 16)

            def reload(t, u):
                sp.wait_ge(xn_ready, t - 1)
                load(t, u)

            load(0, 0)
            load(1, 1)
            sp.dma_start(w[:], a["w1"]).then_inc(w_in, 16)
            reload(2, 0)
            with sp.Fori(0, PAIRS // 2 - 2) as tt:
                for u in range(2):
                    reload(2 * tt + u + 3, 1 - u)
                    leave(2 * tt + u)
            reload(PAIRS - 1, 1)
            for t in range(PAIRS - 4, PAIRS):
                leave(t)
            for u in range(2):
                sp.wait_ge(hid_out[u], 16 * (MC // 2) * PAIRS)

        @block.gpsimd
        def _(pool):
            pool.memset(minus_half[:, :], -0.5).then_inc(half_set, 1)
            pool.wait_ge(half_set, 1)

            def norm(t):
                pool.wait_ge(ln, LN_STEPS * t + LN_VAR)
                pool.tensor_tensor(rstd[0:ROWS, :], ve[0:ROWS, :], minus_half[0:ROWS, :], ALU.pow).then_inc(pow_done, 1)
                pool.wait_ge(xn_ready, t + 1)
                pool.sem_inc(spl.held, 1)
                pool.tensor_copy(xn[0:ROWS, :, D:W2X], xn[0:ROWS, :, D0:D]).then_inc(twice, 1)

            norm(0)
            spl.cube_pool(pool, 0, True)
            norm(1)
            with pool.Fori(1, PAIRS - 1) as t:
                spl.cube_pool(pool, t, False)
                norm(t + 1)
            spl.cube_pool(pool, PAIRS - 1, False)

        @block.vector
        def _(dve):
            dve.wait_ge(const_in, 32)

            def norm(t, tt, u, first=False):
                dve.wait_ge(x_in[u], 16 * tt + 16)
                if not first:
                    dve.wait_ge(xT_ready, t)
                layer_norm(nc, dve, Step(dve, ln, LN_STEPS * t), dve_held, pow_done, t + 1, x[u], xn, stats, mv,
                           ve, rstd, tmp).then_inc(xn_ready, 1)

            def tile(tt, u, first, more, more2):
                k, v = 2 * tt + u, (u + 1) % 2
                spl.take_dve(dve, k, u, 0, first)
                if more:
                    spl.center_dve(dve, k + 1, v)
                spl.take_dve(dve, k, u, 1, first)
                if more2:
                    norm(k + 2, tt + 1, u)
                spl.take_dve(dve, k, u, 2, first)
                if more:
                    spl.cube_dve(dve, k + 1)
                spl.take_dve(dve, k, u, 3, first)
                if more:
                    spl.value_dve(dve, k + 1, v)

            norm(0, 0, 0, True)
            spl.center_dve(dve, 0, 0)
            spl.cube_dve(dve, 0)
            spl.value_dve(dve, 0, 0)
            norm(1, 0, 1)
            tile(0, 0, True, True, True)
            tile(0, 1, False, True, True)
            with dve.Fori(1, PAIRS // 2 - 1) as tt:
                for u in range(2):
                    tile(tt, u, False, True, True)
            tile(PAIRS // 2 - 1, 0, False, True, False)
            tile(PAIRS // 2 - 1, 1, False, False, False)

        @block.scalar
        def _(act):
            act.wait_ge(const_in, 32)

            def basis(tt, u, first, second=False):
                k = 2 * tt + u
                act.wait_ge(xT_ready, k + 1)
                for r in range(SETS):
                    nc.scalar.activation(spl.s[:, r * PT:(r + 1) * PT], xT[:, r // 4, 0:PT], ACT.Identity,
                                         bias=bias[:, r:r + 1], scale=SPL_SCALE).then_inc(spl.s_ready, 1)
                spl.round_act(act, k, u, first or second, SETS)
                spl.powers_act(act, k, first)

            def empty(t, first):
                for m in range(MC):
                    if m < MC - 1:
                        act.wait_ge(summed, (MC - 1) * t + m + 1)
                    else:
                        act.wait_ge(spl.f_used, 4 * t + 4)
                    if not (first and m < 2):
                        act.wait_ge(hid_out[m % 2], 16 * ((MC // 2) * t + m // 2))
                    nc.scalar.activation(hid[m % 2][:], acc[:, m, 0:PT], ACT.Copy, scale=1.0 / 6.0).then_inc(emptied, 1)

            basis(0, 0, True)
            basis(0, 1, False, True)
            empty(0, True)
            with act.Fori(1, PAIRS // 2) as tt:
                basis(tt, 0, False)
                empty(2 * tt - 1, False)
                basis(tt, 1, False)
                empty(2 * tt, False)
            empty(PAIRS - 1, False)

        @block.tensor
        def _(pe):
            def turn(t, first=False):
                pe.wait_ge(xn_ready, t + 1)
                pe.wait_ge(twice, t + 1)
                if not first:
                    pe.wait_ge(spl.s_ready, SETS * t)
                for i in range(2):
                    for n in range(4):
                        last = nc.tensor.transpose(xT[:, i, n * ROWS:(n + 1) * ROWS],
                                                   xn[0:ROWS, n, i * D0:(i + 1) * D0], ident[0:ROWS, 0:ROWS])
                last.then_inc(xT_ready, 1)

            def layer(k, first, more):
                for i in range(4):
                    pe.wait_ge(spl.f_ready, 4 * k + i + 1)
                    for r in range(SETS):
                        for m in range(MC):
                            start, stop = i == 0 and r == 0, i == 3 and r == SETS - 1
                            if start and not first:
                                pe.wait_ge(emptied, MC * (k - 1) + m + 1)
                            last = nc.tensor.matmul(acc[:, m, 0:PT], w[:, i, r, m * P:(m + 1) * P],
                                                    spl.f[i][:, r * PT:(r + 1) * PT], start=start, stop=stop)
                            if stop and m < MC - 1:
                                last.then_inc(summed, 1)
                    last.then_inc(spl.f_used, 1)
                    if i == 0 and more:
                        turn(k + 2)

            pe.wait_ge(const_in, 32)
            turn(0, True)
            turn(1)
            pe.wait_ge(w_in, 16)
            layer(0, True, True)
            with pe.Fori(1, PAIRS - 2) as k:
                layer(k, False, True)
            layer(PAIRS - 2, False, False)
            layer(PAIRS - 1, False, False)


def spline2_phase(nc, a, h_scr, hid_scr, out):
    CH = HID // P
    SETS = 4 * CH
    with ExitStack() as stack:
        sb, ps, sem = memories(nc, stack)
        spl = Spline(nc, sb, sem, "spline2", SETS * P)
        w = sb("spline2_weights", [P, 4, SETS, D])
        bias = sb("spline2_offset", [P, 4])
        x = [sb(f"spline2_x{u}", [P, CH, P]) for u in range(2)]
        h = [sb(f"spline2_h{u}", [P, D]) for u in range(2)]
        y = [sb(f"spline2_y{u}", [P, D]) for u in range(2)]
        acc = ps("spline2_acc", [P, 2, 512])
        const_in, w_in = sem("spline2_const_in"), sem("spline2_w_in")
        x_in = [sem(f"spline2_x_in{u}") for u in range(2)]
        h_in = [sem(f"spline2_h_in{u}") for u in range(2)]
        y_ready = sem("spline2_y_ready")
        y_out = [sem(f"spline2_y_out{u}") for u in range(2)]
        block = stack.enter_context(nc.Block())

        @block.sync
        def _(sp):
            sp.dma_start(bias[:], a["spline2_bias"]).then_inc(const_in, 16)

            def load_h(t, u):
                sp.dma_start(h[u][:], h_scr[bass.ds(t * P, P), :]).then_inc(h_in[u], 16)

            def tile(k, u, more=True):
                sp.wait_ge(y_ready, k + 1)
                sp.dma_start(out[bass.ds(k * P, P), :], y[u][:]).then_inc(y_out[u], 16)
                if more:
                    load_h(k + 2, u)

            sp.dma_start(w[:], a["w2"]).then_inc(w_in, 16)
            load_h(0, 0)
            load_h(1, 1)
            tile(0, 0)
            with sp.Fori(0, OT // 2 - 1) as tt:
                tile(2 * tt + 1, 1)
                tile(2 * tt + 2, 0)
            tile(OT - 2, 1, False)
            tile(OT - 1, 0, False)
            sp.wait_ge(y_out[0], 16 * (OT // 2 + 1))
            sp.wait_ge(y_out[1], 16 * (OT // 2))

        @block.gpsimd
        def _(pool):
            spl.cube_pool(pool, 0, True)
            with pool.Fori(1, OT) as k:
                spl.cube_pool(pool, k, False)

        @block.scalar
        def _(act):
            act.wait_ge(const_in, 16)

            def load_x(t, u):
                act.dma_start(x[u][:], hid_scr[:, :, bass.ds(t * P, P)]).then_inc(x_in[u], 16)

            def basis(tt, k, u, first=False, second=False, more=True):
                act.wait_ge(x_in[u], 16 * tt + 16)
                for r in range(4):
                    nc.scalar.activation(spl.s[:, r * HID:(r + 1) * HID].rearrange("p (c n) -> p c n", c=CH), x[u][:],
                                         ACT.Identity, bias=bias[:, r:r + 1], scale=SPL_SCALE).then_inc(spl.s_ready, 1)
                spl.round_act(act, k, u, first or second, 4)
                if more:
                    load_x(k + 2, u)
                spl.powers_act(act, k, first)

            load_x(0, 0)
            load_x(1, 1)
            basis(0, 0, 0, True)
            basis(0, 1, 1, False, True)
            with act.Fori(1, OT // 2 - 1) as tt:
                basis(tt, 2 * tt, 0)
                basis(tt, 2 * tt + 1, 1)
            basis(OT // 2 - 1, OT - 3, 0)
            basis(OT // 2 - 1, OT - 2, 1, more=False)
            basis(OT // 2, OT - 1, 0, more=False)

        @block.vector
        def _(dve):
            def tile(tt, k, u, first=False, more=True, early=False):
                v = 1 - u
                spl.take_dve(dve, k, u, 0, first)
                if more:
                    spl.center_dve(dve, k + 1, v)
                spl.take_dve(dve, k, u, 1, first)
                spl.take_dve(dve, k, u, 2, first)
                if more:
                    spl.cube_dve(dve, k + 1)
                spl.take_dve(dve, k, u, 3, first)
                if more:
                    spl.value_dve(dve, k + 1, v)
                if not first:
                    leave(tt - 1 if u == 0 else tt, k - 1, v, early)

            def leave(tt, k, u, early):
                dve.wait_ge(spl.f_used, 4 * k + 4)
                dve.wait_ge(h_in[u], 16 * tt + 16)
                if not early:
                    dve.wait_ge(y_out[u], 16 * tt)
                nc.vector.scalar_tensor_tensor(y[u][:], acc[:, u, 0:D], 1.0 / 6.0, h[u][:], ALU.mult,
                                               ALU.add).then_inc(y_ready, 1)

            spl.center_dve(dve, 0, 0)
            spl.cube_dve(dve, 0)
            spl.value_dve(dve, 0, 0)
            tile(0, 0, 0, True)
            tile(0, 1, 1, early=True)
            tile(1, 2, 0, early=True)
            with dve.Fori(1, OT // 2 - 1) as tt:
                tile(tt, 2 * tt + 1, 1)
                tile(tt + 1, 2 * tt + 2, 0)
            tile(OT // 2 - 1, OT - 2, 1)
            tile(OT // 2, OT - 1, 0, more=False)
            leave(OT // 2, OT - 1, 0, False)

        @block.tensor
        def _(pe):
            pe.wait_ge(w_in, 16)

            def layer(k, u, first=False):
                for i in range(4):
                    pe.wait_ge(spl.f_ready, 4 * k + i + 1)
                    if i == 0 and not first:
                        pe.wait_ge(y_ready, k - 1)
                    for r in range(SETS):
                        last = nc.tensor.matmul(acc[:, u, 0:D], spl.f[i][:, r * P:(r + 1) * P], w[:, i, r, :],
                                                start=(i == 0 and r == 0), stop=(i == 3 and r == SETS - 1))
                    last.then_inc(spl.f_used, 1)

            layer(0, 0, True)
            layer(1, 1, True)
            with pe.Fori(1, OT // 2) as tt:
                layer(2 * tt, 0)
                layer(2 * tt + 1, 1)
            layer(OT - 1, 0)


def program(nc, a, out):
    def scratch(name, *shape):
        return nc.dram_tensor(name, shape, F32, kind="Internal").ap()

    txt_scr = scratch("txt_scr", B * TXT, D)
    pos_scr = scratch("pos_scr", B, 2 * SAMPLES)
    pix_scr = scratch("pix_scr", B, PIXC, PIX)
    vis_scr = scratch("vis_scr", B * VIS, D)
    h_scr = scratch("h_scr", ALL, D)
    tokens(nc, a, txt_scr, pos_scr, pix_scr, vis_scr)
    attend_phase(nc, a, vis_scr, txt_scr, h_scr)
    hid_scr = scratch("hid_scr", P, HID // P, ALL)
    spline1_phase(nc, a, h_scr, hid_scr)
    spline2_phase(nc, a, h_scr, hid_scr, out.rearrange("b n d -> (b n) d"))


def tokens(nc, a, txt_scr, pos_scr, pix_scr, vis_scr):
    with ExitStack() as stack:
        hT_all = memories(nc, stack)[0]("stem_by_channel", [P, B * PIX])
        stem_phase(nc, a["patches"], a["stem_w"], a["stem_vec"], hT_all, pix_scr,
                   a["txt_idx"], a["table"], txt_scr)
        offset_phase(nc, a["off_w"], a["off_bias"], a["off_grid"], hT_all, pos_scr)
    with ExitStack() as stack:
        samp_all = memories(nc, stack)[0]("samples", [P, TAPS, B * VIS])
        sample_phase(nc, pos_scr, a["pix_neg"], pix_scr, samp_all)
        deform_phase(nc, a["dcn_w"], a["dcn_vec"], samp_all, vis_scr)


def layouts(i):
    import numpy as np

    f32 = np.float32

    def rep(*v):
        v = np.stack([np.asarray(x) for x in v])
        return np.broadcast_to(v[None], (P,) + v.shape)

    x = np.asarray(i["x"])
    tap = np.arange(TAPS)
    at = np.arange(HO) * K
    grid = np.zeros((TAPS, 2, HO, HO), f32)
    grid[:, 0] = at[None, :, None] + (tap // K)[:, None, None]
    grid[:, 1] = at[None, None, :] + (tap % K)[:, None, None]
    p = np.arange(PIXC)

    def chunks(w):
        r = np.zeros((P, 2) + w.shape[1:], w.dtype)
        r[:, 0], r[0:D1, 1] = w[0:D0], w[D0:D]
        return r

    def heads(w):
        r = np.zeros(w.shape[:-1] + (HG, 4, 32), w.dtype)
        r[..., 0:DH] = w.reshape(w.shape[:-1] + (HG, 4, DH))
        return r.reshape(w.shape[:-1] + (HG, P))

    w = {k: np.asarray(v) for k, v in i.items() if k.startswith("L0_attn")}
    dist = np.abs(np.arange(P)[:, None, None] + ROWS * np.arange(2)[:, None] - np.arange(TOK))
    w1 = np.asarray(i["L0_ffn_w1"]).reshape(HID, D, 4, 4).transpose(1, 2, 3, 0)
    w1t = np.empty((P, 4, 6, HID), f32)
    w1t[:, :, 0:4] = w1[0:D0]
    w1t[0:D1, :, 4:6], w1t[D1:P, :, 4:6] = w1[D0:D, :, 0:2], w1[D0:D, :, 2:4]
    w2t = np.asarray(i["L0_ffn_w2"]).reshape(D, HID // P, P, 4, 4).transpose(2, 3, 4, 1, 0).reshape(P, 4, 16, D)
    r1 = np.tile(np.array([0, 1, 2, 3, 0, 1], f32), (P, 1))
    r1[D1:P, 4:6] += 2
    return {
        "w1": w1t,
        "w2": w2t,
        "spline1_bias": (SPL_BIAS - r1 / 4).astype(f32),
        "spline2_bias": np.tile((SPL_BIAS - np.arange(4) / 4).astype(f32), (P, 1)),
        "wq": chunks(heads(w["L0_attn_Wq"])),
        "wk": chunks(heads(w["L0_attn_Wk"])),
        "wv": chunks(w["L0_attn_Wv"]),
        "wo": chunks(w["L0_attn_Wo"]),
        "bqk": np.concatenate([heads(w["L0_attn_bq"]), heads(w["L0_attn_bk"])]).T,
        "bv_bo": rep(w["L0_attn_bv"], w["L0_attn_bo"]),
        "identity": np.eye(P, dtype=f32),
        "mask": np.tile(np.where(dist <= 64, 0.0, NEG).astype(f32), (1, 1, 3)),
        "patches": x.reshape(B, 3, HS, K, HS, K).transpose(1, 3, 5, 0, 2, 4).reshape(PATCH, B, PIX),
        "stem_w": np.asarray(i["L0_tok_stem_w"]).reshape(C1, PATCH).T,
        "stem_vec": rep(i["L0_tok_stem_b"], i["L0_tok_bn1_g"], i["L0_tok_bn1_b"], i["L0_tok_bn1_m"], i["L0_tok_bn1_v"]),
        "txt_idx": np.asarray(i["x_txt"]).T,
        "table": np.asarray(i["L0_txt_weight"]),
        "off_w": np.asarray(i["L0_tok_off_w"]).reshape(2 * TAPS, C1, TAPS).transpose(1, 2, 0),
        "off_bias": np.asarray(i["L0_tok_off_b"])[:, None],
        "off_grid": np.tile(grid.reshape(2 * TAPS, VIS), (1, 8)),
        "pix_neg": -np.concatenate([(p // HS)[:, None] + 4 * np.arange(NPIXC)[None], (p % HS)[:, None]], 1).astype(f32),
        "dcn_w": np.asarray(i["L0_tok_dcn_w"]).reshape(D, C1, TAPS).transpose(1, 2, 0),
        "dcn_vec": rep(i["L0_tok_dcn_b"], i["L0_tok_bn2_g"], i["L0_tok_bn2_b"], i["L0_tok_bn2_m"], i["L0_tok_bn2_v"]),
    }


def kernel(**inputs):
    import numpy as np
    import concourse.bacc as bacc
    from concourse.bass_utils import run_bass_kernel_spmd

    nc = bacc.Bacc("TRN2", target_bir_lowering=False, num_devices=1)
    arrays = {k: np.ascontiguousarray(v) for k, v in layouts(inputs).items()}
    aps = {k: nc.dram_tensor(k, v.shape, mybir.dt.from_np(v.dtype), kind="ExternalInput").ap()
           for k, v in arrays.items()}
    out = nc.dram_tensor("out", (B, TOK, D), F32, kind="ExternalOutput").ap()
    program(nc, aps, out)
    return run_bass_kernel_spmd(nc, [arrays], core_ids=[0]).results[0]["out"]
```

```python
from contextlib import ExitStack

import concourse.bass as bass
from concourse import mybir

ALU = mybir.AluOpType
ACT = mybir.ActivationFunctionType
F32 = mybir.dt.float32
F32R = mybir.dt.float32r
BF16 = mybir.dt.bfloat16
I32 = mybir.dt.int32
AX_X = mybir.AxisListType.X

P = 128
B = 32
D = 192
D0, D1 = 128, 64
C1 = 96
K = 4
TAPS = K * K
HS = 24
PIX = HS * HS
HO = 6
VIS = HO * HO
TXT = 128
TOK = VIS + TXT
ROWS = TOK // 2
PAIRS = B // 2
PT = 2 * TOK
ALL = B * TOK
SAMPLES = TAPS * VIS
PATCH = 3 * TAPS
PIXC = 96
NPIXC = PIX // PIXC
HEADS, DH = 12, 16
HG = HEADS // 4
KPAD = 96
HID = 512
NCP = 16
EPS = 1e-5
SLOPE = 0.01
QMAX = 127.0
MAGIC = 12582912.0
NEG = -1.0e30
SPL_SCALE = 13.0 / 32.0
SPL_BIAS = (4.0 * 13.0 / 8.0 + 3.0) / 4.0 - 0.5
VT = B * VIS // P
OT = ALL // P


class Step:

    def __init__(self, engine, sem, base=0):
        self.engine, self.sem, self.base, self.n = engine, sem, base, 0

    def mark(self, ins):
        ins.then_inc(self.sem, 1)
        self.n += 1
        return self.n

    def after(self, n):
        self.engine.wait_ge(self.sem, self.base + n)

    def run(self, ins):
        self.after(self.mark(ins))


def memories(nc, stack):
    def sb(name, shape, dt=F32):
        return stack.enter_context(nc.sbuf_tensor(name, shape, dt))

    def ps(name, shape):
        return stack.enter_context(nc.psum_tensor(name, shape, F32))

    def sem(name):
        return stack.enter_context(nc.semaphore(name))

    return sb, ps, sem


def fold_norm(nc, dve, s, pow_done, rows, std, inv, half):
    bias, gamma, beta, mean, var = (rows[:, j, :] for j in range(5))
    s.run(nc.vector.tensor_scalar(std[:, :], var, EPS, None, ALU.add))
    dve.wait_ge(pow_done, 1)
    s.run(nc.vector.tensor_tensor(half[:, :], inv[:, :], inv[:, :], ALU.mult))
    s.run(nc.vector.tensor_tensor(half[:, :], half[:, :], std[:, :], ALU.mult))
    s.run(nc.vector.tensor_scalar(half[:, :], half[:, :], -0.5, 1.5, ALU.mult, ALU.add))
    s.run(nc.vector.tensor_tensor(inv[:, :], inv[:, :], half[:, :], ALU.mult))
    s.run(nc.vector.tensor_tensor(inv[:, :], inv[:, :], gamma, ALU.mult))
    s.run(nc.vector.tensor_tensor(std[:, :], bias, mean, ALU.subtract))
    s.run(nc.vector.tensor_tensor(std[:, :], std[:, :], inv[:, :], ALU.mult))
    s.run(nc.vector.tensor_tensor(std[:, :], std[:, :], beta, ALU.add))
    return std[:, :]


def stem_phase(nc, patches, stem_w, cvec, hT_all, pix_scr, txt_idx, table, txt_scr):
    with ExitStack() as stack:
        sb, ps, sem = memories(nc, stack)
        patch = [sb(f"patch{u}", [P, PIX]) for u in range(2)]
        w = sb("stem_weights", [P, C1])
        rows = sb("stem_vectors", [P, 5, C1])
        half = sb("stem_half", [P, C1])
        std = sb("stem_std", [P, C1])
        inv = sb("stem_inv", [P, C1])
        chan = ps("by_channel", [P, 2, 2, 512])
        pix = ps("by_pixel", [P, 2, 2, 512])
        by_pixel = [sb(f"stem_by_pixel{u}", [P, PIX]) for u in range(4)]
        idx = sb("text_index", [P, B], I32)
        emb = [sb(f"text_rows{u}", [P, D]) for u in range(4)]
        quant = [sb(f"text_quant{u}", [P, D]) for u in range(4)]
        q_amax = sb("text_amax", [P, 4])
        q_scale = sb("text_scale", [P, 4])
        q_rec = sb("text_rec", [P, 4])
        vectors_in = sem("vectors_in")
        zeroed = sem("stem_zeroed")
        ones_set = sem("stem_ones")
        bn = sem("stem_bn")
        bn_pow = sem("stem_pow")
        w_ready = sem("stem_w_ready")
        patch_in = [sem(f"patch_in{u}") for u in range(2)]
        stem_done = sem("stem_done")
        scaled = sem("stem_scaled")
        stem_read = sem("stem_read")
        pixel_out = [sem(f"stem_pixel_out{u}") for u in range(4)]
        idx_in = sem("text_index_in")
        emb_in = [sem(f"text_in{u}") for u in range(4)]
        q_step = sem("text_step")
        q_done = sem("text_done")
        txt_out = [sem(f"text_out{u}") for u in range(4)]
        block = stack.enter_context(nc.Block())

        @block.sync
        def _(sp):
            sp.dma_start(rows[:, :, :], cvec).then_inc(vectors_in, 16)
            sp.wait_ge(zeroed, 1)
            sp.dma_start(w[0:PATCH, :], stem_w).then_inc(vectors_in, 16)
            for u in range(2):
                sp.dma_start(patch[u][0:PATCH, :], patches[:, u, :]).then_inc(patch_in[u], 16)

            def results_out(t, u):
                sp.wait_ge(stem_read, 2 * (4 * t + u) + 2)
                sp.dma_start(pix_scr[bass.ds(4 * t + u, 1), :, :].rearrange("b p n -> p (b n)"),
                             by_pixel[u][0:PIXC, :]).then_inc(pixel_out[u], 16)
                sp.wait_ge(q_done, 4 * t + u + 1)
                sp.dma_start(txt_scr[bass.ds((4 * t + u) * TXT, TXT), :], quant[u][:, :]).then_inc(txt_out[u], 16)

            with sp.Fori(0, B // 4 - 1) as t:
                for u in range(4):
                    sp.wait_ge(stem_done, 4 * t + u + 1)
                    sp.dma_start(patch[u % 2][0:PATCH, :],
                                 patches[:, bass.ds(4 * t + u + 2, 1), :].rearrange("p b n -> p (b n)")
                                 ).then_inc(patch_in[u % 2], 16)
                    results_out(t, u)
            for u in range(4):
                t = B // 4 - 1
                if u < 2:
                    sp.wait_ge(stem_done, 4 * t + u + 1)
                    sp.dma_start(patch[u][0:PATCH, :], patches[:, 4 * t + u + 2, :]).then_inc(patch_in[u], 16)
                results_out(t, u)
            for u in range(4):
                sp.wait_ge(txt_out[u], 16 * (B // 4))
                sp.wait_ge(pixel_out[u], 16 * (B // 4))

        @block.gpsimd
        def _(pool):
            pool.memset(patch[0][:, :], 0.0)
            pool.memset(patch[1][:, :], 0.0)
            pool.memset(w[:, :], 0.0).then_inc(zeroed, 1)
            pool.memset(half[:, :], -0.5).then_inc(zeroed, 1)
            pool.dma_start(idx[:, :], txt_idx).then_inc(idx_in, 16)
            pool.wait_ge(zeroed, 2)
            pool.memset(patch[0][KPAD:KPAD + 1, :], 1.0).then_inc(ones_set, 1)
            pool.memset(patch[1][KPAD:KPAD + 1, :], 1.0).then_inc(ones_set, 1)
            pool.wait_ge(ones_set, 2)
            pool.wait_ge(bn, 1)
            pool.tensor_tensor(inv[:, :], std[:, :], half[:, :], ALU.pow).then_inc(bn_pow, 1)
            pool.wait_ge(idx_in, 16)
            for b in range(B):
                if b >= 4:
                    pool.wait_ge(q_done, b - 3)
                pool.indirect_dma_start(emb[b % 4][:, :], None, table,
                                        bass.IndirectOffsetOnAxis(idx[:, b:b + 1], 0)).then_inc(emb_in[b % 4], 16)

        @block.vector
        def _(dve):
            s = Step(dve, bn)
            dve.wait_ge(vectors_in, 32)
            shift = fold_norm(nc, dve, s, bn_pow, rows, std, inv, half)
            nc.vector.tensor_tensor(w[0:PATCH, :], w[0:PATCH, :], inv[0:PATCH, :], ALU.mult).then_inc(w_ready, 1)
            nc.vector.tensor_copy(w[KPAD:KPAD + 1, :], shift[KPAD:KPAD + 1, :]).then_inc(w_ready, 1)

            def image(t, u, first):
                for n, (src, dst) in enumerate(((chan, hT_all[0:C1, bass.ds((4 * t + u) * PIX, PIX)]),
                                                (pix, by_pixel[u][0:PIXC, :]))):
                    dve.wait_ge(scaled, 8 * t + 2 * u + n + 1)
                    y = dst.rearrange("p (h n) -> p h n", h=2)
                    nc.vector.tensor_tensor(y, src[0:C1, u % 2, :, 0:PIX // 2], y, ALU.max).then_inc(stem_read, 1)
                e, q = emb[u], quant[u]
                s = Step(dve, q_step, 7 * (4 * t + u))
                dve.wait_ge(emb_in[u], 16 * t + 16)
                s.run(nc.vector.tensor_reduce(q_amax[:, u:u + 1], e[:, :], AX_X, ALU.max, apply_absolute_value=True))
                s.run(nc.vector.tensor_scalar(q_scale[:, u:u + 1], q_amax[:, u:u + 1], 1e-8, 1.0 / QMAX,
                                              ALU.max, ALU.mult))
                s.run(nc.vector.reciprocal(q_rec[:, u:u + 1], q_scale[:, u:u + 1]))
                if not first:
                    dve.wait_ge(txt_out[u], 16 * t)
                s.run(nc.vector.tensor_scalar(q[:, :], e[:, :], q_rec[:, u:u + 1], MAGIC, ALU.mult, ALU.add))
                s.run(nc.vector.tensor_scalar(q[:, :], q[:, :], MAGIC, -QMAX, ALU.subtract, ALU.max))
                s.run(nc.vector.tensor_scalar(q[:, :], q[:, :], QMAX, q_scale[:, u:u + 1], ALU.min, ALU.mult))
                s.run(nc.vector.tensor_tensor(q[:, :], q[:, :], e[:, :], ALU.subtract))
                nc.vector.tensor_tensor(q[:, :], e[:, :], q[:, :], ALU.add).then_inc(q_done, 1)

            for u in range(4):
                image(0, u, True)
            with dve.Fori(1, B // 4) as t:
                for u in range(4):
                    image(t, u, False)

        @block.tensor
        def _(pe):
            pe.wait_ge(w_ready, 2)
            pe.wait_ge(ones_set, 2)

            def image(t, u, first):
                pe.wait_ge(patch_in[u], 16 * t + 16)
                if not first:
                    pe.wait_ge(stem_read, 4 * t + 2 * u - 2)
                x = patch[u]
                for h in range(2):
                    nc.tensor.matmul(chan[0:C1, u, h, 0:PIX // 2], w[0:KPAD + 1, :],
                                     x[0:KPAD + 1, h * PIX // 2:(h + 1) * PIX // 2], start=True, stop=True)
                for c in range(NPIXC):
                    last = nc.tensor.matmul(pix[0:PIXC, u, c // 3, (c % 3) * C1:(c % 3 + 1) * C1],
                                            x[0:KPAD + 1, c * PIXC:(c + 1) * PIXC], w[0:KPAD + 1, :],
                                            start=True, stop=True)
                last.then_inc(stem_done, 1)

            for u in range(2):
                image(0, u, True)
            with pe.Fori(1, B // 2) as t:
                for u in range(2):
                    image(t, u, False)

        @block.scalar
        def _(act):
            def image(t, u, first):
                act.wait_ge(stem_done, 4 * t + u + 1)
                if not first:
                    act.wait_ge(pixel_out[u], 16 * t)
                for src, dst in ((chan, hT_all[0:C1, bass.ds((4 * t + u) * PIX, PIX)]),
                                 (pix, by_pixel[u][0:PIXC, :])):
                    nc.scalar.activation(dst.rearrange("p (h n) -> p h n", h=2),
                                         src[0:C1, u % 2, :, 0:PIX // 2], ACT.Copy, scale=SLOPE).then_inc(scaled, 1)

            for u in range(4):
                image(0, u, True)
            with act.Fori(1, B // 4) as t:
                for u in range(4):
                    image(t, u, False)


def offset_phase(nc, off_w, off_vec, grid, hT_all, pos_scr):
    GI = 8
    NG = B // GI
    with ExitStack() as stack:
        sb, ps, sem = memories(nc, stack)
        w = sb("offset_weights", [P, TAPS, 2 * TAPS])
        bias = sb("offset_bias", [P, 1])
        base = sb("offset_grid", [P, GI * VIS])
        pos = sb("offset_pos", [P, NG, GI * VIS])
        acc = ps("offset_acc", [P, NG, 512])
        weights_in = sem("offset_weights_in")
        conv_done = sem("offset_conv_done")
        pos_ready = sem("offset_pos_ready")
        pos_out = sem("offset_pos_out")
        block = stack.enter_context(nc.Block())

        @block.sync
        def _(sp):
            sp.dma_start(w[0:C1, :, :], off_w).then_inc(weights_in, 16)
            sp.dma_start(bias[0:2 * TAPS, :], off_vec).then_inc(weights_in, 16)
            sp.dma_start(base[0:2 * TAPS, :], grid).then_inc(weights_in, 16)
            for g in range(NG):
                sp.wait_ge(pos_ready, g + 1)
                sp.dma_start(pos_scr[g * GI:(g + 1) * GI, :].rearrange("b (c n) -> c b n", n=VIS),
                             pos[0:2 * TAPS, g, :].rearrange("c (b n) -> c b n", n=VIS)).then_inc(pos_out, 16)
            sp.wait_ge(pos_out, 16 * NG)

        @block.tensor
        def _(pe):
            pe.wait_ge(weights_in, 48)
            taps = hT_all[0:C1, :].rearrange("p (b i r j s) -> p r s b i j", b=B, i=HO, r=K, j=HO, s=K)
            for g in range(NG):
                for kk in range(TAPS):
                    last = nc.tensor.matmul(acc[0:2 * TAPS, g, 0:GI * VIS], w[0:C1, kk, :],
                                            taps[:, kk // K, kk % K, g * GI:(g + 1) * GI],
                                            start=(kk == 0), stop=(kk == TAPS - 1))
                last.then_inc(conv_done, 1)

        @block.vector
        def _(dve):
            dve.wait_ge(weights_in, 48)
            for g in range(NG):
                dve.wait_ge(conv_done, g + 1)
                nc.vector.scalar_tensor_tensor(pos[0:2 * TAPS, g, :], acc[0:2 * TAPS, g, 0:GI * VIS],
                                               bias[0:2 * TAPS, 0:1], base[0:2 * TAPS, :],
                                               ALU.add, ALU.add).then_inc(pos_ready, 1)


def sample_phase(nc, pos_scr, pix_neg, pix_scr, samp_all):
    S2 = SAMPLES // 2
    with ExitStack() as stack:
        sb, ps, sem = memories(nc, stack)
        neg = sb("pixel_neg", [P, NPIXC + 1])
        pos = [sb(f"sample_pos{u}", [P, 2 * SAMPLES]) for u in range(2)]
        h = [sb(f"sample_h{u}", [P, PIX]) for u in range(2)]
        hx = [sb(f"hat_x{u}", [P, SAMPLES]) for u in range(2)]
        dy = [sb(f"dist_y{u}", [P, NPIXC, SAMPLES]) for u in range(2)]
        wt = sb("hat_weights", [P, 2, NPIXC, SAMPLES])
        acc = ps("sample_acc", [P, 2, 2, 512])
        const_in = sem("pixel_in")
        pos_in = [sem(f"sample_pos_in{u}") for u in range(2)]
        h_in = [sem(f"sample_h_in{u}") for u in range(2)]
        dist = sem("sample_dist")
        clipped = sem("sample_clipped")
        weights = sem("sample_weights")
        product = sem("sample_product")
        stored = sem("sample_stored")
        block = stack.enter_context(nc.Block())

        @block.sync
        def _(sp):
            sp.dma_start(neg[0:PIXC, :], pix_neg).then_inc(const_in, 16)

            def load(b, u):
                sp.dma_start(pos[u][0:PIXC, :], pos_scr[bass.ds(b, 1), :].rearrange("a n -> (a n)")
                             .partition_broadcast(PIXC)).then_inc(pos_in[u], 16)

            for u in range(2):
                load(u, u)
            with sp.Fori(1, B // 2) as t:
                for u in range(2):
                    sp.wait_ge(dist, 2 * t + u - 1)
                    load(2 * t + u, u)

        @block.gpsimd
        def _(pool):
            def load(b, u):
                pool.dma_start(h[u][0:PIXC, :], pix_scr[bass.ds(b, 1), :, :].rearrange("b p n -> p (b n)")
                               ).then_inc(h_in[u], 16)

            for u in range(2):
                load(u, u)
            with pool.Fori(1, B // 2) as t:
                for u in range(2):
                    pool.wait_ge(product, 2 * t + u - 1)
                    load(2 * t + u, u)

        @block.vector
        def _(dve):
            def weigh(t, u, first):
                s = Step(dve, clipped, 2 * (2 * t + u))
                dve.wait_ge(dist, 2 * t + u + 1)
                s.mark(nc.vector.tensor_scalar(hx[u][0:PIXC, :], hx[u][0:PIXC, :], 1.0, 1.0, ALU.min, ALU.subtract))
                s.run(nc.vector.tensor_scalar(dy[u][0:PIXC], dy[u][0:PIXC], 1.0, 1.0, ALU.min, ALU.subtract))
                if not first:
                    dve.wait_ge(product, 2 * t + u - 1)
                nc.vector.tensor_tensor(wt[0:PIXC, u], dy[u][0:PIXC],
                                        hx[u][0:PIXC, :].rearrange("p (a n) -> p a n", a=1)
                                        .to_broadcast([PIXC, NPIXC, SAMPLES]), ALU.mult).then_inc(weights, 1)

            for u in range(2):
                weigh(0, u, True)
            with dve.Fori(1, B // 2) as t:
                for u in range(2):
                    weigh(t, u, False)

        @block.scalar
        def _(act):
            act.wait_ge(const_in, 16)

            def distances(t, u, first):
                p = pos[u][0:PIXC, :].rearrange("p (k a n) -> p a k n", k=TAPS, a=2)
                act.wait_ge(pos_in[u], 16 * t + 16)
                if not first:
                    act.wait_ge(weights, 2 * t + u - 1)
                for c in range(NPIXC):
                    nc.scalar.activation(dy[u][0:PIXC, c, :].rearrange("p (k n) -> p k n", k=TAPS), p[:, 0],
                                         ACT.Abs, bias=neg[0:PIXC, c:c + 1])
                nc.scalar.activation(hx[u][0:PIXC, :].rearrange("p (k n) -> p k n", k=TAPS), p[:, 1],
                                     ACT.Abs, bias=neg[0:PIXC, NPIXC:NPIXC + 1]).then_inc(dist, 1)

            def store(t, u):
                act.wait_ge(product, 2 * t + u + 1)
                nc.scalar.activation(
                    samp_all[0:C1, :, bass.ds((2 * t + u) * VIS, VIS)],
                    acc[0:C1, u, :, 0:S2].rearrange("p h (k n) -> p h k n", n=VIS), ACT.Copy).then_inc(stored, 1)

            distances(0, 0, True)
            distances(0, 1, True)
            with act.Fori(1, B // 2) as t:
                for u in range(2):
                    distances(t, u, False)
                    store(t - 1, u)
            for u in range(2):
                store(B // 2 - 1, u)

        @block.tensor
        def _(pe):
            def image(t, u, first):
                pe.wait_ge(h_in[u], 16 * t + 16)
                pe.wait_ge(weights, 2 * t + u + 1)
                if not first:
                    pe.wait_ge(stored, 2 * t + u - 1)
                for half in range(2):
                    for c in range(NPIXC):
                        last = nc.tensor.matmul(acc[0:C1, u, half, 0:S2], h[u][0:PIXC, c * C1:(c + 1) * C1],
                                                wt[0:PIXC, u, c, half * S2:(half + 1) * S2],
                                                start=(c == 0), stop=(c == NPIXC - 1))
                last.then_inc(product, 1)

            for u in range(2):
                image(0, u, True)
            with pe.Fori(1, B // 2) as t:
                for u in range(2):
                    image(t, u, False)


def deform_phase(nc, dcn_w, vec, samp_all, vis_scr):
    with ExitStack() as stack:
        sb, ps, sem = memories(nc, stack)
        w = sb("deform_weights", [P, TAPS, D])
        rows = sb("deform_vectors", [P, 5, D])
        half = sb("deform_half", [P, D])
        std = sb("deform_std", [P, D])
        inv = sb("deform_inv", [P, D])
        tok = sb("deform_tokens", [P, VT, D])
        acc = ps("deform_acc", [P, 4, 512])
        vectors_in = sem("deform_in")
        half_set = sem("deform_half_set")
        bn = sem("deform_bn")
        bn_pow = sem("deform_pow")
        product = sem("deform_product")
        step = sem("deform_step")
        tok_ready = sem("deform_ready")
        tok_out = sem("deform_out")
        block = stack.enter_context(nc.Block())

        @block.sync
        def _(sp):
            sp.dma_start(rows[:, :, :], vec).then_inc(vectors_in, 16)
            sp.dma_start(w[0:C1, :, :], dcn_w).then_inc(vectors_in, 16)
            for t in range(VT):
                sp.wait_ge(tok_ready, t + 1)
                sp.dma_start(vis_scr[t * P:(t + 1) * P, :], tok[:, t, :]).then_inc(tok_out, 16)
            sp.wait_ge(tok_out, 16 * VT)

        @block.gpsimd
        def _(pool):
            pool.memset(half[:, :], -0.5).then_inc(half_set, 1)
            pool.wait_ge(half_set, 1)
            pool.wait_ge(bn, 1)
            pool.tensor_tensor(inv[:, :], std[:, :], half[:, :], ALU.pow).then_inc(bn_pow, 1)

        @block.tensor
        def _(pe):
            pe.wait_ge(vectors_in, 32)
            for t in range(VT):
                if t >= 4:
                    pe.wait_ge(step, 3 * (t - 4) + 1)
                for kk in range(TAPS):
                    last = nc.tensor.matmul(acc[:, t % 4, 0:D], samp_all[0:C1, kk, t * P:(t + 1) * P],
                                            w[0:C1, kk, :], start=(kk == 0), stop=(kk == TAPS - 1))
                last.then_inc(product, 1)

        @block.vector
        def _(dve):
            dve.wait_ge(vectors_in, 32)
            s = Step(dve, bn)
            shift = fold_norm(nc, dve, s, bn_pow, rows, std, inv, half)
            s = Step(dve, step)
            for t in range(VT):
                dve.wait_ge(product, t + 1)
                y = tok[:, t, :]
                s.run(nc.vector.tensor_tensor(y, acc[:, t % 4, 0:D], inv[:, :], ALU.mult))
                s.run(nc.vector.tensor_tensor(y, y, shift, ALU.add))
                s.run(nc.vector.scalar_tensor_tensor(y, y, SLOPE, y, ALU.mult, ALU.max))
                dve.sem_inc(tok_ready, 1)


def layer_stats(nc, dve, s, held, x, stats, mv, ve):
    for n in range(4):
        s.mark(nc.vector.bn_stats(stats[0:ROWS, n, :], x[0:ROWS, n, :]))
    s.after(4)
    dve.sem_inc(held, 1)
    for n in range(4):
        last = s.mark(nc.vector.bn_aggr(mv[0:ROWS, n, :], stats[0:ROWS, n, :]))
    s.after(last)
    s.mark(nc.vector.tensor_scalar(ve[0:ROWS, :], mv[0:ROWS, :, 1], EPS, None, ALU.add))


def layer_rest(nc, dve, s, pow_done, pow_count, x, xn, mv, ve, rstd, tmp):
    s.n = LN_VAR
    dve.wait_ge(pow_done, pow_count)
    s.run(nc.vector.tensor_tensor(tmp[0:ROWS, :], rstd[0:ROWS, :], rstd[0:ROWS, :], ALU.mult))
    s.run(nc.vector.tensor_tensor(tmp[0:ROWS, :], tmp[0:ROWS, :], ve[0:ROWS, :], ALU.mult))
    s.run(nc.vector.tensor_scalar(tmp[0:ROWS, :], tmp[0:ROWS, :], -0.5, 1.5, ALU.mult, ALU.add))
    s.run(nc.vector.tensor_tensor(rstd[0:ROWS, :], rstd[0:ROWS, :], tmp[0:ROWS, :], ALU.mult))
    for n in range(4):
        last = nc.vector.tensor_scalar(xn[0:ROWS, n, 0:D], x[0:ROWS, n, :], mv[0:ROWS, n, 0:1],
                                       rstd[0:ROWS, n:n + 1], ALU.subtract, ALU.mult)
        if n < 3:
            s.mark(last)
    return last


LN_VAR = 9
LN_STEPS = 16


def attend_phase(nc, a, vis_scr, txt_scr, h_scr):
    SCALE = DH ** -0.5
    SC = HG * TOK
    NX = 18
    with ExitStack() as stack:
        sb, ps, sem = memories(nc, stack)
        wq = sb("attend_wq", [P, 2, HG, P])
        wk = sb("attend_wk", [P, 2, HG, P])
        wv = sb("attend_wv", [P, 2, D])
        wo = sb("attend_wo", [P, HG, D])
        bo = sb("attend_bo", [P, 1, D])
        ident = sb("attend_identity", [P, P])
        identb = sb("attend_identity_bf16", [P, P], BF16)
        mask = sb("window_mask", [P, 2, SC])
        maskb = sb("window_mask_bf16", [P, 2, SC], BF16)
        pick = sb("attend_pick", [P, HG, ROWS])
        pickr = sb("attend_pick_r", [P, HG, ROWS], F32R)
        minus_low = sb("attend_minus_low", [P, 2])
        minus_half = sb("attend_half", [P, 4])
        ones = sb("attend_ones", [P, 32])
        x = [sb(f"attend_x{u}", [P, 4, D]) for u in range(2)]
        resid = [sb(f"attend_resid{u}", [P, 4, D]) for u in range(2)]
        xn = sb("attend_xn", [P, 4, D])
        stats, mv = sb("attend_stats", [P, 4, 6]), sb("attend_mv", [P, 4, 2])
        ve, rstd, tmp = (sb(f"attend_{k}", [P, 4]) for k in ("ve", "rstd", "tmp"))
        xT = sb("attend_xT", [P, 2, PT])
        qh = sb("attend_q_high", [P, HG, PT], F32R)
        q1, k1, k2 = ([sb(f"attend_{k}{u}", [P, HG, PT], F32R) for u in range(2)] for k in ("q1_", "k1_", "k2_"))
        va = [sb(f"attend_v{u}", [P, 4, HEADS, 32]) for u in range(2)]
        mx = sb("attend_max", [P, 2, 4, 32])
        mh = sb("attend_max_high", [P, TOK], F32R)
        mT = sb("attend_max_split", [P, TOK], F32R)
        prT = sb("attend_probs", [P, 2, HEADS, TOK])
        total = sb("attend_total", [P, SC])
        rec = sb("attend_rec", [P, SC])
        oT = sb("attend_oT", [P, HG, TOK])
        h2 = [sb(f"attend_h{u}", [P, 4, D]) for u in range(2)]
        sc = ps("scores_by_query", [P, 2, 512])
        tp = ps("scores_by_key", [P, 4, 512])
        xb = ps("attend_spare", [P, 2, 512])
        dve_held, pe_held = sem("attend_dve_held"), sem("attend_pe_held")
        const_in, consts, half_set = sem("attend_const_in"), sem("attend_consts"), sem("attend_half_set")
        zeros_set, ones_set = sem("attend_zeros"), sem("attend_ones")
        x_in = [sem(f"attend_x_in{u}") for u in range(2)]
        resid_ready = sem("attend_resid_ready")
        ln, pow_done, xn_ready = sem("attend_ln"), sem("attend_pow"), sem("attend_xn_ready")
        filled = [sem(f"spare_filled{i}") for i in range(2)]
        split = sem("attend_split")
        emptied = [sem(f"spare_emptied{i}") for i in range(2)]
        by_query, by_key = sem("attend_by_query"), sem("attend_by_key")
        maxed, doubled, exped = sem("attend_maxed"), sem("attend_doubled"), sem("attend_exped")
        inverted = sem("attend_inverted")
        h_ready = sem("attend_h_ready")
        h_out = [sem(f"attend_h_out{u}") for u in range(2)]
        block = stack.enter_context(nc.Block())
        loads = ((wq, a["wq"]), (wk, a["wk"]), (wv, a["wv"]), (wo, a["wo"]), (bo, a["bo"]), (ident, a["identity"]),
                 (mask, a["mask"]), (pick, a["pick"]), (minus_low, a["minus_low"]))
        CONSTS = 16 * len(loads)

        X, Q, K_, V = (0, 1), (3, 4, 5), (8, 9, 10), (13, 16)
        Y, SUM, MAX, MIX = (2, 12), (6, 14), (7, 15), (11, 17)
        START = dict(X=(0, 1), Q=(2, 3, 4), K=(5, 6, 7), V=(8, 9), MAX=10)
        SPLIT0, SPLITS = 2 * HG + 1, 2 * HG + 2
        SKIPPED = X + Q + K_ + V + (MAX[1],)

        def use(t, k):
            n = len(START["X"] + START["Q"] + START["K"] + START["V"]) // 2 + NX // 2 * t + k // 2
            if isinstance(t, int):
                n += t == 0 and k == 0
                past = SKIPPED + X[:1] if t == PAIRS else [j for j in SKIPPED if j < k] if t == PAIRS - 1 else []
                n -= sum(j % 2 == k % 2 for j in past)
            return k % 2, n

        def start(k):
            return k % 2, k // 2

        @block.sync
        def _(sp):
            for dst, src in loads:
                sp.dma_start(dst[:], src).then_inc(const_in, 16)

            vis = vis_scr.rearrange("(b v) d -> v b d", v=VIS)
            txt = txt_scr.rearrange("(b v) d -> v b d", v=TXT)
            rest = ROWS - VIS

            def load(t, u):
                b = bass.ds(2 * t, 2)
                even, odd = x[u][:, 0:4:2, :], x[u][:, 1:4:2, :]
                sp.dma_start(even[0:VIS], vis[:, b, :]).then_inc(x_in[u], 16)
                sp.dma_start(even[VIS:ROWS], txt[0:rest, b, :]).then_inc(x_in[u], 16)
                sp.dma_start(odd[0:ROWS], txt[rest:TXT, b, :]).then_inc(x_in[u], 16)

            def leave(t, u):
                sp.wait_ge(h_ready, 2 * t + 2)
                sp.dma_start(h_scr[bass.ds(t * PT, PT), :].rearrange("(n p) d -> p n d", p=ROWS),
                             h2[u][0:ROWS]).then_inc(h_out[u], 16)

            load(0, 0)
            load(1, 1)
            with sp.Fori(0, PAIRS // 2 - 1) as tt:
                for u in range(2):
                    sp.wait_ge(resid_ready, 2 * tt + u + 1)
                    sp.wait_ge(xn_ready, 2 * tt + u + 1)
                    load(2 * tt + u + 2, u)
                    leave(2 * tt + u, u)
            for u in range(2):
                leave(PAIRS - 2 + u, u)
            for u in range(2):
                sp.wait_ge(h_out[u], 16 * (PAIRS // 2))

        @block.gpsimd
        def _(pool):
            pool.memset(minus_half[:, :], -0.5).then_inc(half_set, 1)
            pool.memset(mx[:], 0.0).then_inc(zeros_set, 1)
            pool.memset(ones[:], 1.0).then_inc(ones_set, 1)
            for u in range(2):
                pool.memset(va[u][:], 0.0).then_inc(zeros_set, 1)
            pool.wait_ge(half_set, 1)
            pool.wait_ge(zeros_set, 3)
            pool.wait_ge(ones_set, 1)
            pool.memset(xT[D1:D1 + 1, 1, :], 1.0).then_inc(ones_set, 1)
            pool.wait_ge(ones_set, 2)
            pool.wait_ge(const_in, CONSTS)

            def pair(tt, u):
                t = 2 * tt + u
                pool.wait_ge(ln, LN_STEPS * t + LN_VAR)
                pool.tensor_tensor(rstd[0:ROWS, :], ve[0:ROWS, :], minus_half[0:ROWS, :], ALU.pow).then_inc(pow_done, 1)
                if not (isinstance(tt, int) and tt == 0):
                    pool.wait_ge(h_ready, 2 * t - 2)
                pool.tensor_tensor(resid[u][0:ROWS], x[u][0:ROWS],
                                   bo[0:ROWS, :, :].to_broadcast([ROWS, 4, D]), ALU.add).then_inc(resid_ready, 1)

            pair(0, 0)
            pair(0, 1)
            with pool.Fori(1, PAIRS // 2) as tt:
                for u in range(2):
                    pair(tt, u)

        @block.vector
        def _(dve):
            dve.wait_ge(const_in, CONSTS)
            nc.vector.tensor_copy(identb[:], ident[:]).then_inc(consts, 1)
            nc.vector.tensor_copy(maskb[:], mask[:]).then_inc(consts, 1)
            nc.vector.tensor_copy(pickr[:], pick[:]).then_inc(consts, 1)
            dve.wait_ge(zeros_set, 3)

            def norm_in(tt, u):
                dve.wait_ge(x_in[u], 48 * tt + 48)
                layer_stats(nc, dve, Step(dve, ln, LN_STEPS * (2 * tt + u)), dve_held, x[u], stats, mv, ve)

            def norm_out(tt, u, turned):
                t = 2 * tt + u
                if turned is not None:
                    bank, c = turned
                    dve.wait_ge(filled[bank], c + 1)
                layer_rest(nc, dve, Step(dve, ln, LN_STEPS * t), pow_done, t + 1, x[u], xn, mv, ve, rstd,
                           tmp).then_inc(xn_ready, 1)

            def maximum(a, q):
                n, h = divmod(q, 2)
                dve.wait_ge(by_query, 4 * a + q + 1)
                nc.vector.tensor_reduce(mx[0:ROWS, n, 2 * h:2 * h + 2, 0:HG],
                                        sc[0:ROWS, :, 0:SC].rearrange("p j (g n) -> p j g n", n=TOK),
                                        AX_X, ALU.max).then_inc(maxed, 1)

            def double(a):
                dve.wait_ge(maxed, 4 * a + 4)
                nc.vector.tensor_copy(mx[0:ROWS, :, :, HG:2 * HG], mx[0:ROWS, :, :, 0:HG]).then_inc(doubled, 1)

            def low(at, count, dst, high, factor):
                bank, c = at
                cols = dst.shape[-1]
                dve.wait_ge(split, count)
                nc.vector.scalar_tensor_tensor(dst, high.bitcast(F32), factor, xb[:, bank, 0:cols], ALU.mult,
                                               ALU.add).then_inc(emptied[bank], 1)

            def low_q(u, g, at, count):
                low(at, count, q1[u][:, g, :], qh[:, g, :], minus_low[:, 0:1])

            def low_k(u, g, at, count):
                low(at, count, k2[u][:, g, :], k1[u][:, g, :], -1.0)

            def low_max(at, count):
                low(at, count, mT[:], mh[:], minus_low[:, 1:2])

            def values(u, i, at):
                bank, c = at
                dve.wait_ge(filled[bank], c + 1)
                nc.vector.tensor_copy(va[u][0:ROWS, 2 * i:2 * i + 2, :, 0:DH],
                                      xb[0:ROWS, bank, 0:2 * D].rearrange("p (n h d) -> p n h d", n=2, d=DH)
                                      ).then_inc(emptied[bank], 1)

            def invert(g, at):
                bank, c = at
                dve.wait_ge(emptied[bank], c + 1)
                cols = slice(g * TOK, (g + 1) * TOK)
                nc.vector.reciprocal(rec[:, cols], total[:, cols]).then_inc(inverted, 1)

            def weigh(a, at):
                bank, c = at
                dve.wait_ge(filled[bank], c + 1)
                dve.wait_ge(inverted, HG * a + HG)
                nc.vector.tensor_tensor(oT[:], xb[:, bank, 0:SC].rearrange("p (g n) -> p g n", n=TOK),
                                        rec[:].rearrange("p (g n) -> p g n", n=TOK), ALU.mult).then_inc(emptied[bank], 1)

            def residual(u, i, at):
                bank, c = at
                dve.wait_ge(filled[bank], c + 1)
                nc.vector.tensor_tensor(h2[u][0:ROWS, 2 * i:2 * i + 2, :],
                                        xb[0:ROWS, bank, 0:2 * D].rearrange("p (n d) -> p n d", n=2),
                                        resid[u][0:ROWS, 2 * i:2 * i + 2, :], ALU.add).then_inc(emptied[bank], 1)
                dve.wait_ge(emptied[bank], c + 1)
                dve.sem_inc(h_ready, 1)

            def pair(tt, u, first=False, more=True, more2=True):
                t = 2 * tt + u
                v = 1 - u
                splits = SPLIT0 + SPLITS * t
                for i in range(2):
                    nxt = 2 * t + i + 1
                    for q in range(4):
                        if i == 0 or more:
                            maximum(nxt, q)
                        if i == 1 and more2 and q == 0:
                            norm_in(tt + 1, u)
                        if q == 1:
                            if i == 1:
                                if not (isinstance(tt, int) and tt == 0):
                                    dve.wait_ge(h_out[u], 16 * tt)
                                dve.wait_ge(resid_ready, t + 1)
                                residual(u, 0, use(t, Y[1]))
                                if more2:
                                    norm_out(tt + 1, u, use(t, X[1]))
                            elif not first:
                                residual(v, 1, use(t, Y[0]))
                        if q == 2 and more:
                            if i == 0:
                                low_q(v, 0, use(t, Q[0]), splits + 1)
                                low_q(v, 1, use(t, Q[1]), splits + 2)
                            else:
                                values(v, 0, use(t, V[0]))
                    if i == 0 or more:
                        double(nxt)
                    if i == 0 and more:
                        low_q(v, 2, use(t, Q[2]), splits + 3)
                    if i == 0 or more:
                        low_max(use(t, MAX[i]), splits + (8 if i == 1 else 4 if more else 1))
                    if i == 1 and more:
                        values(v, 1, use(t, V[1]))
                    for g in range(HG):
                        invert(g, use(t, SUM[i]))
                        if i == 0 and more:
                            low_k(v, g, use(t, K_[g]), splits + 5 + g)
                    weigh(2 * t + i, use(t, MIX[i]))

            norm_in(0, 0)
            norm_out(0, 0, None)
            for g in range(HG):
                low_q(0, g, start(START["Q"][g]), g + 1)
            for g in range(HG):
                low_k(0, g, start(START["K"][g]), HG + g + 1)
            for i in range(2):
                values(0, i, start(START["V"][i]))
            for q in range(4):
                maximum(0, q)
            double(0)
            low_max(start(START["MAX"]), SPLIT0)
            norm_in(0, 1)
            norm_out(0, 1, start(START["X"][1]))
            pair(0, 0, first=True)
            pair(0, 1)
            with dve.Fori(1, PAIRS // 2 - 1) as tt:
                for u in range(2):
                    pair(tt, u)
            pair(PAIRS // 2 - 1, 0, more2=False)
            pair(PAIRS // 2 - 1, 1, more=False, more2=False)
            residual(1, 1, use(PAIRS, Y[0]))

        @block.scalar
        def _(act):
            act.wait_ge(const_in, CONSTS)

            def turned(i, at):
                bank, c = at
                rows = (D0, D1)[i]
                act.wait_ge(filled[bank], c + 1)
                nc.scalar.activation(xT[0:rows, i, :], xb[0:rows, bank, 0:PT], ACT.Copy).then_inc(emptied[bank], 1)

            def high(dst, at):
                bank, c = at
                act.wait_ge(filled[bank], c + 1)
                nc.scalar.activation(dst, xb[:, bank, 0:dst.shape[-1]], ACT.Copy).then_inc(split, 1)

            def sums(at):
                bank, c = at
                act.wait_ge(filled[bank], c + 1)
                nc.scalar.activation(total[:], xb[:, bank, 0:SC], ACT.Copy).then_inc(emptied[bank], 1)

            def expo(a, q):
                c, h = divmod(q, 2)
                act.wait_ge(by_key, 4 * a + q + 1)
                nc.scalar.activation(prT[0:ROWS, c, 6 * h:6 * h + 6, :].rearrange("p (j g) n -> p j (g n)", j=2),
                                     tp[0:ROWS, 2 * h:2 * h + 2, 0:SC], ACT.Exp, scale=SCALE).then_inc(exped, 1)

            def pair(tt, u, more=True):
                t = 2 * tt + u
                v = 1 - u
                for i in range(2):
                    for q in range(4):
                        expo(2 * t + i, q)
                        if i == 0 and more:
                            if q == 0:
                                for j in range(2):
                                    turned(j, use(t, X[j]))
                            if q == 2:
                                for g in range(2):
                                    high(qh[:, g, :], use(t, Q[g]))
                    if i == 0 and more:
                        high(qh[:, 2, :], use(t, Q[2]))
                    sums(use(t, SUM[i]))
                    if i == 0 or more:
                        high(mh[:], use(t, MAX[i]))
                    if i == 0 and more:
                        for g in range(HG):
                            high(k1[v][:, g, :], use(t, K_[g]))

            for i in range(2):
                turned(i, start(START["X"][i]))
            for g in range(HG):
                high(qh[:, g, :], start(START["Q"][g]))
            for g in range(HG):
                high(k1[0][:, g, :], start(START["K"][g]))
            high(mh[:], start(START["MAX"]))
            for u in range(2):
                pair(0, u)
            with act.Fori(1, PAIRS // 2 - 1) as tt:
                for u in range(2):
                    pair(tt, u)
            pair(PAIRS // 2 - 1, 0)
            pair(PAIRS // 2 - 1, 1, more=False)

        @block.tensor
        def _(pe):
            pe.wait_ge(const_in, CONSTS)
            pe.wait_ge(consts, 3)
            pe.wait_ge(ones_set, 2)

            def claim(at):
                bank, c = at
                if not (isinstance(c, int) and c == 0):
                    pe.wait_ge(emptied[bank], c)
                return bank

            def read(*at):
                for bank, c in at:
                    pe.wait_ge(emptied[bank], c + 1)

            def turn_x(t, i, at):
                d, rows = ((0, D0), (D0, D1))[i]
                if i == 0:
                    pe.wait_ge(xn_ready, t + 1)
                bank = claim(at)
                pe.sem_inc(pe_held, 1)
                for n in range(4):
                    last = nc.tensor.transpose(xb[0:rows, bank, n * ROWS:(n + 1) * ROWS],
                                               xn[0:ROWS, n, d:d + rows], ident[0:ROWS, 0:ROWS])
                last.then_inc(filled[bank], 1)

            def project(w, g, at):
                bank = claim(at)
                nc.tensor.matmul(xb[:, bank, 0:PT], w[0:D0, 0, g, :], xT[0:D0, 0, :], start=True, stop=False)
                nc.tensor.matmul(xb[:, bank, 0:PT], w[0:D1 + 1, 1, g, :], xT[0:D1 + 1, 1, :],
                                 start=False, stop=True).then_inc(filled[bank], 1)

            def values(i, at):
                bank = claim(at)
                for n in range(2):
                    cols = slice((2 * i + n) * ROWS, (2 * i + n + 1) * ROWS)
                    y = xb[0:ROWS, bank, n * D:(n + 1) * D]
                    nc.tensor.matmul(y, xT[0:D0, 0, cols], wv[0:D0, 0, :], start=True, stop=False)
                    last = nc.tensor.matmul(y, xT[0:D1 + 1, 1, cols], wv[0:D1 + 1, 1, :], start=False, stop=True)
                last.then_inc(filled[bank], 1)

            def queries_scores(a, u, i, q, first=False):
                n, h = divmod(q, 2)
                if not (first and q == 0):
                    pe.wait_ge(maxed, 4 * a + q)
                for j in range(2):
                    nc.tensor.matmul(sc[0:ROWS, j, 0:SC], identb[0:ROWS, 0:ROWS], maskb[0:ROWS, n, :],
                                     start=True, stop=False)
                for g in range(HG):
                    for k in (k1[u], k2[u]):
                        for j in range(2):
                            r = slice(64 * h + 32 * j, 64 * h + 32 * j + 32)
                            last = nc.tensor.matmul(sc[0:ROWS, j, g * TOK:(g + 1) * TOK],
                                                    q1[u][r, g, i * TOK + n * ROWS:i * TOK + (n + 1) * ROWS],
                                                    k[r, g, i * TOK:(i + 1) * TOK],
                                                    start=False, stop=(g == HG - 1 and k is k2[u]))
                last.then_inc(by_query, 1)

            def keys_scores(a, u, i, q, first=False):
                c, h = divmod(q, 2)
                if not (first and q < 2):
                    pe.wait_ge(exped, 4 * a + q - 1)
                for j in range(2):
                    nc.tensor.matmul(tp[0:ROWS, 2 * h + j, 0:SC], identb[0:ROWS, 0:ROWS], maskb[0:ROWS, c, :],
                                     start=True, stop=False)
                for g in range(HG):
                    for k in (k1[u], k2[u], None):
                        for j in range(2):
                            r = slice(64 * h + 32 * j, 64 * h + 32 * j + 32)
                            left = (pickr[r, g, :] if k is None else
                                    k[r, g, i * TOK + c * ROWS:i * TOK + (c + 1) * ROWS])
                            right = mT[r, :] if k is None else q1[u][r, g, i * TOK:(i + 1) * TOK]
                            last = nc.tensor.matmul(tp[0:ROWS, 2 * h + j, g * TOK:(g + 1) * TOK], left, right,
                                                    start=False, stop=(g == HG - 1 and k is None))
                last.then_inc(by_key, 1)

            def turn_max(a, at):
                bank = claim(at)
                pe.wait_ge(doubled, a + 1)
                for n in range(2):
                    last = nc.tensor.transpose(xb[:, bank, n * ROWS:(n + 1) * ROWS],
                                               mx[0:ROWS, n, :, :].rearrange("p j g -> p (j g)"),
                                               ident[0:ROWS, 0:ROWS])
                last.then_inc(filled[bank], 1)

            def mix(u, i, at, sums):
                bank = claim(at)
                for g in range(HG):
                    for c in range(2):
                        for j in range(4):
                            left = ones[0:ROWS, :] if sums else va[u][0:ROWS, 2 * i + c, 4 * g + j, :]
                            last = nc.tensor.matmul(xb[32 * j:32 * j + 32, bank, g * TOK:(g + 1) * TOK], left,
                                                    prT[0:ROWS, c, HG * j + g, :], start=(c == 0), stop=(c == 1))
                last.then_inc(filled[bank], 1)

            def project_out(at, mixed):
                bank = claim(at)
                read(mixed)
                for n in range(2):
                    for g in range(HG):
                        last = nc.tensor.matmul(xb[0:ROWS, bank, n * D:(n + 1) * D], oT[:, g, n * ROWS:(n + 1) * ROWS],
                                                wo[:, g, :], start=(g == 0), stop=(g == HG - 1))
                last.then_inc(filled[bank], 1)

            def pair(tt, u, first=False, more=True):
                t = 2 * tt + u
                v = 1 - u
                for i in range(2):
                    a = 2 * t + i
                    w = u if i == 0 else v
                    nxt = i == 0 or more
                    for q in range(4):
                        if q == 0:
                            read(use(t, MAX[0]) if i == 1 else start(START["MAX"]) if first else use(t - 1, MAX[1]))
                            if i == 1 and more:
                                read(use(t, K_[1]), use(t, K_[2]))
                        keys_scores(a, u, i, q, first and i == 0)
                        if nxt:
                            queries_scores(a + 1, w, 1 - i, q)
                        if i == 0 and more and q == 0:
                            for j in range(2):
                                turn_x(t + 1, j, use(t, X[j]))
                        if q == 1:
                            if i == 1:
                                project_out(use(t, Y[1]), use(t, MIX[0]))
                            elif not first:
                                project_out(use(t, Y[0]), use(t - 1, MIX[1]))
                        if q == 2 and more:
                            if i == 0:
                                read(use(t, X[0]), use(t, X[1]))
                                for g in range(2):
                                    project(wq, g, use(t, Q[g]))
                            else:
                                values(0, use(t, V[0]))
                    if i == 0 and more:
                        project(wq, 2, use(t, Q[2]))
                    pe.wait_ge(exped, 4 * a + 4)
                    mix(u, i, use(t, SUM[i]), True)
                    if nxt:
                        turn_max(a + 1, use(t, MAX[i]))
                    if more:
                        if i == 0:
                            for g in range(HG):
                                project(wk, g, use(t, K_[g]))
                        else:
                            values(1, use(t, V[1]))
                    if i == 0:
                        read(*(start(START["V"][j]) if first else use(t - 1, V[j]) for j in range(2)))
                    mix(u, i, use(t, MIX[i]), False)

            for j in range(2):
                turn_x(0, j, start(START["X"][j]))
            read(*(start(START["X"][j]) for j in range(2)))
            for g in range(HG):
                project(wq, g, start(START["Q"][g]))
            for g in range(HG):
                project(wk, g, start(START["K"][g]))
            for i in range(2):
                values(i, start(START["V"][i]))
            read(start(START["K"][1]), start(START["K"][2]))
            for q in range(4):
                queries_scores(0, 0, 0, q, True)
            turn_max(0, start(START["MAX"]))
            pair(0, 0, first=True)
            pair(0, 1)
            with pe.Fori(1, PAIRS // 2 - 1) as tt:
                for u in range(2):
                    pair(tt, u)
            pair(PAIRS // 2 - 1, 0)
            pair(PAIRS // 2 - 1, 1, more=False)
            project_out(use(PAIRS, Y[0]), use(PAIRS - 1, MIX[1]))


class Spline:

    def __init__(self, nc, sb, sem, name, cols):
        self.nc, self.cols = nc, cols
        self.s, self.t, self.a, self.a2, self.b, self.b2 = (
            sb(f"{name}_{k}", [P, cols]) for k in ("s", "t", "a", "a2", "b", "b2"))
        self.n = [sb(f"{name}_n{u}", [P, cols]) for u in range(2)]
        self.v = [sb(f"{name}_v{u}", [P, cols]) for u in range(2)]
        self.f = [sb(f"{name}_f{i}", [P, cols]) for i in range(4)]
        (self.s_ready, self.n_ready, self.z_ready, self.t_ready, self.a_ready, self.a2_ready, self.b_ready,
         self.b2_ready, self.a3_ready, self.b3_ready, self.v_ready, self.f_ready, self.f_used) = (
            sem(f"{name}_{k}") for k in ("s_ready", "n_ready", "z_ready", "t_ready", "a_ready", "a2_ready", "b_ready",
                                         "b2_ready", "a3_ready", "b3_ready", "v_ready", "f_ready", "f_used"))

        self.held = sem(f"{name}_pool_held")

    def round_act(self, act, k, u, first, parts):
        act.wait_ge(self.s_ready, parts * (k + 1))
        if not first:
            act.wait_ge(self.f_ready, 4 * (k - 1))
        self.nc.scalar.activation(self.n[u][:], self.s[:], ACT.Copy, bias=MAGIC).then_inc(self.n_ready, 1)

    def powers_act(self, act, k, first):
        act.wait_ge(self.z_ready, k + 1)
        if not first:
            act.wait_ge(self.a_ready, k)
        self.nc.scalar.activation(self.t[:], self.s[:], ACT.Abs, scale=4.0).then_inc(self.t_ready, 1)
        act.wait_ge(self.t_ready, k + 1)
        if not first:
            act.wait_ge(self.v_ready, k)
        self.nc.scalar.activation(self.b[:], self.t[:], ACT.Relu, bias=1.0, scale=-1.0).then_inc(self.b_ready, 1)
        self.nc.scalar.activation(self.a2[:], self.t[:], ACT.Square, bias=2.0, scale=-1.0).then_inc(self.a2_ready, 1)
        act.wait_ge(self.b_ready, k + 1)
        self.nc.scalar.activation(self.b2[:], self.b[:], ACT.Square, scale=2.0).then_inc(self.b2_ready, 1)

    def cube_pool(self, pool, k, first):
        if not first:
            pool.wait_ge(self.a3_ready, k)
        pool.wait_ge(self.t_ready, k + 1)
        pool.sem_inc(self.held, 1)
        pool.tensor_scalar(self.a[:], self.t[:], -1.0, 2.0, ALU.mult, ALU.add).then_inc(self.a_ready, 1)
        pool.wait_ge(self.b2_ready, k + 1)
        pool.tensor_tensor(self.b2[:], self.b2[:], self.b[:], ALU.mult).then_inc(self.b3_ready, 1)

    def center_dve(self, dve, k, u):
        dve.wait_ge(self.n_ready, k + 1)
        self.nc.vector.scalar_tensor_tensor(self.s[:], self.n[u][:], MAGIC, self.s[:], ALU.subtract,
                                            ALU.subtract).then_inc(self.z_ready, 1)

    def cube_dve(self, dve, k):
        dve.wait_ge(self.a_ready, k + 1)
        dve.wait_ge(self.a2_ready, k + 1)
        self.nc.vector.tensor_tensor(self.a2[:], self.a2[:], self.a[:], ALU.mult).then_inc(self.a3_ready, 1)

    def value_dve(self, dve, k, u):
        dve.wait_ge(self.b3_ready, k + 1)
        dve.wait_ge(self.a3_ready, k + 1)
        self.nc.vector.tensor_tensor(self.v[u][:], self.a2[:], self.b2[:], ALU.subtract).then_inc(self.v_ready, 1)

    def take_dve(self, dve, k, u, i, first):
        if i == 0:
            dve.wait_ge(self.v_ready, k + 1)
        if not first:
            dve.wait_ge(self.f_used, 4 * k + i - 3)
        self.nc.vector.scalar_tensor_tensor(self.f[i][:], self.n[u][:], MAGIC + i, self.v[u][:], ALU.is_equal,
                                            ALU.mult).then_inc(self.f_ready, 1)


def spline1_phase(nc, a, h_scr, hid_scr):
    SETS = 6
    W2X = 2 * D0
    MC = HID // P
    with ExitStack() as stack:
        sb, ps, sem = memories(nc, stack)
        spl = Spline(nc, sb, sem, "spline1", SETS * PT)
        w = sb("spline1_weights", [P, 4, SETS, HID])
        bias = sb("spline1_offset", [P, SETS])
        ident = sb("spline1_identity", [P, P])
        minus_half = sb("spline1_half", [P, 4])
        x = [sb(f"spline1_x{u}", [P, 4, D]) for u in range(2)]
        xn = sb("spline1_xn", [P, 4, W2X])
        stats, mv = sb("spline1_stats", [P, 4, 6]), sb("spline1_mv", [P, 4, 2])
        ve, rstd, tmp = (sb(f"spline1_{k}", [P, 4]) for k in ("ve", "rstd", "tmp"))
        hid = [sb(f"spline1_hid{u}", [P, PT]) for u in range(2)]
        acc = ps("spline1_acc", [P, MC, 512])
        xT = ps("spline1_xT", [P, 2, 512])
        dve_held = sem("spline1_dve_held")
        const_in, w_in, half_set = sem("spline1_const_in"), sem("spline1_w_in"), sem("spline1_half_set")
        x_in = [sem(f"spline1_x_in{u}") for u in range(2)]
        ln, pow_done, xn_ready, twice = (sem(f"spline1_{k}") for k in ("ln", "pow", "xn_ready", "twice"))
        xT_ready = sem("spline1_xT_ready")
        summed = sem("spline1_summed")
        emptied = sem("spline1_emptied")
        hid_out = [sem(f"spline1_hid_out{u}") for u in range(2)]
        block = stack.enter_context(nc.Block())

        @block.sync
        def _(sp):
            sp.dma_start(ident[:], a["identity"]).then_inc(const_in, 16)
            sp.dma_start(bias[:], a["spline1_bias"]).then_inc(const_in, 16)

            def load(t, u):
                sp.dma_start(x[u][0:ROWS], h_scr[bass.ds(t * PT, PT), :].rearrange("(n p) d -> p n d", p=ROWS)
                             ).then_inc(x_in[u], 16)

            def leave(t):
                for m in range(MC):
                    sp.wait_ge(emptied, MC * t + m + 1)
                    sp.dma_start(hid_scr[:, m, bass.ds(t * PT, PT)], hid[m % 2][:]).then_inc(hid_out[m % 2], 16)

            def reload(t, u):
                sp.wait_ge(xn_ready, t - 1)
                load(t, u)

            load(0, 0)
            load(1, 1)
            for i in range(4):
                if i > 0:
                    sp.wait_ge(w_in, 16 * i)
                sp.dma_start(w[:, i], a["w1"][:, i]).then_inc(w_in, 16)
            reload(2, 0)
            with sp.Fori(0, PAIRS // 2 - 2) as tt:
                for u in range(2):
                    reload(2 * tt + u + 3, 1 - u)
                    leave(2 * tt + u)
            reload(PAIRS - 1, 1)
            for t in range(PAIRS - 4, PAIRS):
                leave(t)
            for u in range(2):
                sp.wait_ge(hid_out[u], 16 * (MC // 2) * PAIRS)

        @block.gpsimd
        def _(pool):
            pool.memset(minus_half[:, :], -0.5).then_inc(half_set, 1)
            pool.wait_ge(half_set, 1)

            def power(t):
                pool.wait_ge(ln, LN_STEPS * t + LN_VAR)
                pool.tensor_tensor(rstd[0:ROWS, :], ve[0:ROWS, :], minus_half[0:ROWS, :], ALU.pow).then_inc(pow_done, 1)

            def double(t):
                pool.wait_ge(xn_ready, t + 1)
                pool.sem_inc(spl.held, 1)
                pool.tensor_copy(xn[0:ROWS, :, D:W2X], xn[0:ROWS, :, D0:D]).then_inc(twice, 1)

            power(0)
            double(0)
            power(1)
            spl.cube_pool(pool, 0, True)
            double(1)
            with pool.Fori(1, PAIRS - 1) as t:
                power(t + 1)
                spl.cube_pool(pool, t, False)
                double(t + 1)
            spl.cube_pool(pool, PAIRS - 1, False)

        @block.vector
        def _(dve):
            dve.wait_ge(const_in, 32)

            def norm(t, tt, u, first=False):
                dve.wait_ge(x_in[u], 16 * tt + 16)
                if not first:
                    dve.wait_ge(xT_ready, t)
                s = Step(dve, ln, LN_STEPS * t)
                layer_stats(nc, dve, s, dve_held, x[u], stats, mv, ve)
                layer_rest(nc, dve, s, pow_done, t + 1, x[u], xn, mv, ve, rstd, tmp).then_inc(xn_ready, 1)

            def tile(tt, u, first, more, more2):
                k, v = 2 * tt + u, (u + 1) % 2
                for i in range(4):
                    spl.take_dve(dve, k, u, i, first)
                if more:
                    spl.center_dve(dve, k + 1, v)
                if more2:
                    norm(k + 2, tt + 1, u)
                if more:
                    spl.cube_dve(dve, k + 1)
                    spl.value_dve(dve, k + 1, v)

            norm(0, 0, 0, True)
            spl.center_dve(dve, 0, 0)
            norm(1, 0, 1)
            spl.cube_dve(dve, 0)
            spl.value_dve(dve, 0, 0)
            tile(0, 0, True, True, True)
            tile(0, 1, False, True, True)
            with dve.Fori(1, PAIRS // 2 - 1) as tt:
                for u in range(2):
                    tile(tt, u, False, True, True)
            tile(PAIRS // 2 - 1, 0, False, True, False)
            tile(PAIRS // 2 - 1, 1, False, False, False)

        @block.scalar
        def _(act):
            act.wait_ge(const_in, 32)

            def basis(tt, u, first, second=False):
                k = 2 * tt + u
                act.wait_ge(xT_ready, k + 1)
                for r in range(SETS):
                    nc.scalar.activation(spl.s[:, r * PT:(r + 1) * PT], xT[:, r // 4, 0:PT], ACT.Identity,
                                         bias=bias[:, r:r + 1], scale=SPL_SCALE).then_inc(spl.s_ready, 1)
                spl.round_act(act, k, u, first or second, SETS)
                spl.powers_act(act, k, first)

            def empty(t, first):
                for m in range(MC):
                    if m < MC - 1:
                        act.wait_ge(summed, (MC - 1) * t + m + 1)
                    else:
                        act.wait_ge(spl.f_used, 4 * t + 4)
                    if not (first and m < 2):
                        act.wait_ge(hid_out[m % 2], 16 * ((MC // 2) * t + m // 2))
                    nc.scalar.activation(hid[m % 2][:], acc[:, m, 0:PT], ACT.Copy, scale=1.0 / 6.0).then_inc(emptied, 1)

            basis(0, 0, True)
            basis(0, 1, False, True)
            empty(0, True)
            with act.Fori(1, PAIRS // 2) as tt:
                basis(tt, 0, False)
                empty(2 * tt - 1, False)
                basis(tt, 1, False)
                empty(2 * tt, False)
            empty(PAIRS - 1, False)

        @block.tensor
        def _(pe):
            def turn(t, first=False):
                pe.wait_ge(xn_ready, t + 1)
                pe.wait_ge(twice, t + 1)
                if not first:
                    pe.wait_ge(spl.s_ready, SETS * t)
                for i in range(2):
                    for n in range(4):
                        last = nc.tensor.transpose(xT[:, i, n * ROWS:(n + 1) * ROWS],
                                                   xn[0:ROWS, n, i * D0:(i + 1) * D0], ident[0:ROWS, 0:ROWS])
                last.then_inc(xT_ready, 1)

            def layer(k, first, more):
                for i in range(4):
                    if first:
                        pe.wait_ge(w_in, 16 * i + 16)
                    pe.wait_ge(spl.f_ready, 4 * k + i + 1)
                    for r in range(SETS):
                        for m in range(MC):
                            start, stop = i == 0 and r == 0, i == 3 and r == SETS - 1
                            if start and not first:
                                pe.wait_ge(emptied, MC * (k - 1) + m + 1)
                            last = nc.tensor.matmul(acc[:, m, 0:PT], w[:, i, r, m * P:(m + 1) * P],
                                                    spl.f[i][:, r * PT:(r + 1) * PT], start=start, stop=stop)
                            if stop and m < MC - 1:
                                last.then_inc(summed, 1)
                    last.then_inc(spl.f_used, 1)
                    if i == 2 and more:
                        turn(k + 2)

            pe.wait_ge(const_in, 32)
            turn(0, True)
            turn(1)
            layer(0, True, True)
            with pe.Fori(1, PAIRS - 2) as k:
                layer(k, False, True)
            layer(PAIRS - 2, False, False)
            layer(PAIRS - 1, False, False)


def spline2_phase(nc, a, h_scr, hid_scr, out):
    CH = HID // P
    SETS = 4 * CH
    with ExitStack() as stack:
        sb, ps, sem = memories(nc, stack)
        spl = Spline(nc, sb, sem, "spline2", SETS * P)
        w = sb("spline2_weights", [P, 4, SETS, D])
        bias = sb("spline2_offset", [P, 4])
        x = [sb(f"spline2_x{u}", [P, CH, P]) for u in range(2)]
        h = [sb(f"spline2_h{u}", [P, D]) for u in range(2)]
        y = [sb(f"spline2_y{u}", [P, D]) for u in range(2)]
        acc = ps("spline2_acc", [P, 2, 512])
        const_in, w_in = sem("spline2_const_in"), sem("spline2_w_in")
        x_in = [sem(f"spline2_x_in{u}") for u in range(2)]
        h_in = [sem(f"spline2_h_in{u}") for u in range(2)]
        y_ready = sem("spline2_y_ready")
        y_out = [sem(f"spline2_y_out{u}") for u in range(2)]
        block = stack.enter_context(nc.Block())

        @block.sync
        def _(sp):
            sp.dma_start(bias[:], a["spline2_bias"]).then_inc(const_in, 16)

            def load_h(t, u):
                sp.dma_start(h[u][:], h_scr[bass.ds(t * P, P), :]).then_inc(h_in[u], 16)

            def tile(k, u, more=True):
                sp.wait_ge(y_ready, k + 1)
                sp.dma_start(out[bass.ds(k * P, P), :], y[u][:]).then_inc(y_out[u], 16)
                if more:
                    load_h(k + 2, u)

            load_h(0, 0)
            load_h(1, 1)
            for i in range(4):
                if i > 0:
                    sp.wait_ge(w_in, 16 * i)
                sp.dma_start(w[:, i], a["w2"][:, i]).then_inc(w_in, 16)
            tile(0, 0)
            with sp.Fori(0, OT // 2 - 1) as tt:
                tile(2 * tt + 1, 1)
                tile(2 * tt + 2, 0)
            tile(OT - 2, 1, False)
            tile(OT - 1, 0, False)
            sp.wait_ge(y_out[0], 16 * (OT // 2 + 1))
            sp.wait_ge(y_out[1], 16 * (OT // 2))

        @block.gpsimd
        def _(pool):
            spl.cube_pool(pool, 0, True)
            with pool.Fori(1, OT) as k:
                spl.cube_pool(pool, k, False)

        @block.scalar
        def _(act):
            act.wait_ge(const_in, 16)

            def load_x(t, u):
                act.dma_start(x[u][:], hid_scr[:, :, bass.ds(t * P, P)]).then_inc(x_in[u], 16)

            def basis(tt, k, u, first=False, second=False, more=True):
                act.wait_ge(x_in[u], 16 * tt + 16)
                for r in range(4):
                    nc.scalar.activation(spl.s[:, r * HID:(r + 1) * HID].rearrange("p (c n) -> p c n", c=CH), x[u][:],
                                         ACT.Identity, bias=bias[:, r:r + 1], scale=SPL_SCALE).then_inc(spl.s_ready, 1)
                spl.round_act(act, k, u, first or second, 4)
                if more:
                    load_x(k + 2, u)
                spl.powers_act(act, k, first)

            load_x(0, 0)
            load_x(1, 1)
            basis(0, 0, 0, True)
            basis(0, 1, 1, False, True)
            with act.Fori(1, OT // 2 - 1) as tt:
                basis(tt, 2 * tt, 0)
                basis(tt, 2 * tt + 1, 1)
            basis(OT // 2 - 1, OT - 3, 0)
            basis(OT // 2 - 1, OT - 2, 1, more=False)
            basis(OT // 2, OT - 1, 0, more=False)

        @block.vector
        def _(dve):
            def tile(tt, k, u, first=False, more=True, early=False):
                v = 1 - u
                spl.take_dve(dve, k, u, 0, first)
                if more:
                    spl.center_dve(dve, k + 1, v)
                spl.take_dve(dve, k, u, 1, first)
                spl.take_dve(dve, k, u, 2, first)
                if more:
                    spl.cube_dve(dve, k + 1)
                spl.take_dve(dve, k, u, 3, first)
                if more:
                    spl.value_dve(dve, k + 1, v)
                if not first:
                    leave(tt - 1 if u == 0 else tt, k - 1, v, early)

            def leave(tt, k, u, early):
                dve.wait_ge(spl.f_used, 4 * k + 4)
                dve.wait_ge(h_in[u], 16 * tt + 16)
                if not early:
                    dve.wait_ge(y_out[u], 16 * tt)
                nc.vector.scalar_tensor_tensor(y[u][:], acc[:, u, 0:D], 1.0 / 6.0, h[u][:], ALU.mult,
                                               ALU.add).then_inc(y_ready, 1)

            spl.center_dve(dve, 0, 0)
            spl.cube_dve(dve, 0)
            spl.value_dve(dve, 0, 0)
            tile(0, 0, 0, True)
            tile(0, 1, 1, early=True)
            tile(1, 2, 0, early=True)
            with dve.Fori(1, OT // 2 - 1) as tt:
                tile(tt, 2 * tt + 1, 1)
                tile(tt + 1, 2 * tt + 2, 0)
            tile(OT // 2 - 1, OT - 2, 1)
            tile(OT // 2, OT - 1, 0, more=False)
            leave(OT // 2, OT - 1, 0, False)

        @block.tensor
        def _(pe):
            def layer(k, u, first=False):
                for i in range(4):
                    if isinstance(k, int) and k == 0:
                        pe.wait_ge(w_in, 16 * i + 16)
                    pe.wait_ge(spl.f_ready, 4 * k + i + 1)
                    if i == 0 and not first:
                        pe.wait_ge(y_ready, k - 1)
                    for r in range(SETS):
                        last = nc.tensor.matmul(acc[:, u, 0:D], spl.f[i][:, r * P:(r + 1) * P], w[:, i, r, :],
                                                start=(i == 0 and r == 0), stop=(i == 3 and r == SETS - 1))
                    last.then_inc(spl.f_used, 1)

            layer(0, 0, True)
            layer(1, 1, True)
            with pe.Fori(1, OT // 2) as tt:
                layer(2 * tt, 0)
                layer(2 * tt + 1, 1)
            layer(OT - 1, 0)


def program(nc, a, out):
    def scratch(name, *shape):
        return nc.dram_tensor(name, shape, F32, kind="Internal").ap()

    txt_scr = scratch("txt_scr", B * TXT, D)
    pos_scr = scratch("pos_scr", B, 2 * SAMPLES)
    pix_scr = scratch("pix_scr", B, PIXC, PIX)
    vis_scr = scratch("vis_scr", B * VIS, D)
    h_scr = scratch("h_scr", ALL, D)
    tokens(nc, a, txt_scr, pos_scr, pix_scr, vis_scr)
    attend_phase(nc, a, vis_scr, txt_scr, h_scr)
    hid_scr = scratch("hid_scr", P, HID // P, ALL)
    spline1_phase(nc, a, h_scr, hid_scr)
    spline2_phase(nc, a, h_scr, hid_scr, out.rearrange("b n d -> (b n) d"))


def tokens(nc, a, txt_scr, pos_scr, pix_scr, vis_scr):
    with ExitStack() as stack:
        hT_all = memories(nc, stack)[0]("stem_by_channel", [P, B * PIX])
        stem_phase(nc, a["patches"], a["stem_w"], a["stem_vec"], hT_all, pix_scr,
                   a["txt_idx"], a["table"], txt_scr)
        offset_phase(nc, a["off_w"], a["off_bias"], a["off_grid"], hT_all, pos_scr)
    with ExitStack() as stack:
        samp_all = memories(nc, stack)[0]("samples", [P, TAPS, B * VIS])
        sample_phase(nc, pos_scr, a["pix_neg"], pix_scr, samp_all)
        deform_phase(nc, a["dcn_w"], a["dcn_vec"], samp_all, vis_scr)


def layouts(i):
    import numpy as np

    f32 = np.float32

    def rep(*v):
        v = np.stack([np.asarray(x) for x in v])
        return np.broadcast_to(v[None], (P,) + v.shape)

    x = np.asarray(i["x"])
    tap = np.arange(TAPS)
    at = np.arange(HO) * K
    grid = np.zeros((TAPS, 2, HO, HO), f32)
    grid[:, 0] = at[None, :, None] + (tap // K)[:, None, None]
    grid[:, 1] = at[None, None, :] + (tap % K)[:, None, None]
    p = np.arange(PIXC)

    def chunks(w):
        r = np.zeros((P, 2) + w.shape[1:], w.dtype)
        r[:, 0], r[0:D1, 1] = w[0:D0], w[D0:D]
        return r

    def heads(w):
        w = w.reshape(w.shape[:-1] + (HG, 4, DH))
        return np.concatenate([w, w], -1).reshape(w.shape[:-3] + (HG, P))

    def biased(w, b):
        r = chunks(w)
        r[D1, 1] = b
        return r

    w = {k: np.asarray(v) for k, v in i.items() if k.startswith("L0_attn")}
    dist = np.abs(np.arange(P)[:, None, None] + ROWS * np.arange(2)[:, None] - np.arange(TOK))
    wo = np.zeros((4, 32, HG, D), f32)
    wo[:, 0:DH] = w["L0_attn_Wo"].reshape(HG, 4, DH, D).transpose(1, 2, 0, 3)
    row, group = np.arange(P)[:, None], np.arange(HG)[None]
    w1 = np.asarray(i["L0_ffn_w1"]).reshape(HID, D, 4, 4).transpose(1, 2, 3, 0)
    w1t = np.empty((P, 4, 6, HID), f32)
    w1t[:, :, 0:4] = w1[0:D0]
    w1t[0:D1, :, 4:6], w1t[D1:P, :, 4:6] = w1[D0:D, :, 0:2], w1[D0:D, :, 2:4]
    w2t = np.asarray(i["L0_ffn_w2"]).reshape(D, HID // P, P, 4, 4).transpose(2, 3, 4, 1, 0).reshape(P, 4, 16, D)
    r1 = np.tile(np.array([0, 1, 2, 3, 0, 1], f32), (P, 1))
    r1[D1:P, 4:6] += 2
    return {
        "w1": w1t,
        "w2": w2t,
        "spline1_bias": (SPL_BIAS - r1 / 4).astype(f32),
        "spline2_bias": np.tile((SPL_BIAS - np.arange(4) / 4).astype(f32), (P, 1)),
        "wq": biased(heads(w["L0_attn_Wq"]), heads(w["L0_attn_bq"])),
        "wk": biased(heads(w["L0_attn_Wk"]), heads(w["L0_attn_bk"])),
        "wv": biased(w["L0_attn_Wv"], w["L0_attn_bv"]),
        "wo": wo.reshape(P, HG, D),
        "bo": rep(w["L0_attn_bo"]),
        "pick": np.tile(-((row % 32 == group) | (row % 32 == HG + group)).astype(f32)[..., None], (1, 1, ROWS)),
        "minus_low": -np.concatenate([row % 32 >= DH, (row % 32 >= HG) & (row % 32 < 2 * HG)], 1).astype(f32),
        "identity": np.eye(P, dtype=f32),
        "mask": np.tile(np.where(dist <= 64, 0.0, NEG).astype(f32), (1, 1, 3)),
        "patches": x.reshape(B, 3, HS, K, HS, K).transpose(1, 3, 5, 0, 2, 4).reshape(PATCH, B, PIX),
        "stem_w": np.asarray(i["L0_tok_stem_w"]).reshape(C1, PATCH).T,
        "stem_vec": rep(i["L0_tok_stem_b"], i["L0_tok_bn1_g"], i["L0_tok_bn1_b"], i["L0_tok_bn1_m"], i["L0_tok_bn1_v"]),
        "txt_idx": np.asarray(i["x_txt"]).T,
        "table": np.asarray(i["L0_txt_weight"]),
        "off_w": np.asarray(i["L0_tok_off_w"]).reshape(2 * TAPS, C1, TAPS).transpose(1, 2, 0),
        "off_bias": np.asarray(i["L0_tok_off_b"])[:, None],
        "off_grid": np.tile(grid.reshape(2 * TAPS, VIS), (1, 8)),
        "pix_neg": -np.concatenate([(p // HS)[:, None] + 4 * np.arange(NPIXC)[None], (p % HS)[:, None]], 1).astype(f32),
        "dcn_w": np.asarray(i["L0_tok_dcn_w"]).reshape(D, C1, TAPS).transpose(1, 2, 0),
        "dcn_vec": rep(i["L0_tok_dcn_b"], i["L0_tok_bn2_g"], i["L0_tok_bn2_b"], i["L0_tok_bn2_m"], i["L0_tok_bn2_v"]),
    }


def kernel(**inputs):
    import numpy as np
    import concourse.bacc as bacc
    from concourse.bass_utils import run_bass_kernel_spmd

    nc = bacc.Bacc("TRN2", target_bir_lowering=False, num_devices=1)
    arrays = {k: np.ascontiguousarray(v) for k, v in layouts(inputs).items()}
    aps = {k: nc.dram_tensor(k, v.shape, mybir.dt.from_np(v.dtype), kind="ExternalInput").ap()
           for k, v in arrays.items()}
    out = nc.dram_tensor("out", (B, TOK, D), F32, kind="ExternalOutput").ap()
    program(nc, aps, out)
    return run_bass_kernel_spmd(nc, [arrays], core_ids=[0]).results[0]["out"]
```

```python
from contextlib import ExitStack

import concourse.bass as bass
from concourse import mybir

ALU = mybir.AluOpType
ACT = mybir.ActivationFunctionType
F32 = mybir.dt.float32
F32R = mybir.dt.float32r
BF16 = mybir.dt.bfloat16
I32 = mybir.dt.int32
AX_X = mybir.AxisListType.X

P = 128
B = 32
D = 192
D0, D1 = 128, 64
C1 = 96
K = 4
TAPS = K * K
HS = 24
PIX = HS * HS
HO = 6
VIS = HO * HO
TXT = 128
TOK = VIS + TXT
ROWS = TOK // 2
PAIRS = B // 2
PT = 2 * TOK
ALL = B * TOK
SAMPLES = TAPS * VIS
PATCH = 3 * TAPS
PIXC = 96
NPIXC = PIX // PIXC
HEADS, DH = 12, 16
HG = HEADS // 4
KPAD = 96
HID = 512
NCP = 16
EPS = 1e-5
SLOPE = 0.01
QMAX = 127.0
MAGIC = 12582912.0
NEG = -1.0e30
SPL_SCALE = 13.0 / 32.0
SPL_BIAS = (4.0 * 13.0 / 8.0 + 3.0) / 4.0 - 0.5
VT = B * VIS // P
OT = ALL // P


class Step:

    def __init__(self, engine, sem, base=0):
        self.engine, self.sem, self.base, self.n = engine, sem, base, 0

    def mark(self, ins):
        ins.then_inc(self.sem, 1)
        self.n += 1
        return self.n

    def after(self, n):
        self.engine.wait_ge(self.sem, self.base + n)

    def run(self, ins):
        self.after(self.mark(ins))


def memories(nc, stack):
    def sb(name, shape, dt=F32):
        return stack.enter_context(nc.sbuf_tensor(name, shape, dt))

    def ps(name, shape):
        return stack.enter_context(nc.psum_tensor(name, shape, F32))

    def sem(name):
        return stack.enter_context(nc.semaphore(name))

    return sb, ps, sem


def fold_norm(nc, dve, s, pow_done, rows, std, inv, half):
    bias, gamma, beta, mean, var = (rows[:, j, :] for j in range(5))
    s.run(nc.vector.tensor_scalar(std[:, :], var, EPS, None, ALU.add))
    dve.wait_ge(pow_done, 1)
    s.run(nc.vector.tensor_tensor(half[:, :], inv[:, :], inv[:, :], ALU.mult))
    s.run(nc.vector.tensor_tensor(half[:, :], half[:, :], std[:, :], ALU.mult))
    s.run(nc.vector.tensor_scalar(half[:, :], half[:, :], -0.5, 1.5, ALU.mult, ALU.add))
    s.run(nc.vector.tensor_tensor(inv[:, :], inv[:, :], half[:, :], ALU.mult))
    s.run(nc.vector.tensor_tensor(inv[:, :], inv[:, :], gamma, ALU.mult))
    s.run(nc.vector.tensor_tensor(std[:, :], bias, mean, ALU.subtract))
    s.run(nc.vector.tensor_tensor(std[:, :], std[:, :], inv[:, :], ALU.mult))
    s.run(nc.vector.tensor_tensor(std[:, :], std[:, :], beta, ALU.add))
    return std[:, :]


def stem_phase(nc, patches, stem_w, cvec, hT_all, pix_scr, txt_idx, table, txt_scr):
    with ExitStack() as stack:
        sb, ps, sem = memories(nc, stack)
        patch = [sb(f"patch{u}", [P, PIX]) for u in range(2)]
        w = sb("stem_weights", [P, C1])
        rows = sb("stem_vectors", [P, 5, C1])
        half = sb("stem_half", [P, C1])
        std = sb("stem_std", [P, C1])
        inv = sb("stem_inv", [P, C1])
        chan = ps("by_channel", [P, 2, 2, 512])
        pix = ps("by_pixel", [P, 2, 2, 512])
        by_pixel = [sb(f"stem_by_pixel{u}", [P, PIX]) for u in range(4)]
        idx = sb("text_index", [P, B], I32)
        emb = [sb(f"text_rows{u}", [P, D]) for u in range(4)]
        quant = [sb(f"text_quant{u}", [P, D]) for u in range(4)]
        q_amax = sb("text_amax", [P, 4])
        q_scale = sb("text_scale", [P, 4])
        q_rec = sb("text_rec", [P, 4])
        vectors_in = sem("vectors_in")
        zeroed = sem("stem_zeroed")
        ones_set = sem("stem_ones")
        bn = sem("stem_bn")
        bn_pow = sem("stem_pow")
        w_ready = sem("stem_w_ready")
        patch_in = [sem(f"patch_in{u}") for u in range(2)]
        stem_done = sem("stem_done")
        scaled = sem("stem_scaled")
        stem_read = sem("stem_read")
        pixel_out = [sem(f"stem_pixel_out{u}") for u in range(4)]
        idx_in = sem("text_index_in")
        emb_in = [sem(f"text_in{u}") for u in range(4)]
        q_step = sem("text_step")
        q_done = sem("text_done")
        txt_out = [sem(f"text_out{u}") for u in range(4)]
        block = stack.enter_context(nc.Block())

        @block.sync
        def _(sp):
            sp.dma_start(rows[:, :, :], cvec).then_inc(vectors_in, 16)
            sp.wait_ge(zeroed, 1)
            sp.dma_start(w[0:PATCH, :], stem_w).then_inc(vectors_in, 16)
            for u in range(2):
                sp.dma_start(patch[u][0:PATCH, :], patches[:, u, :]).then_inc(patch_in[u], 16)

            def results_out(t, u):
                sp.wait_ge(stem_read, 2 * (4 * t + u) + 2)
                sp.dma_start(pix_scr[bass.ds(4 * t + u, 1), :, :].rearrange("b p n -> p (b n)"),
                             by_pixel[u][0:PIXC, :]).then_inc(pixel_out[u], 16)
                sp.wait_ge(q_done, 4 * t + u + 1)
                sp.dma_start(txt_scr[bass.ds((4 * t + u) * TXT, TXT), :], quant[u][:, :]).then_inc(txt_out[u], 16)

            with sp.Fori(0, B // 4 - 1) as t:
                for u in range(4):
                    sp.wait_ge(stem_done, 4 * t + u + 1)
                    sp.dma_start(patch[u % 2][0:PATCH, :],
                                 patches[:, bass.ds(4 * t + u + 2, 1), :].rearrange("p b n -> p (b n)")
                                 ).then_inc(patch_in[u % 2], 16)
                    results_out(t, u)
            for u in range(4):
                t = B // 4 - 1
                if u < 2:
                    sp.wait_ge(stem_done, 4 * t + u + 1)
                    sp.dma_start(patch[u][0:PATCH, :], patches[:, 4 * t + u + 2, :]).then_inc(patch_in[u], 16)
                results_out(t, u)
            for u in range(4):
                sp.wait_ge(txt_out[u], 16 * (B // 4))
                sp.wait_ge(pixel_out[u], 16 * (B // 4))

        @block.gpsimd
        def _(pool):
            pool.memset(patch[0][:, :], 0.0)
            pool.memset(patch[1][:, :], 0.0)
            pool.memset(w[:, :], 0.0).then_inc(zeroed, 1)
            pool.memset(half[:, :], -0.5).then_inc(zeroed, 1)
            pool.dma_start(idx[:, :], txt_idx).then_inc(idx_in, 16)
            pool.wait_ge(zeroed, 2)
            pool.memset(patch[0][KPAD:KPAD + 1, :], 1.0).then_inc(ones_set, 1)
            pool.memset(patch[1][KPAD:KPAD + 1, :], 1.0).then_inc(ones_set, 1)
            pool.wait_ge(ones_set, 2)
            pool.wait_ge(bn, 1)
            pool.tensor_tensor(inv[:, :], std[:, :], half[:, :], ALU.pow).then_inc(bn_pow, 1)
            pool.wait_ge(idx_in, 16)
            for b in range(B):
                if b >= 4:
                    pool.wait_ge(q_done, b - 3)
                pool.indirect_dma_start(emb[b % 4][:, :], None, table,
                                        bass.IndirectOffsetOnAxis(idx[:, b:b + 1], 0)).then_inc(emb_in[b % 4], 16)

        @block.vector
        def _(dve):
            s = Step(dve, bn)
            dve.wait_ge(vectors_in, 32)
            shift = fold_norm(nc, dve, s, bn_pow, rows, std, inv, half)
            nc.vector.tensor_tensor(w[0:PATCH, :], w[0:PATCH, :], inv[0:PATCH, :], ALU.mult).then_inc(w_ready, 1)
            nc.vector.tensor_copy(w[KPAD:KPAD + 1, :], shift[KPAD:KPAD + 1, :]).then_inc(w_ready, 1)

            def image(t, u, first):
                for n, (src, dst) in enumerate(((chan, hT_all[0:C1, bass.ds((4 * t + u) * PIX, PIX)]),
                                                (pix, by_pixel[u][0:PIXC, :]))):
                    dve.wait_ge(scaled, 8 * t + 2 * u + n + 1)
                    y = dst.rearrange("p (h n) -> p h n", h=2)
                    nc.vector.tensor_tensor(y, src[0:C1, u % 2, :, 0:PIX // 2], y, ALU.max).then_inc(stem_read, 1)
                e, q = emb[u], quant[u]
                s = Step(dve, q_step, 7 * (4 * t + u))
                dve.wait_ge(emb_in[u], 16 * t + 16)
                s.run(nc.vector.tensor_reduce(q_amax[:, u:u + 1], e[:, :], AX_X, ALU.max, apply_absolute_value=True))
                s.run(nc.vector.tensor_scalar(q_scale[:, u:u + 1], q_amax[:, u:u + 1], 1e-8, 1.0 / QMAX,
                                              ALU.max, ALU.mult))
                s.run(nc.vector.reciprocal(q_rec[:, u:u + 1], q_scale[:, u:u + 1]))
                if not first:
                    dve.wait_ge(txt_out[u], 16 * t)
                s.run(nc.vector.tensor_scalar(q[:, :], e[:, :], q_rec[:, u:u + 1], MAGIC, ALU.mult, ALU.add))
                s.run(nc.vector.tensor_scalar(q[:, :], q[:, :], MAGIC, -QMAX, ALU.subtract, ALU.max))
                s.run(nc.vector.tensor_scalar(q[:, :], q[:, :], QMAX, q_scale[:, u:u + 1], ALU.min, ALU.mult))
                s.run(nc.vector.tensor_tensor(q[:, :], q[:, :], e[:, :], ALU.subtract))
                nc.vector.tensor_tensor(q[:, :], e[:, :], q[:, :], ALU.add).then_inc(q_done, 1)

            for u in range(4):
                image(0, u, True)
            with dve.Fori(1, B // 4) as t:
                for u in range(4):
                    image(t, u, False)

        @block.tensor
        def _(pe):
            pe.wait_ge(w_ready, 2)
            pe.wait_ge(ones_set, 2)

            def image(t, u, first):
                pe.wait_ge(patch_in[u], 16 * t + 16)
                if not first:
                    pe.wait_ge(stem_read, 4 * t + 2 * u - 2)
                x = patch[u]
                for h in range(2):
                    nc.tensor.matmul(chan[0:C1, u, h, 0:PIX // 2], w[0:KPAD + 1, :],
                                     x[0:KPAD + 1, h * PIX // 2:(h + 1) * PIX // 2], start=True, stop=True)
                for c in range(NPIXC):
                    last = nc.tensor.matmul(pix[0:PIXC, u, c // 3, (c % 3) * C1:(c % 3 + 1) * C1],
                                            x[0:KPAD + 1, c * PIXC:(c + 1) * PIXC], w[0:KPAD + 1, :],
                                            start=True, stop=True)
                last.then_inc(stem_done, 1)

            for u in range(2):
                image(0, u, True)
            with pe.Fori(1, B // 2) as t:
                for u in range(2):
                    image(t, u, False)

        @block.scalar
        def _(act):
            def image(t, u, first):
                act.wait_ge(stem_done, 4 * t + u + 1)
                if not first:
                    act.wait_ge(pixel_out[u], 16 * t)
                for src, dst in ((chan, hT_all[0:C1, bass.ds((4 * t + u) * PIX, PIX)]),
                                 (pix, by_pixel[u][0:PIXC, :])):
                    nc.scalar.activation(dst.rearrange("p (h n) -> p h n", h=2),
                                         src[0:C1, u % 2, :, 0:PIX // 2], ACT.Copy, scale=SLOPE).then_inc(scaled, 1)

            for u in range(4):
                image(0, u, True)
            with act.Fori(1, B // 4) as t:
                for u in range(4):
                    image(t, u, False)


def offset_phase(nc, off_w, off_vec, grid, hT_all, pos_scr):
    GI = 8
    NG = B // GI
    with ExitStack() as stack:
        sb, ps, sem = memories(nc, stack)
        w = sb("offset_weights", [P, TAPS, 2 * TAPS])
        bias = sb("offset_bias", [P, 1])
        base = sb("offset_grid", [P, GI * VIS])
        pos = sb("offset_pos", [P, NG, GI * VIS])
        acc = ps("offset_acc", [P, NG, 512])
        weights_in = sem("offset_weights_in")
        conv_done = sem("offset_conv_done")
        pos_ready = sem("offset_pos_ready")
        pos_out = sem("offset_pos_out")
        block = stack.enter_context(nc.Block())

        @block.sync
        def _(sp):
            sp.dma_start(w[0:C1, :, :], off_w).then_inc(weights_in, 16)
            sp.dma_start(bias[0:2 * TAPS, :], off_vec).then_inc(weights_in, 16)
            sp.dma_start(base[0:2 * TAPS, :], grid).then_inc(weights_in, 16)
            for g in range(NG):
                sp.wait_ge(pos_ready, g + 1)
                sp.dma_start(pos_scr[g * GI:(g + 1) * GI, :].rearrange("b (c n) -> c b n", n=VIS),
                             pos[0:2 * TAPS, g, :].rearrange("c (b n) -> c b n", n=VIS)).then_inc(pos_out, 16)
            sp.wait_ge(pos_out, 16 * NG)

        @block.tensor
        def _(pe):
            pe.wait_ge(weights_in, 48)
            taps = hT_all[0:C1, :].rearrange("p (b i r j s) -> p r s b i j", b=B, i=HO, r=K, j=HO, s=K)
            for g in range(NG):
                for kk in range(TAPS):
                    last = nc.tensor.matmul(acc[0:2 * TAPS, g, 0:GI * VIS], w[0:C1, kk, :],
                                            taps[:, kk // K, kk % K, g * GI:(g + 1) * GI],
                                            start=(kk == 0), stop=(kk == TAPS - 1))
                last.then_inc(conv_done, 1)

        @block.vector
        def _(dve):
            dve.wait_ge(weights_in, 48)
            for g in range(NG):
                dve.wait_ge(conv_done, g + 1)
                nc.vector.scalar_tensor_tensor(pos[0:2 * TAPS, g, :], acc[0:2 * TAPS, g, 0:GI * VIS],
                                               bias[0:2 * TAPS, 0:1], base[0:2 * TAPS, :],
                                               ALU.add, ALU.add).then_inc(pos_ready, 1)


def sample_phase(nc, pos_scr, pix_neg, pix_scr, samp_all):
    S2 = SAMPLES // 2
    with ExitStack() as stack:
        sb, ps, sem = memories(nc, stack)
        neg = sb("pixel_neg", [P, NPIXC + 1])
        pos = [sb(f"sample_pos{u}", [P, 2 * SAMPLES]) for u in range(2)]
        h = [sb(f"sample_h{u}", [P, PIX]) for u in range(2)]
        hx = [sb(f"hat_x{u}", [P, SAMPLES]) for u in range(2)]
        dy = [sb(f"dist_y{u}", [P, NPIXC, SAMPLES]) for u in range(2)]
        wt = sb("hat_weights", [P, 2, NPIXC, SAMPLES])
        acc = ps("sample_acc", [P, 2, 2, 512])
        const_in = sem("pixel_in")
        pos_in = [sem(f"sample_pos_in{u}") for u in range(2)]
        h_in = [sem(f"sample_h_in{u}") for u in range(2)]
        dist = sem("sample_dist")
        clipped = sem("sample_clipped")
        weights = sem("sample_weights")
        product = sem("sample_product")
        stored = sem("sample_stored")
        block = stack.enter_context(nc.Block())

        @block.sync
        def _(sp):
            sp.dma_start(neg[0:PIXC, :], pix_neg).then_inc(const_in, 16)

            def load(b, u):
                sp.dma_start(pos[u][0:PIXC, :], pos_scr[bass.ds(b, 1), :].rearrange("a n -> (a n)")
                             .partition_broadcast(PIXC)).then_inc(pos_in[u], 16)

            for u in range(2):
                load(u, u)
            with sp.Fori(1, B // 2) as t:
                for u in range(2):
                    sp.wait_ge(dist, 2 * t + u - 1)
                    load(2 * t + u, u)

        @block.gpsimd
        def _(pool):
            def load(b, u):
                pool.dma_start(h[u][0:PIXC, :], pix_scr[bass.ds(b, 1), :, :].rearrange("b p n -> p (b n)")
                               ).then_inc(h_in[u], 16)

            for u in range(2):
                load(u, u)
            with pool.Fori(1, B // 2) as t:
                for u in range(2):
                    pool.wait_ge(product, 2 * t + u - 1)
                    load(2 * t + u, u)

        @block.vector
        def _(dve):
            def weigh(t, u, first):
                s = Step(dve, clipped, 2 * (2 * t + u))
                dve.wait_ge(dist, 2 * t + u + 1)
                s.mark(nc.vector.tensor_scalar(hx[u][0:PIXC, :], hx[u][0:PIXC, :], 1.0, 1.0, ALU.min, ALU.subtract))
                s.run(nc.vector.tensor_scalar(dy[u][0:PIXC], dy[u][0:PIXC], 1.0, 1.0, ALU.min, ALU.subtract))
                if not first:
                    dve.wait_ge(product, 2 * t + u - 1)
                nc.vector.tensor_tensor(wt[0:PIXC, u], dy[u][0:PIXC],
                                        hx[u][0:PIXC, :].rearrange("p (a n) -> p a n", a=1)
                                        .to_broadcast([PIXC, NPIXC, SAMPLES]), ALU.mult).then_inc(weights, 1)

            for u in range(2):
                weigh(0, u, True)
            with dve.Fori(1, B // 2) as t:
                for u in range(2):
                    weigh(t, u, False)

        @block.scalar
        def _(act):
            act.wait_ge(const_in, 16)

            def distances(t, u, first):
                p = pos[u][0:PIXC, :].rearrange("p (k a n) -> p a k n", k=TAPS, a=2)
                act.wait_ge(pos_in[u], 16 * t + 16)
                if not first:
                    act.wait_ge(weights, 2 * t + u - 1)
                for c in range(NPIXC):
                    nc.scalar.activation(dy[u][0:PIXC, c, :].rearrange("p (k n) -> p k n", k=TAPS), p[:, 0],
                                         ACT.Abs, bias=neg[0:PIXC, c:c + 1])
                nc.scalar.activation(hx[u][0:PIXC, :].rearrange("p (k n) -> p k n", k=TAPS), p[:, 1],
                                     ACT.Abs, bias=neg[0:PIXC, NPIXC:NPIXC + 1]).then_inc(dist, 1)

            def store(t, u):
                act.wait_ge(product, 2 * t + u + 1)
                nc.scalar.activation(
                    samp_all[0:C1, :, bass.ds((2 * t + u) * VIS, VIS)],
                    acc[0:C1, u, :, 0:S2].rearrange("p h (k n) -> p h k n", n=VIS), ACT.Copy).then_inc(stored, 1)

            distances(0, 0, True)
            distances(0, 1, True)
            with act.Fori(1, B // 2) as t:
                for u in range(2):
                    distances(t, u, False)
                    store(t - 1, u)
            for u in range(2):
                store(B // 2 - 1, u)

        @block.tensor
        def _(pe):
            def image(t, u, first):
                pe.wait_ge(h_in[u], 16 * t + 16)
                pe.wait_ge(weights, 2 * t + u + 1)
                if not first:
                    pe.wait_ge(stored, 2 * t + u - 1)
                for half in range(2):
                    for c in range(NPIXC):
                        last = nc.tensor.matmul(acc[0:C1, u, half, 0:S2], h[u][0:PIXC, c * C1:(c + 1) * C1],
                                                wt[0:PIXC, u, c, half * S2:(half + 1) * S2],
                                                start=(c == 0), stop=(c == NPIXC - 1))
                last.then_inc(product, 1)

            for u in range(2):
                image(0, u, True)
            with pe.Fori(1, B // 2) as t:
                for u in range(2):
                    image(t, u, False)


def deform_phase(nc, dcn_w, vec, samp_all, vis_scr):
    with ExitStack() as stack:
        sb, ps, sem = memories(nc, stack)
        w = sb("deform_weights", [P, TAPS, D])
        rows = sb("deform_vectors", [P, 5, D])
        half = sb("deform_half", [P, D])
        std = sb("deform_std", [P, D])
        inv = sb("deform_inv", [P, D])
        tok = sb("deform_tokens", [P, VT, D])
        acc = ps("deform_acc", [P, 4, 512])
        vectors_in = sem("deform_in")
        half_set = sem("deform_half_set")
        bn = sem("deform_bn")
        bn_pow = sem("deform_pow")
        product = sem("deform_product")
        step = sem("deform_step")
        tok_ready = sem("deform_ready")
        tok_out = sem("deform_out")
        block = stack.enter_context(nc.Block())

        @block.sync
        def _(sp):
            sp.dma_start(rows[:, :, :], vec).then_inc(vectors_in, 16)
            sp.dma_start(w[0:C1, :, :], dcn_w).then_inc(vectors_in, 16)
            for t in range(VT):
                sp.wait_ge(tok_ready, t + 1)
                sp.dma_start(vis_scr[t * P:(t + 1) * P, :], tok[:, t, :]).then_inc(tok_out, 16)
            sp.wait_ge(tok_out, 16 * VT)

        @block.gpsimd
        def _(pool):
            pool.memset(half[:, :], -0.5).then_inc(half_set, 1)
            pool.wait_ge(half_set, 1)
            pool.wait_ge(bn, 1)
            pool.tensor_tensor(inv[:, :], std[:, :], half[:, :], ALU.pow).then_inc(bn_pow, 1)

        @block.tensor
        def _(pe):
            pe.wait_ge(vectors_in, 32)
            for t in range(VT):
                if t >= 4:
                    pe.wait_ge(step, 3 * (t - 4) + 1)
                for kk in range(TAPS):
                    last = nc.tensor.matmul(acc[:, t % 4, 0:D], samp_all[0:C1, kk, t * P:(t + 1) * P],
                                            w[0:C1, kk, :], start=(kk == 0), stop=(kk == TAPS - 1))
                last.then_inc(product, 1)

        @block.vector
        def _(dve):
            dve.wait_ge(vectors_in, 32)
            s = Step(dve, bn)
            shift = fold_norm(nc, dve, s, bn_pow, rows, std, inv, half)
            s = Step(dve, step)
            for t in range(VT):
                dve.wait_ge(product, t + 1)
                y = tok[:, t, :]
                s.run(nc.vector.tensor_tensor(y, acc[:, t % 4, 0:D], inv[:, :], ALU.mult))
                s.run(nc.vector.tensor_tensor(y, y, shift, ALU.add))
                s.run(nc.vector.scalar_tensor_tensor(y, y, SLOPE, y, ALU.mult, ALU.max))
                dve.sem_inc(tok_ready, 1)


def layer_stats(nc, dve, s, held, x, stats, mv, ve):
    for n in range(4):
        s.mark(nc.vector.bn_stats(stats[0:ROWS, n, :], x[0:ROWS, n, :]))
    s.after(4)
    dve.sem_inc(held, 1)
    for n in range(4):
        last = s.mark(nc.vector.bn_aggr(mv[0:ROWS, n, :], stats[0:ROWS, n, :]))
    s.after(last)
    s.mark(nc.vector.tensor_scalar(ve[0:ROWS, :], mv[0:ROWS, :, 1], EPS, None, ALU.add))


def layer_rest(nc, dve, s, pow_done, pow_count, x, xn, mv, ve, rstd, tmp):
    s.n = LN_VAR
    dve.wait_ge(pow_done, pow_count)
    s.run(nc.vector.tensor_tensor(tmp[0:ROWS, :], rstd[0:ROWS, :], rstd[0:ROWS, :], ALU.mult))
    s.run(nc.vector.tensor_tensor(tmp[0:ROWS, :], tmp[0:ROWS, :], ve[0:ROWS, :], ALU.mult))
    s.run(nc.vector.tensor_scalar(tmp[0:ROWS, :], tmp[0:ROWS, :], -0.5, 1.5, ALU.mult, ALU.add))
    s.run(nc.vector.tensor_tensor(rstd[0:ROWS, :], rstd[0:ROWS, :], tmp[0:ROWS, :], ALU.mult))
    for n in range(4):
        last = nc.vector.tensor_scalar(xn[0:ROWS, n, 0:D], x[0:ROWS, n, :], mv[0:ROWS, n, 0:1],
                                       rstd[0:ROWS, n:n + 1], ALU.subtract, ALU.mult)
        if n < 3:
            s.mark(last)
    return last


LN_VAR = 9
LN_STEPS = 16


def attend_phase(nc, a, vis_scr, txt_scr, h_scr):
    SCALE = DH ** -0.5
    SC = HG * TOK
    NX = 18
    with ExitStack() as stack:
        sb, ps, sem = memories(nc, stack)
        wq = sb("attend_wq", [P, 2, HG, P])
        wk = sb("attend_wk", [P, 2, HG, P])
        wv = sb("attend_wv", [P, 2, D])
        wo = sb("attend_wo", [P, HG, D])
        bo = sb("attend_bo", [P, 1, D])
        ident = sb("attend_identity", [P, P])
        identb = sb("attend_identity_bf16", [P, P], BF16)
        mask = sb("window_mask", [P, 2, SC])
        maskb = sb("window_mask_bf16", [P, 2, SC], BF16)
        pick = sb("attend_pick", [P, HG, ROWS])
        pickr = sb("attend_pick_r", [P, HG, ROWS], F32R)
        minus_low = sb("attend_minus_low", [P, 2])
        minus_half = sb("attend_half", [P, 4])
        ones = sb("attend_ones", [P, 32])
        x = [sb(f"attend_x{u}", [P, 4, D]) for u in range(2)]
        resid = [sb(f"attend_resid{u}", [P, 4, D]) for u in range(2)]
        xn = sb("attend_xn", [P, 4, D])
        stats, mv = sb("attend_stats", [P, 4, 6]), sb("attend_mv", [P, 4, 2])
        ve, rstd, tmp = (sb(f"attend_{k}", [P, 4]) for k in ("ve", "rstd", "tmp"))
        xT = sb("attend_xT", [P, 2, PT])
        qh = sb("attend_q_high", [P, HG, PT], F32R)
        q1, k1, k2 = ([sb(f"attend_{k}{u}", [P, HG, PT], F32R) for u in range(2)] for k in ("q1_", "k1_", "k2_"))
        va = [sb(f"attend_v{u}", [P, 4, HEADS, 32]) for u in range(2)]
        mx = sb("attend_max", [P, 2, 4, 32])
        mh = sb("attend_max_high", [P, TOK], F32R)
        mT = sb("attend_max_split", [P, TOK], F32R)
        prT = sb("attend_probs", [P, 2, HEADS, TOK])
        total = sb("attend_total", [P, SC])
        rec = sb("attend_rec", [P, SC])
        oT = sb("attend_oT", [P, HG, TOK])
        h2 = [sb(f"attend_h{u}", [P, 4, D]) for u in range(2)]
        sc = ps("scores_by_query", [P, 2, 512])
        tp = ps("scores_by_key", [P, 4, 512])
        xb = ps("attend_spare", [P, 2, 512])
        dve_held, pe_held = sem("attend_dve_held"), sem("attend_pe_held")
        const_in, consts, half_set = sem("attend_const_in"), sem("attend_consts"), sem("attend_half_set")
        zeros_set, ones_set = sem("attend_zeros"), sem("attend_ones")
        x_in = [sem(f"attend_x_in{u}") for u in range(2)]
        resid_ready = sem("attend_resid_ready")
        ln, pow_done, xn_ready = sem("attend_ln"), sem("attend_pow"), sem("attend_xn_ready")
        filled = [sem(f"spare_filled{i}") for i in range(2)]
        split = sem("attend_split")
        emptied = [sem(f"spare_emptied{i}") for i in range(2)]
        by_query, by_key = sem("attend_by_query"), sem("attend_by_key")
        maxed, doubled, exped = sem("attend_maxed"), sem("attend_doubled"), sem("attend_exped")
        inverted = sem("attend_inverted")
        h_ready = sem("attend_h_ready")
        h_out = [sem(f"attend_h_out{u}") for u in range(2)]
        block = stack.enter_context(nc.Block())
        loads = ((wq, a["wq"]), (wk, a["wk"]), (wv, a["wv"]), (wo, a["wo"]), (bo, a["bo"]), (ident, a["identity"]),
                 (mask, a["mask"]), (pick, a["pick"]), (minus_low, a["minus_low"]))
        CONSTS = 16 * len(loads)

        X, Q, K_, V = (0, 1), (3, 4, 5), (8, 9, 10), (13, 16)
        Y, SUM, MAX, MIX = (2, 12), (6, 14), (7, 15), (11, 17)
        START = dict(X=(0, 1), Q=(2, 3, 4), K=(5, 6, 7), V=(8, 9), MAX=10)
        SPLIT0, SPLITS = 2 * HG + 1, 2 * HG + 2
        SKIPPED = X + Q + K_ + V + (MAX[1],)

        def use(t, k):
            n = len(START["X"] + START["Q"] + START["K"] + START["V"]) // 2 + NX // 2 * t + k // 2
            if isinstance(t, int):
                n += t == 0 and k == 0
                past = SKIPPED + X[:1] if t == PAIRS else [j for j in SKIPPED if j < k] if t == PAIRS - 1 else []
                n -= sum(j % 2 == k % 2 for j in past)
            return k % 2, n

        def start(k):
            return k % 2, k // 2

        @block.sync
        def _(sp):
            for dst, src in loads:
                sp.dma_start(dst[:], src).then_inc(const_in, 16)

            vis = vis_scr.rearrange("(b v) d -> v b d", v=VIS)
            txt = txt_scr.rearrange("(b v) d -> v b d", v=TXT)
            rest = ROWS - VIS

            def load(t, u):
                b = bass.ds(2 * t, 2)
                even, odd = x[u][:, 0:4:2, :], x[u][:, 1:4:2, :]
                sp.dma_start(even[0:VIS], vis[:, b, :]).then_inc(x_in[u], 16)
                sp.dma_start(even[VIS:ROWS], txt[0:rest, b, :]).then_inc(x_in[u], 16)
                sp.dma_start(odd[0:ROWS], txt[rest:TXT, b, :]).then_inc(x_in[u], 16)

            def leave(t, u):
                sp.wait_ge(h_ready, 2 * t + 2)
                sp.dma_start(h_scr[bass.ds(t * PT, PT), :].rearrange("(n p) d -> p n d", p=ROWS),
                             h2[u][0:ROWS]).then_inc(h_out[u], 16)

            load(0, 0)
            load(1, 1)
            with sp.Fori(0, PAIRS // 2 - 1) as tt:
                for u in range(2):
                    sp.wait_ge(resid_ready, 2 * tt + u + 1)
                    sp.wait_ge(xn_ready, 2 * tt + u + 1)
                    load(2 * tt + u + 2, u)
                    leave(2 * tt + u, u)
            for u in range(2):
                leave(PAIRS - 2 + u, u)
            for u in range(2):
                sp.wait_ge(h_out[u], 16 * (PAIRS // 2))

        @block.gpsimd
        def _(pool):
            pool.memset(minus_half[:, :], -0.5).then_inc(half_set, 1)
            pool.memset(mx[:], 0.0).then_inc(zeros_set, 1)
            pool.memset(ones[:], 1.0).then_inc(ones_set, 1)
            for u in range(2):
                pool.memset(va[u][:], 0.0).then_inc(zeros_set, 1)
            pool.wait_ge(half_set, 1)
            pool.wait_ge(zeros_set, 3)
            pool.wait_ge(ones_set, 1)
            pool.memset(xT[D1:D1 + 1, 1, :], 1.0).then_inc(ones_set, 1)
            pool.wait_ge(ones_set, 2)
            pool.wait_ge(const_in, CONSTS)

            def pair(tt, u):
                t = 2 * tt + u
                pool.wait_ge(ln, LN_STEPS * t + LN_VAR)
                pool.tensor_tensor(rstd[0:ROWS, :], ve[0:ROWS, :], minus_half[0:ROWS, :], ALU.pow).then_inc(pow_done, 1)
                if not (isinstance(tt, int) and tt == 0):
                    pool.wait_ge(h_ready, 2 * t - 2)
                pool.tensor_tensor(resid[u][0:ROWS], x[u][0:ROWS],
                                   bo[0:ROWS, :, :].to_broadcast([ROWS, 4, D]), ALU.add).then_inc(resid_ready, 1)

            pair(0, 0)
            pair(0, 1)
            with pool.Fori(1, PAIRS // 2) as tt:
                for u in range(2):
                    pair(tt, u)

        @block.vector
        def _(dve):
            dve.wait_ge(const_in, CONSTS)
            nc.vector.tensor_copy(identb[:], ident[:]).then_inc(consts, 1)
            nc.vector.tensor_copy(maskb[:], mask[:]).then_inc(consts, 1)
            nc.vector.tensor_copy(pickr[:], pick[:]).then_inc(consts, 1)
            dve.wait_ge(zeros_set, 3)

            def norm_in(tt, u):
                dve.wait_ge(x_in[u], 48 * tt + 48)
                layer_stats(nc, dve, Step(dve, ln, LN_STEPS * (2 * tt + u)), dve_held, x[u], stats, mv, ve)

            def norm_out(tt, u, turned):
                t = 2 * tt + u
                if turned is not None:
                    bank, c = turned
                    dve.wait_ge(filled[bank], c + 1)
                layer_rest(nc, dve, Step(dve, ln, LN_STEPS * t), pow_done, t + 1, x[u], xn, mv, ve, rstd,
                           tmp).then_inc(xn_ready, 1)

            def maximum(a, q):
                n, h = divmod(q, 2)
                dve.wait_ge(by_query, 4 * a + q + 1)
                nc.vector.tensor_reduce(mx[0:ROWS, n, 2 * h:2 * h + 2, 0:HG],
                                        sc[0:ROWS, :, 0:SC].rearrange("p j (g n) -> p j g n", n=TOK),
                                        AX_X, ALU.max).then_inc(maxed, 1)

            def double(a):
                dve.wait_ge(maxed, 4 * a + 4)
                nc.vector.tensor_copy(mx[0:ROWS, :, :, HG:2 * HG], mx[0:ROWS, :, :, 0:HG]).then_inc(doubled, 1)

            def low(at, count, dst, high, factor):
                bank, c = at
                cols = dst.shape[-1]
                dve.wait_ge(split, count)
                nc.vector.scalar_tensor_tensor(dst, high.bitcast(F32), factor, xb[:, bank, 0:cols], ALU.mult,
                                               ALU.add).then_inc(emptied[bank], 1)

            def low_q(u, g, at, count):
                low(at, count, q1[u][:, g, :], qh[:, g, :], minus_low[:, 0:1])

            def low_k(u, g, at, count):
                low(at, count, k2[u][:, g, :], k1[u][:, g, :], -1.0)

            def low_max(at, count):
                low(at, count, mT[:], mh[:], minus_low[:, 1:2])

            def values(u, i, at):
                bank, c = at
                dve.wait_ge(filled[bank], c + 1)
                nc.vector.tensor_copy(va[u][0:ROWS, 2 * i:2 * i + 2, :, 0:DH],
                                      xb[0:ROWS, bank, 0:2 * D].rearrange("p (n h d) -> p n h d", n=2, d=DH)
                                      ).then_inc(emptied[bank], 1)

            def invert(g, at):
                bank, c = at
                dve.wait_ge(emptied[bank], c + 1)
                cols = slice(g * TOK, (g + 1) * TOK)
                nc.vector.reciprocal(rec[:, cols], total[:, cols]).then_inc(inverted, 1)

            def weigh(a, at):
                bank, c = at
                dve.wait_ge(filled[bank], c + 1)
                dve.wait_ge(inverted, HG * a + HG)
                nc.vector.tensor_tensor(oT[:], xb[:, bank, 0:SC].rearrange("p (g n) -> p g n", n=TOK),
                                        rec[:].rearrange("p (g n) -> p g n", n=TOK), ALU.mult).then_inc(emptied[bank], 1)

            def residual(u, i, at):
                bank, c = at
                dve.wait_ge(filled[bank], c + 1)
                nc.vector.tensor_tensor(h2[u][0:ROWS, 2 * i:2 * i + 2, :],
                                        xb[0:ROWS, bank, 0:2 * D].rearrange("p (n d) -> p n d", n=2),
                                        resid[u][0:ROWS, 2 * i:2 * i + 2, :], ALU.add).then_inc(emptied[bank], 1)
                dve.wait_ge(emptied[bank], c + 1)
                dve.sem_inc(h_ready, 1)

            def pair(tt, u, first=False, more=True, more2=True):
                t = 2 * tt + u
                v = 1 - u
                splits = SPLIT0 + SPLITS * t
                for i in range(2):
                    nxt = 2 * t + i + 1
                    for q in range(4):
                        if i == 0 or more:
                            maximum(nxt, q)
                        if i == 1 and more2 and q == 0:
                            norm_in(tt + 1, u)
                        if q == 1:
                            if i == 1:
                                if not (isinstance(tt, int) and tt == 0):
                                    dve.wait_ge(h_out[u], 16 * tt)
                                dve.wait_ge(resid_ready, t + 1)
                                residual(u, 0, use(t, Y[1]))
                                if more2:
                                    norm_out(tt + 1, u, use(t, X[1]))
                            elif not first:
                                residual(v, 1, use(t, Y[0]))
                        if q == 2 and more:
                            if i == 0:
                                low_q(v, 0, use(t, Q[0]), splits + 1)
                                low_q(v, 1, use(t, Q[1]), splits + 2)
                            else:
                                values(v, 0, use(t, V[0]))
                    if i == 0 or more:
                        double(nxt)
                    if i == 0 and more:
                        low_q(v, 2, use(t, Q[2]), splits + 3)
                    if i == 0 or more:
                        low_max(use(t, MAX[i]), splits + (8 if i == 1 else 4 if more else 1))
                    if i == 1 and more:
                        values(v, 1, use(t, V[1]))
                    for g in range(HG):
                        invert(g, use(t, SUM[i]))
                        if i == 0 and more:
                            low_k(v, g, use(t, K_[g]), splits + 5 + g)
                    weigh(2 * t + i, use(t, MIX[i]))

            norm_in(0, 0)
            norm_out(0, 0, None)
            for g in range(HG):
                low_q(0, g, start(START["Q"][g]), g + 1)
            for g in range(HG):
                low_k(0, g, start(START["K"][g]), HG + g + 1)
            for i in range(2):
                values(0, i, start(START["V"][i]))
            for q in range(4):
                maximum(0, q)
            double(0)
            low_max(start(START["MAX"]), SPLIT0)
            norm_in(0, 1)
            norm_out(0, 1, start(START["X"][1]))
            pair(0, 0, first=True)
            pair(0, 1)
            with dve.Fori(1, PAIRS // 2 - 1) as tt:
                for u in range(2):
                    pair(tt, u)
            pair(PAIRS // 2 - 1, 0, more2=False)
            pair(PAIRS // 2 - 1, 1, more=False, more2=False)
            residual(1, 1, use(PAIRS, Y[0]))

        @block.scalar
        def _(act):
            act.wait_ge(const_in, CONSTS)

            def turned(i, at):
                bank, c = at
                rows = (D0, D1)[i]
                act.wait_ge(filled[bank], c + 1)
                nc.scalar.activation(xT[0:rows, i, :], xb[0:rows, bank, 0:PT], ACT.Copy).then_inc(emptied[bank], 1)

            def high(dst, at):
                bank, c = at
                act.wait_ge(filled[bank], c + 1)
                nc.scalar.activation(dst, xb[:, bank, 0:dst.shape[-1]], ACT.Copy).then_inc(split, 1)

            def sums(at):
                bank, c = at
                act.wait_ge(filled[bank], c + 1)
                nc.scalar.activation(total[:], xb[:, bank, 0:SC], ACT.Copy).then_inc(emptied[bank], 1)

            def expo(a, q):
                c, h = divmod(q, 2)
                act.wait_ge(by_key, 4 * a + q + 1)
                nc.scalar.activation(prT[0:ROWS, c, 6 * h:6 * h + 6, :].rearrange("p (j g) n -> p j (g n)", j=2),
                                     tp[0:ROWS, 2 * h:2 * h + 2, 0:SC], ACT.Exp, scale=SCALE).then_inc(exped, 1)

            def pair(tt, u, more=True):
                t = 2 * tt + u
                v = 1 - u
                for i in range(2):
                    for q in range(4):
                        expo(2 * t + i, q)
                        if i == 0 and more:
                            if q == 0:
                                for j in range(2):
                                    turned(j, use(t, X[j]))
                            if q == 2:
                                for g in range(2):
                                    high(qh[:, g, :], use(t, Q[g]))
                    if i == 0 and more:
                        high(qh[:, 2, :], use(t, Q[2]))
                    sums(use(t, SUM[i]))
                    if i == 0 or more:
                        high(mh[:], use(t, MAX[i]))
                    if i == 0 and more:
                        for g in range(HG):
                            high(k1[v][:, g, :], use(t, K_[g]))

            for i in range(2):
                turned(i, start(START["X"][i]))
            for g in range(HG):
                high(qh[:, g, :], start(START["Q"][g]))
            for g in range(HG):
                high(k1[0][:, g, :], start(START["K"][g]))
            high(mh[:], start(START["MAX"]))
            for u in range(2):
                pair(0, u)
            with act.Fori(1, PAIRS // 2 - 1) as tt:
                for u in range(2):
                    pair(tt, u)
            pair(PAIRS // 2 - 1, 0)
            pair(PAIRS // 2 - 1, 1, more=False)

        @block.tensor
        def _(pe):
            pe.wait_ge(const_in, CONSTS)
            pe.wait_ge(consts, 3)
            pe.wait_ge(ones_set, 2)

            def claim(at):
                bank, c = at
                if not (isinstance(c, int) and c == 0):
                    pe.wait_ge(emptied[bank], c)
                return bank

            def read(*at):
                for bank, c in at:
                    pe.wait_ge(emptied[bank], c + 1)

            def turn_x(t, i, at):
                d, rows = ((0, D0), (D0, D1))[i]
                if i == 0:
                    pe.wait_ge(xn_ready, t + 1)
                bank = claim(at)
                pe.sem_inc(pe_held, 1)
                for n in range(4):
                    last = nc.tensor.transpose(xb[0:rows, bank, n * ROWS:(n + 1) * ROWS],
                                               xn[0:ROWS, n, d:d + rows], ident[0:ROWS, 0:ROWS])
                last.then_inc(filled[bank], 1)

            def project(w, g, at):
                bank = claim(at)
                nc.tensor.matmul(xb[:, bank, 0:PT], w[0:D0, 0, g, :], xT[0:D0, 0, :], start=True, stop=False)
                nc.tensor.matmul(xb[:, bank, 0:PT], w[0:D1 + 1, 1, g, :], xT[0:D1 + 1, 1, :],
                                 start=False, stop=True).then_inc(filled[bank], 1)

            def values(i, at):
                bank = claim(at)
                for n in range(2):
                    cols = slice((2 * i + n) * ROWS, (2 * i + n + 1) * ROWS)
                    y = xb[0:ROWS, bank, n * D:(n + 1) * D]
                    nc.tensor.matmul(y, xT[0:D0, 0, cols], wv[0:D0, 0, :], start=True, stop=False)
                    last = nc.tensor.matmul(y, xT[0:D1 + 1, 1, cols], wv[0:D1 + 1, 1, :], start=False, stop=True)
                last.then_inc(filled[bank], 1)

            def queries_scores(a, u, i, q, first=False):
                n, h = divmod(q, 2)
                if not (first and q == 0):
                    pe.wait_ge(maxed, 4 * a + q)
                for j in range(2):
                    nc.tensor.matmul(sc[0:ROWS, j, 0:SC], identb[0:ROWS, 0:ROWS], maskb[0:ROWS, n, :],
                                     start=True, stop=False)
                for g in range(HG):
                    for k in (k1[u], k2[u]):
                        for j in range(2):
                            r = slice(64 * h + 32 * j, 64 * h + 32 * j + 32)
                            last = nc.tensor.matmul(sc[0:ROWS, j, g * TOK:(g + 1) * TOK],
                                                    q1[u][r, g, i * TOK + n * ROWS:i * TOK + (n + 1) * ROWS],
                                                    k[r, g, i * TOK:(i + 1) * TOK],
                                                    start=False, stop=(g == HG - 1 and k is k2[u]))
                last.then_inc(by_query, 1)

            def keys_scores(a, u, i, q, first=False):
                c, h = divmod(q, 2)
                if not (first and q < 2):
                    pe.wait_ge(exped, 4 * a + q - 1)
                for j in range(2):
                    nc.tensor.matmul(tp[0:ROWS, 2 * h + j, 0:SC], identb[0:ROWS, 0:ROWS], maskb[0:ROWS, c, :],
                                     start=True, stop=False)
                for g in range(HG):
                    for k in (k1[u], k2[u], None):
                        for j in range(2):
                            r = slice(64 * h + 32 * j, 64 * h + 32 * j + 32)
                            left = (pickr[r, g, :] if k is None else
                                    k[r, g, i * TOK + c * ROWS:i * TOK + (c + 1) * ROWS])
                            right = mT[r, :] if k is None else q1[u][r, g, i * TOK:(i + 1) * TOK]
                            last = nc.tensor.matmul(tp[0:ROWS, 2 * h + j, g * TOK:(g + 1) * TOK], left, right,
                                                    start=False, stop=(g == HG - 1 and k is None))
                last.then_inc(by_key, 1)

            def turn_max(a, at):
                bank = claim(at)
                pe.wait_ge(doubled, a + 1)
                for n in range(2):
                    last = nc.tensor.transpose(xb[:, bank, n * ROWS:(n + 1) * ROWS],
                                               mx[0:ROWS, n, :, :].rearrange("p j g -> p (j g)"),
                                               ident[0:ROWS, 0:ROWS])
                last.then_inc(filled[bank], 1)

            def mix(u, i, at, sums):
                bank = claim(at)
                for g in range(HG):
                    for c in range(2):
                        for j in range(4):
                            left = ones[0:ROWS, :] if sums else va[u][0:ROWS, 2 * i + c, 4 * g + j, :]
                            last = nc.tensor.matmul(xb[32 * j:32 * j + 32, bank, g * TOK:(g + 1) * TOK], left,
                                                    prT[0:ROWS, c, HG * j + g, :], start=(c == 0), stop=(c == 1))
                last.then_inc(filled[bank], 1)

            def project_out(at, mixed):
                bank = claim(at)
                read(mixed)
                for n in range(2):
                    for g in range(HG):
                        last = nc.tensor.matmul(xb[0:ROWS, bank, n * D:(n + 1) * D], oT[:, g, n * ROWS:(n + 1) * ROWS],
                                                wo[:, g, :], start=(g == 0), stop=(g == HG - 1))
                last.then_inc(filled[bank], 1)

            def pair(tt, u, first=False, more=True):
                t = 2 * tt + u
                v = 1 - u
                for i in range(2):
                    a = 2 * t + i
                    w = u if i == 0 else v
                    nxt = i == 0 or more
                    for q in range(4):
                        if q == 0:
                            read(use(t, MAX[0]) if i == 1 else start(START["MAX"]) if first else use(t - 1, MAX[1]))
                            if i == 1 and more:
                                read(use(t, K_[1]), use(t, K_[2]))
                        keys_scores(a, u, i, q, first and i == 0)
                        if nxt:
                            queries_scores(a + 1, w, 1 - i, q)
                        if i == 0 and more and q == 0:
                            for j in range(2):
                                turn_x(t + 1, j, use(t, X[j]))
                        if q == 1:
                            if i == 1:
                                project_out(use(t, Y[1]), use(t, MIX[0]))
                            elif not first:
                                project_out(use(t, Y[0]), use(t - 1, MIX[1]))
                        if q == 2 and more:
                            if i == 0:
                                read(use(t, X[0]), use(t, X[1]))
                                for g in range(2):
                                    project(wq, g, use(t, Q[g]))
                            else:
                                values(0, use(t, V[0]))
                    if i == 0 and more:
                        project(wq, 2, use(t, Q[2]))
                    pe.wait_ge(exped, 4 * a + 4)
                    mix(u, i, use(t, SUM[i]), True)
                    if nxt:
                        turn_max(a + 1, use(t, MAX[i]))
                    if more:
                        if i == 0:
                            for g in range(HG):
                                project(wk, g, use(t, K_[g]))
                        else:
                            values(1, use(t, V[1]))
                    if i == 0:
                        read(*(start(START["V"][j]) if first else use(t - 1, V[j]) for j in range(2)))
                    mix(u, i, use(t, MIX[i]), False)

            for j in range(2):
                turn_x(0, j, start(START["X"][j]))
            read(*(start(START["X"][j]) for j in range(2)))
            for g in range(HG):
                project(wq, g, start(START["Q"][g]))
            for g in range(HG):
                project(wk, g, start(START["K"][g]))
            for i in range(2):
                values(i, start(START["V"][i]))
            read(start(START["K"][1]), start(START["K"][2]))
            for q in range(4):
                queries_scores(0, 0, 0, q, True)
            turn_max(0, start(START["MAX"]))
            pair(0, 0, first=True)
            pair(0, 1)
            with pe.Fori(1, PAIRS // 2 - 1) as tt:
                for u in range(2):
                    pair(tt, u)
            pair(PAIRS // 2 - 1, 0)
            pair(PAIRS // 2 - 1, 1, more=False)
            project_out(use(PAIRS, Y[0]), use(PAIRS - 1, MIX[1]))


class Spline:

    def __init__(self, nc, sb, sem, name, cols):
        self.nc, self.cols = nc, cols
        self.s, self.t, self.a, self.a2, self.b, self.b2 = (
            sb(f"{name}_{k}", [P, cols]) for k in ("s", "t", "a", "a2", "b", "b2"))
        self.n = [sb(f"{name}_n{u}", [P, cols]) for u in range(2)]
        self.v = [sb(f"{name}_v{u}", [P, cols]) for u in range(2)]
        self.f = [sb(f"{name}_f{i}", [P, cols]) for i in range(4)]
        (self.s_ready, self.n_ready, self.z_ready, self.t_ready, self.a_ready, self.a2_ready, self.b_ready,
         self.b2_ready, self.a3_ready, self.b3_ready, self.v_ready, self.f_ready, self.f_used) = (
            sem(f"{name}_{k}") for k in ("s_ready", "n_ready", "z_ready", "t_ready", "a_ready", "a2_ready", "b_ready",
                                         "b2_ready", "a3_ready", "b3_ready", "v_ready", "f_ready", "f_used"))

        self.held = sem(f"{name}_pool_held")

    def round_act(self, act, k, u, first, parts):
        act.wait_ge(self.s_ready, parts * (k + 1))
        if not first:
            act.wait_ge(self.f_ready, 4 * (k - 1))
        self.nc.scalar.activation(self.n[u][:], self.s[:], ACT.Copy, bias=MAGIC).then_inc(self.n_ready, 1)

    def powers_act(self, act, k, first):
        act.wait_ge(self.z_ready, k + 1)
        if not first:
            act.wait_ge(self.a_ready, k)
        self.nc.scalar.activation(self.t[:], self.s[:], ACT.Abs, scale=4.0).then_inc(self.t_ready, 1)
        act.wait_ge(self.t_ready, k + 1)
        if not first:
            act.wait_ge(self.v_ready, k)
        self.nc.scalar.activation(self.b[:], self.t[:], ACT.Relu, bias=1.0, scale=-1.0).then_inc(self.b_ready, 1)
        self.nc.scalar.activation(self.a2[:], self.t[:], ACT.Square, bias=2.0, scale=-1.0).then_inc(self.a2_ready, 1)
        act.wait_ge(self.b_ready, k + 1)
        self.nc.scalar.activation(self.b2[:], self.b[:], ACT.Square, scale=2.0).then_inc(self.b2_ready, 1)

    def cube_pool(self, pool, k, first):
        if not first:
            pool.wait_ge(self.a3_ready, k)
        pool.wait_ge(self.t_ready, k + 1)
        pool.sem_inc(self.held, 1)
        pool.tensor_scalar(self.a[:], self.t[:], -1.0, 2.0, ALU.mult, ALU.add).then_inc(self.a_ready, 1)
        pool.wait_ge(self.b2_ready, k + 1)
        pool.tensor_tensor(self.b2[:], self.b2[:], self.b[:], ALU.mult).then_inc(self.b3_ready, 1)

    def center_dve(self, dve, k, u):
        dve.wait_ge(self.n_ready, k + 1)
        self.nc.vector.scalar_tensor_tensor(self.s[:], self.n[u][:], MAGIC, self.s[:], ALU.subtract,
                                            ALU.subtract).then_inc(self.z_ready, 1)

    def cube_dve(self, dve, k):
        dve.wait_ge(self.a_ready, k + 1)
        dve.wait_ge(self.a2_ready, k + 1)
        self.nc.vector.tensor_tensor(self.a2[:], self.a2[:], self.a[:], ALU.mult).then_inc(self.a3_ready, 1)

    def value_dve(self, dve, k, u):
        dve.wait_ge(self.b3_ready, k + 1)
        dve.wait_ge(self.a3_ready, k + 1)
        self.nc.vector.tensor_tensor(self.v[u][:], self.a2[:], self.b2[:], ALU.subtract).then_inc(self.v_ready, 1)

    def take_dve(self, dve, k, u, i, first):
        if i == 0:
            dve.wait_ge(self.v_ready, k + 1)
        if not first:
            dve.wait_ge(self.f_used, 4 * k + i - 3)
        self.nc.vector.scalar_tensor_tensor(self.f[i][:], self.n[u][:], MAGIC + i, self.v[u][:], ALU.is_equal,
                                            ALU.mult).then_inc(self.f_ready, 1)


def spline1_phase(nc, a, h_scr, hid_scr):
    SETS = 6
    W2X = 2 * D0
    MC = HID // P
    COLS = SETS * PT
    HALF = SETS // 2
    HC = HALF * PT
    HALVES = 8
    RING = 4
    with ExitStack() as stack:
        sb, ps, sem = memories(nc, stack)
        w_high, w_low = (sb(f"spline1_weights_{k}", [P, HALVES, HALF * HID], F32R) for k in ("high", "low"))
        s, b2, a_ = (sb(f"spline1_{k}", [P, COLS]) for k in ("s", "b2", "a"))
        n_ = [sb(f"spline1_n{u}", [P, COLS]) for u in range(2)]
        a2 = [sb(f"spline1_a2_{u}", [P, COLS]) for u in range(2)]
        b_ = [sb(f"spline1_b{u}", [P, COLS]) for u in range(2)]
        f = [sb(f"spline1_f{i}", [P, 2, HC], F32R) for i in range(RING)]
        stage = [y[:, 0:HALF * HID] for y in (n_[1], a2[1], b_[1])]
        bias = sb("spline1_offset", [P, SETS])
        ident = sb("spline1_identity", [P, P])
        minus_half = sb("spline1_half", [P, 4])
        x = sb("spline1_x", [P, 4, D])
        xn = sb("spline1_xn", [P, 4, W2X])
        stats, mv = sb("spline1_stats", [P, 4, 6]), sb("spline1_mv", [P, 4, 2])
        ve, rstd, tmp = (sb(f"spline1_{k}", [P, 4]) for k in ("ve", "rstd", "tmp"))
        hid = [sb(f"spline1_hid{u}", [P, PT]) for u in range(3)]
        acc = ps("spline1_acc", [P, MC, 512])
        xT = ps("spline1_xT", [P, 2, 512])
        dve_held, pool_held = sem("spline1_dve_held"), sem("spline1_pool_held")
        const_in, half_set = sem("spline1_const_in"), sem("spline1_half_set")
        w_in = [sem(f"spline1_w_in{i}") for i in range(3)]
        w_high_ready, w_low_ready = sem("spline1_w_high"), sem("spline1_w_low")
        x_in = sem("spline1_x_in")
        ln, pow_done, xn_ready, twice = (sem(f"spline1_{k}") for k in ("ln", "pow", "xn_ready", "twice"))
        xT_ready = sem("spline1_xT_ready")
        s_ready, n_ready, z_ready, t_ready = (sem(f"spline1_{k}") for k in ("s_ready", "n_ready", "z_ready", "t_ready"))
        a_ready, b_ready, a2_ready, b2_ready = (sem(f"spline1_{k}") for k in ("a_ready", "b_ready", "a2_ready", "b2_ready"))
        a3_ready, b3_ready, v_ready = (sem(f"spline1_{k}") for k in ("a3_ready", "b3_ready", "v_ready"))
        high_ready, low_ready = sem("spline1_high_ready"), sem("spline1_low_ready")
        f_ready, f_used = sem("spline1_f_ready"), sem("spline1_f_used")
        summed = sem("spline1_summed")
        emptied = sem("spline1_emptied")
        hid_out = [sem(f"spline1_hid_out{u}") for u in range(3)]
        block = stack.enter_context(nc.Block())

        @block.sync
        def _(sp):
            sp.dma_start(ident[:], a["identity"]).then_inc(const_in, 16)
            sp.dma_start(bias[:], a["spline1_bias"]).then_inc(const_in, 16)

            def load(t):
                sp.dma_start(x[0:ROWS], h_scr[bass.ds(t * PT, PT), :].rearrange("(n p) d -> p n d", p=ROWS)
                             ).then_inc(x_in, 16)

            def reload(t):
                sp.wait_ge(xn_ready, t)
                load(t)

            def leave(t):
                for m in range(MC):
                    sp.wait_ge(emptied, MC * t + m + 1)
                    sp.dma_start(hid_scr[:, m, bass.ds(t * PT, PT)], hid[m % 3][:]).then_inc(hid_out[m % 3], 16)

            weights = a["w1"].rearrange("p i (h r) o -> p (i h) (r o)", h=2)
            load(0)
            for j in range(HALVES):
                if j >= 3:
                    sp.wait_ge(w_low_ready, j - 2)
                sp.dma_start(stage[j % 3], weights[:, j, :]).then_inc(w_in[j % 3], 16)
                if j == 1:
                    reload(1)
            reload(2)
            with sp.Fori(0, PAIRS - 3) as t:
                reload(t + 3)
                leave(t)
            for t in range(PAIRS - 3, PAIRS):
                leave(t)
            for u in range(3):
                sp.wait_ge(hid_out[u], 16 * PAIRS * (2 if u == 0 else 1))

        @block.gpsimd
        def _(pool):
            pool.memset(minus_half[:, :], -0.5).then_inc(half_set, 1)
            pool.wait_ge(half_set, 1)

            def power(t):
                pool.wait_ge(ln, LN_STEPS * t + LN_VAR)
                pool.tensor_tensor(rstd[0:ROWS, :], ve[0:ROWS, :], minus_half[0:ROWS, :], ALU.pow).then_inc(pow_done, 1)

            def double(t):
                pool.wait_ge(xn_ready, t + 1)
                pool.sem_inc(pool_held, 1)
                pool.tensor_copy(xn[0:ROWS, :, D:W2X], xn[0:ROWS, :, D0:D]).then_inc(twice, 1)

            def cube(k, u, first=False):
                if not first:
                    pool.wait_ge(high_ready, k)
                    pool.wait_ge(low_ready, k)
                pool.wait_ge(t_ready, k + 1)
                pool.sem_inc(pool_held, 1)
                pool.tensor_scalar(a_[:], s[:], -1.0, 2.0, ALU.mult, ALU.add).then_inc(a_ready, 1)
                pool.wait_ge(b2_ready, k + 1)
                pool.tensor_tensor(b2[:], b2[:], b_[u][:], ALU.mult).then_inc(b3_ready, 1)

            power(0)
            double(0)
            power(1)
            double(1)
            cube(0, 0, True)
            with pool.Fori(0, PAIRS // 2 - 1) as tt:
                for u in range(2):
                    power(2 * tt + u + 2)
                    double(2 * tt + u + 2)
                    cube(2 * tt + u + 1, 1 - u)
            cube(PAIRS - 1, 1)

        @block.vector
        def _(dve):
            dve.wait_ge(const_in, 32)

            def norm_in(t):
                dve.wait_ge(x_in, 16 * t + 16)
                layer_stats(nc, dve, Step(dve, ln, LN_STEPS * t), dve_held, x, stats, mv, ve)

            def norm_out(t, first=False):
                if not first:
                    dve.wait_ge(xT_ready, t)
                layer_rest(nc, dve, Step(dve, ln, LN_STEPS * t), pow_done, t + 1, x, xn, mv, ve, rstd,
                           tmp).then_inc(xn_ready, 1)

            def center(k, u):
                dve.wait_ge(n_ready, k + 1)
                nc.vector.scalar_tensor_tensor(s[:], n_[u][:], MAGIC, s[:], ALU.subtract, ALU.subtract).then_inc(z_ready, 1)

            def cube(k, u):
                dve.wait_ge(a_ready, k + 1)
                dve.wait_ge(a2_ready, k + 1)
                nc.vector.tensor_tensor(a2[u][:], a2[u][:], a_[:], ALU.mult).then_inc(a3_ready, 1)

            def value(k, u):
                dve.wait_ge(b3_ready, k + 1)
                dve.wait_ge(a3_ready, k + 1)
                nc.vector.tensor_tensor(a_[:], a2[u][:], b2[:], ALU.subtract).then_inc(v_ready, 1)

            def low(k, u):
                dve.wait_ge(high_ready, k + 1)
                nc.vector.tensor_tensor(b_[u][:].bitcast(F32R), a_[:], a2[u][:], ALU.subtract).then_inc(low_ready, 1)

            def weight_low(j):
                dve.wait_ge(w_high_ready, j + 1)
                nc.vector.tensor_tensor(w_low[:, j, :], stage[j % 3], w_high[:, j, :].bitcast(F32),
                                        ALU.subtract).then_inc(w_low_ready, 1)

            def take(k, u, j, first):
                i, half = divmod(j, 2)
                cols = slice(half * HC, (half + 1) * HC)
                if j == 0:
                    dve.wait_ge(low_ready, k + 1)
                if not (first and j < RING):
                    dve.wait_ge(f_used, HALVES * k + j - RING + 1)
                for part, v in enumerate((a2[u], b_[u])):
                    nc.vector.scalar_tensor_tensor(f[j % RING][:, part, :], n_[u][:, cols], MAGIC + i, v[:, cols],
                                                   ALU.is_equal, ALU.mult).then_inc(f_ready, 1)

            def tile(tt, u, first=False, more=True, more2=True):
                k, v = 2 * tt + u, 1 - u
                for j in range(HALVES):
                    last = first and j == HALVES - 1
                    if first:
                        weight_low(j)
                    take(k, u, j, first)
                    if more and (last or j == 0 and not first):
                        center(k + 1, v)
                    if more2 and (last or j == 1 and not first):
                        norm_in(k + 2)
                    if more2 and (last or j == 2 and not first):
                        norm_out(k + 2)
                    if more and (last or j == 4 and not first):
                        cube(k + 1, v)
                    if more and (last or j == 5 and not first):
                        value(k + 1, v)
                    if more and (last or j == 6 and not first):
                        low(k + 1, v)

            norm_in(0)
            norm_out(0, True)
            norm_in(1)
            norm_out(1)
            center(0, 0)
            cube(0, 0)
            value(0, 0)
            low(0, 0)
            tile(0, 0, True)
            tile(0, 1)
            with dve.Fori(1, PAIRS // 2 - 1) as tt:
                for u in range(2):
                    tile(tt, u)
            tile(PAIRS // 2 - 1, 0, more2=False)
            tile(PAIRS // 2 - 1, 1, more=False, more2=False)

        @block.scalar
        def _(act):
            act.wait_ge(const_in, 32)

            def basis(k, u, first=False, second=False):
                act.wait_ge(xT_ready, k + 1)
                if not first:
                    act.wait_ge(a_ready, k)
                for r in range(SETS):
                    nc.scalar.activation(s[:, r * PT:(r + 1) * PT], xT[:, r // 4, 0:PT], ACT.Identity,
                                         bias=bias[:, r:r + 1], scale=SPL_SCALE).then_inc(s_ready, 1)
                act.wait_ge(s_ready, SETS * (k + 1))
                if not (first or second):
                    act.wait_ge(f_ready, 2 * HALVES * (k - 1))
                nc.scalar.activation(n_[u][:], s[:], ACT.Copy, bias=MAGIC).then_inc(n_ready, 1)
                act.wait_ge(z_ready, k + 1)
                nc.scalar.activation(s[:], s[:], ACT.Abs, scale=4.0).then_inc(t_ready, 1)
                act.wait_ge(t_ready, k + 1)
                nc.scalar.activation(b_[u][:], s[:], ACT.Relu, bias=1.0, scale=-1.0).then_inc(b_ready, 1)
                nc.scalar.activation(a2[u][:], s[:], ACT.Square, bias=2.0, scale=-1.0).then_inc(a2_ready, 1)
                act.wait_ge(b_ready, k + 1)
                if not first:
                    act.wait_ge(v_ready, k)
                nc.scalar.activation(b2[:], b_[u][:], ACT.Square, scale=2.0).then_inc(b2_ready, 1)

            def high(k, u):
                act.wait_ge(v_ready, k + 1)
                nc.scalar.activation(a2[u][:].bitcast(F32R), a_[:], ACT.Copy).then_inc(high_ready, 1)

            def weight_high(j):
                act.wait_ge(w_in[j % 3], 16 * (j // 3) + 16)
                nc.scalar.activation(w_high[:, j, :], stage[j % 3], ACT.Copy).then_inc(w_high_ready, 1)

            def empty(t, first=False):
                for m in range(MC):
                    if m < MC - 1:
                        act.wait_ge(summed, (MC - 1) * t + m + 1)
                    else:
                        act.wait_ge(f_used, HALVES * t + HALVES)
                    if not (first and m < 3):
                        act.wait_ge(hid_out[m % 3], 16 * (2 * t + m // 3 if m % 3 == 0 else t))
                    nc.scalar.activation(hid[m % 3][:], acc[:, m, 0:PT], ACT.Copy, scale=1.0 / 6.0).then_inc(emptied, 1)

            basis(0, 0, True)
            for j in range(HALVES):
                weight_high(j)
                if j == 1:
                    high(0, 0)
            act.wait_ge(w_low_ready, HALVES)
            basis(1, 1, second=True)
            high(1, 1)

            def tile(tt, u, first=False):
                k = 2 * tt + u
                basis(k, u)
                empty(k - 2, first)
                high(k, u)

            tile(1, 0, True)
            tile(1, 1)
            with act.Fori(2, PAIRS // 2) as tt:
                for u in range(2):
                    tile(tt, u)
            empty(PAIRS - 2)
            empty(PAIRS - 1)

        @block.tensor
        def _(pe):
            def turn(t, first=False):
                pe.wait_ge(xn_ready, t + 1)
                pe.wait_ge(twice, t + 1)
                if not first:
                    pe.wait_ge(s_ready, SETS * t)
                for i in range(2):
                    for n in range(4):
                        last = nc.tensor.transpose(xT[:, i, n * ROWS:(n + 1) * ROWS],
                                                   xn[0:ROWS, n, i * D0:(i + 1) * D0], ident[0:ROWS, 0:ROWS])
                last.then_inc(xT_ready, 1)

            def layer(k, first=False, more=True):
                for j in range(HALVES):
                    if first:
                        pe.wait_ge(w_low_ready, j + 1)
                    pe.wait_ge(f_ready, 2 * (HALVES * k + j) + 2)
                    for r in range(HALF):
                        for m in range(MC):
                            start, stop = j == 0 and r == 0, j == HALVES - 1 and r == HALF - 1
                            if start and not first:
                                pe.wait_ge(emptied, MC * (k - 1) + m + 1)
                            at = r * HID + m * P
                            high, low = w_high[:, j, at:at + P], w_low[:, j, at:at + P]
                            v_high, v_low = (f[j % RING][:, part, r * PT:(r + 1) * PT] for part in range(2))
                            y = acc[:, m, 0:PT]
                            nc.tensor.matmul(y, high, v_high, start=start, stop=False)
                            nc.tensor.matmul(y, high, v_low, start=False, stop=False)
                            last = nc.tensor.matmul(y, low, v_high, start=False, stop=stop)
                            if stop and m < MC - 1:
                                last.then_inc(summed, 1)
                    last.then_inc(f_used, 1)
                    if j == (HALVES - 1 if first else 1) and more:
                        turn(k + 2)

            pe.wait_ge(const_in, 32)
            turn(0, True)
            turn(1)
            layer(0, True)
            with pe.Fori(1, PAIRS - 2) as k:
                layer(k)
            layer(PAIRS - 2, more=False)
            layer(PAIRS - 1, more=False)


def spline2_phase(nc, a, h_scr, hid_scr, out):
    CH = HID // P
    SETS = 4 * CH
    with ExitStack() as stack:
        sb, ps, sem = memories(nc, stack)
        spl = Spline(nc, sb, sem, "spline2", SETS * P)
        w = sb("spline2_weights", [P, 4, SETS, D])
        bias = sb("spline2_offset", [P, 4])
        x = [sb(f"spline2_x{u}", [P, CH, P]) for u in range(2)]
        h = [sb(f"spline2_h{u}", [P, D]) for u in range(2)]
        y = [sb(f"spline2_y{u}", [P, D]) for u in range(2)]
        acc = ps("spline2_acc", [P, 2, 512])
        const_in, w_in = sem("spline2_const_in"), sem("spline2_w_in")
        x_in = [sem(f"spline2_x_in{u}") for u in range(2)]
        h_in = [sem(f"spline2_h_in{u}") for u in range(2)]
        y_ready = sem("spline2_y_ready")
        y_out = [sem(f"spline2_y_out{u}") for u in range(2)]
        block = stack.enter_context(nc.Block())

        @block.sync
        def _(sp):
            sp.dma_start(bias[:], a["spline2_bias"]).then_inc(const_in, 16)

            def load_h(t, u):
                sp.dma_start(h[u][:], h_scr[bass.ds(t * P, P), :]).then_inc(h_in[u], 16)

            def tile(k, u, more=True):
                sp.wait_ge(y_ready, k + 1)
                sp.dma_start(out[bass.ds(k * P, P), :], y[u][:]).then_inc(y_out[u], 16)
                if more:
                    load_h(k + 2, u)

            load_h(0, 0)
            load_h(1, 1)
            for i in range(4):
                if i > 0:
                    sp.wait_ge(w_in, 16 * i)
                sp.dma_start(w[:, i], a["w2"][:, i]).then_inc(w_in, 16)
            tile(0, 0)
            with sp.Fori(0, OT // 2 - 1) as tt:
                tile(2 * tt + 1, 1)
                tile(2 * tt + 2, 0)
            tile(OT - 2, 1, False)
            tile(OT - 1, 0, False)
            sp.wait_ge(y_out[0], 16 * (OT // 2 + 1))
            sp.wait_ge(y_out[1], 16 * (OT // 2))

        @block.gpsimd
        def _(pool):
            spl.cube_pool(pool, 0, True)
            with pool.Fori(1, OT) as k:
                spl.cube_pool(pool, k, False)

        @block.scalar
        def _(act):
            act.wait_ge(const_in, 16)

            def load_x(t, u):
                act.dma_start(x[u][:], hid_scr[:, :, bass.ds(t * P, P)]).then_inc(x_in[u], 16)

            def basis(tt, k, u, first=False, second=False, more=True):
                act.wait_ge(x_in[u], 16 * tt + 16)
                for r in range(4):
                    nc.scalar.activation(spl.s[:, r * HID:(r + 1) * HID].rearrange("p (c n) -> p c n", c=CH), x[u][:],
                                         ACT.Identity, bias=bias[:, r:r + 1], scale=SPL_SCALE).then_inc(spl.s_ready, 1)
                spl.round_act(act, k, u, first or second, 4)
                if more:
                    load_x(k + 2, u)
                spl.powers_act(act, k, first)

            load_x(0, 0)
            load_x(1, 1)
            basis(0, 0, 0, True)
            basis(0, 1, 1, False, True)
            with act.Fori(1, OT // 2 - 1) as tt:
                basis(tt, 2 * tt, 0)
                basis(tt, 2 * tt + 1, 1)
            basis(OT // 2 - 1, OT - 3, 0)
            basis(OT // 2 - 1, OT - 2, 1, more=False)
            basis(OT // 2, OT - 1, 0, more=False)

        @block.vector
        def _(dve):
            def tile(tt, k, u, first=False, more=True, early=False):
                v = 1 - u
                spl.take_dve(dve, k, u, 0, first)
                if more:
                    spl.center_dve(dve, k + 1, v)
                spl.take_dve(dve, k, u, 1, first)
                spl.take_dve(dve, k, u, 2, first)
                if more:
                    spl.cube_dve(dve, k + 1)
                spl.take_dve(dve, k, u, 3, first)
                if more:
                    spl.value_dve(dve, k + 1, v)
                if not first:
                    leave(tt - 1 if u == 0 else tt, k - 1, v, early)

            def leave(tt, k, u, early):
                dve.wait_ge(spl.f_used, 4 * k + 4)
                dve.wait_ge(h_in[u], 16 * tt + 16)
                if not early:
                    dve.wait_ge(y_out[u], 16 * tt)
                nc.vector.scalar_tensor_tensor(y[u][:], acc[:, u, 0:D], 1.0 / 6.0, h[u][:], ALU.mult,
                                               ALU.add).then_inc(y_ready, 1)

            spl.center_dve(dve, 0, 0)
            spl.cube_dve(dve, 0)
            spl.value_dve(dve, 0, 0)
            tile(0, 0, 0, True)
            tile(0, 1, 1, early=True)
            tile(1, 2, 0, early=True)
            with dve.Fori(1, OT // 2 - 1) as tt:
                tile(tt, 2 * tt + 1, 1)
                tile(tt + 1, 2 * tt + 2, 0)
            tile(OT // 2 - 1, OT - 2, 1)
            tile(OT // 2, OT - 1, 0, more=False)
            leave(OT // 2, OT - 1, 0, False)

        @block.tensor
        def _(pe):
            def layer(k, u, first=False):
                for i in range(4):
                    if isinstance(k, int) and k == 0:
                        pe.wait_ge(w_in, 16 * i + 16)
                    pe.wait_ge(spl.f_ready, 4 * k + i + 1)
                    if i == 0 and not first:
                        pe.wait_ge(y_ready, k - 1)
                    for r in range(SETS):
                        last = nc.tensor.matmul(acc[:, u, 0:D], spl.f[i][:, r * P:(r + 1) * P], w[:, i, r, :],
                                                start=(i == 0 and r == 0), stop=(i == 3 and r == SETS - 1))
                    last.then_inc(spl.f_used, 1)

            layer(0, 0, True)
            layer(1, 1, True)
            with pe.Fori(1, OT // 2) as tt:
                layer(2 * tt, 0)
                layer(2 * tt + 1, 1)
            layer(OT - 1, 0)


def program(nc, a, out):
    def scratch(name, *shape):
        return nc.dram_tensor(name, shape, F32, kind="Internal").ap()

    txt_scr = scratch("txt_scr", B * TXT, D)
    pos_scr = scratch("pos_scr", B, 2 * SAMPLES)
    pix_scr = scratch("pix_scr", B, PIXC, PIX)
    vis_scr = scratch("vis_scr", B * VIS, D)
    h_scr = scratch("h_scr", ALL, D)
    tokens(nc, a, txt_scr, pos_scr, pix_scr, vis_scr)
    attend_phase(nc, a, vis_scr, txt_scr, h_scr)
    hid_scr = scratch("hid_scr", P, HID // P, ALL)
    spline1_phase(nc, a, h_scr, hid_scr)
    spline2_phase(nc, a, h_scr, hid_scr, out.rearrange("b n d -> (b n) d"))


def tokens(nc, a, txt_scr, pos_scr, pix_scr, vis_scr):
    with ExitStack() as stack:
        hT_all = memories(nc, stack)[0]("stem_by_channel", [P, B * PIX])
        stem_phase(nc, a["patches"], a["stem_w"], a["stem_vec"], hT_all, pix_scr,
                   a["txt_idx"], a["table"], txt_scr)
        offset_phase(nc, a["off_w"], a["off_bias"], a["off_grid"], hT_all, pos_scr)
    with ExitStack() as stack:
        samp_all = memories(nc, stack)[0]("samples", [P, TAPS, B * VIS])
        sample_phase(nc, pos_scr, a["pix_neg"], pix_scr, samp_all)
        deform_phase(nc, a["dcn_w"], a["dcn_vec"], samp_all, vis_scr)


def layouts(i):
    import numpy as np

    f32 = np.float32

    def rep(*v):
        v = np.stack([np.asarray(x) for x in v])
        return np.broadcast_to(v[None], (P,) + v.shape)

    x = np.asarray(i["x"])
    tap = np.arange(TAPS)
    at = np.arange(HO) * K
    grid = np.zeros((TAPS, 2, HO, HO), f32)
    grid[:, 0] = at[None, :, None] + (tap // K)[:, None, None]
    grid[:, 1] = at[None, None, :] + (tap % K)[:, None, None]
    p = np.arange(PIXC)

    def chunks(w):
        r = np.zeros((P, 2) + w.shape[1:], w.dtype)
        r[:, 0], r[0:D1, 1] = w[0:D0], w[D0:D]
        return r

    def heads(w):
        w = w.reshape(w.shape[:-1] + (HG, 4, DH))
        return np.concatenate([w, w], -1).reshape(w.shape[:-3] + (HG, P))

    def biased(w, b):
        r = chunks(w)
        r[D1, 1] = b
        return r

    w = {k: np.asarray(v) for k, v in i.items() if k.startswith("L0_attn")}
    dist = np.abs(np.arange(P)[:, None, None] + ROWS * np.arange(2)[:, None] - np.arange(TOK))
    wo = np.zeros((4, 32, HG, D), f32)
    wo[:, 0:DH] = w["L0_attn_Wo"].reshape(HG, 4, DH, D).transpose(1, 2, 0, 3)
    row, group = np.arange(P)[:, None], np.arange(HG)[None]
    w1 = np.asarray(i["L0_ffn_w1"]).reshape(HID, D, 4, 4).transpose(1, 2, 3, 0)
    w1t = np.empty((P, 4, 6, HID), f32)
    w1t[:, :, 0:4] = w1[0:D0]
    w1t[0:D1, :, 4:6], w1t[D1:P, :, 4:6] = w1[D0:D, :, 0:2], w1[D0:D, :, 2:4]
    w2t = np.asarray(i["L0_ffn_w2"]).reshape(D, HID // P, P, 4, 4).transpose(2, 3, 4, 1, 0).reshape(P, 4, 16, D)
    r1 = np.tile(np.array([0, 1, 2, 3, 0, 1], f32), (P, 1))
    r1[D1:P, 4:6] += 2
    return {
        "w1": w1t,
        "w2": w2t,
        "spline1_bias": (SPL_BIAS - r1 / 4).astype(f32),
        "spline2_bias": np.tile((SPL_BIAS - np.arange(4) / 4).astype(f32), (P, 1)),
        "wq": biased(heads(w["L0_attn_Wq"]), heads(w["L0_attn_bq"])),
        "wk": biased(heads(w["L0_attn_Wk"]), heads(w["L0_attn_bk"])),
        "wv": biased(w["L0_attn_Wv"], w["L0_attn_bv"]),
        "wo": wo.reshape(P, HG, D),
        "bo": rep(w["L0_attn_bo"]),
        "pick": np.tile(-((row % 32 == group) | (row % 32 == HG + group)).astype(f32)[..., None], (1, 1, ROWS)),
        "minus_low": -np.concatenate([row % 32 >= DH, (row % 32 >= HG) & (row % 32 < 2 * HG)], 1).astype(f32),
        "identity": np.eye(P, dtype=f32),
        "mask": np.tile(np.where(dist <= 64, 0.0, NEG).astype(f32), (1, 1, 3)),
        "patches": x.reshape(B, 3, HS, K, HS, K).transpose(1, 3, 5, 0, 2, 4).reshape(PATCH, B, PIX),
        "stem_w": np.asarray(i["L0_tok_stem_w"]).reshape(C1, PATCH).T,
        "stem_vec": rep(i["L0_tok_stem_b"], i["L0_tok_bn1_g"], i["L0_tok_bn1_b"], i["L0_tok_bn1_m"], i["L0_tok_bn1_v"]),
        "txt_idx": np.asarray(i["x_txt"]).T,
        "table": np.asarray(i["L0_txt_weight"]),
        "off_w": np.asarray(i["L0_tok_off_w"]).reshape(2 * TAPS, C1, TAPS).transpose(1, 2, 0),
        "off_bias": np.asarray(i["L0_tok_off_b"])[:, None],
        "off_grid": np.tile(grid.reshape(2 * TAPS, VIS), (1, 8)),
        "pix_neg": -np.concatenate([(p // HS)[:, None] + 4 * np.arange(NPIXC)[None], (p % HS)[:, None]], 1).astype(f32),
        "dcn_w": np.asarray(i["L0_tok_dcn_w"]).reshape(D, C1, TAPS).transpose(1, 2, 0),
        "dcn_vec": rep(i["L0_tok_dcn_b"], i["L0_tok_bn2_g"], i["L0_tok_bn2_b"], i["L0_tok_bn2_m"], i["L0_tok_bn2_v"]),
    }


def kernel(**inputs):
    import numpy as np
    import concourse.bacc as bacc
    from concourse.bass_utils import run_bass_kernel_spmd

    nc = bacc.Bacc("TRN2", target_bir_lowering=False, num_devices=1)
    arrays = {k: np.ascontiguousarray(v) for k, v in layouts(inputs).items()}
    aps = {k: nc.dram_tensor(k, v.shape, mybir.dt.from_np(v.dtype), kind="ExternalInput").ap()
           for k, v in arrays.items()}
    out = nc.dram_tensor("out", (B, TOK, D), F32, kind="ExternalOutput").ap()
    program(nc, aps, out)
    return run_bass_kernel_spmd(nc, [arrays], core_ids=[0]).results[0]["out"]
```
